# Optimizing a Trainium2 kernel written in Bass

```python
import numpy as np
import jax
import jax.numpy as jnp

def _softmax(x, axis=-1):
    return jax.nn.softmax(x, axis=axis)

def _gelu(x):
    return jax.nn.gelu(x, approximate=True)

def _silu(x):
    return jax.nn.silu(x)

def _sigmoid(x):
    return jax.nn.sigmoid(x)

def _layernorm(x, axis=-1, eps=1e-05):
    m = jnp.mean(x, axis=axis, keepdims=True)
    v = jnp.var(x, axis=axis, keepdims=True)
    return (x - m) / jnp.sqrt(v + eps)

def _scatter_add(tgt, idx, src, axis=0):
    return tgt.at[idx].add(src)

def _segment_sum(src, seg, n):
    return jax.ops.segment_sum(src, seg, n)
kernel_name = 'mk_pixart_resid_d2_seqx_r8_7ea5da'

def setup_inputs(seed: int=0):
    np.random.seed(seed)
    _w = jnp.asarray

    def _rec_inputs():
        import jax
        import jax.numpy as jnp
        _rk = jax.random.key(seed)
        x = -0.0002928 + 1 * jax.random.normal(jax.random.fold_in(_rk, 1), (2, 512, 128), jnp.float32)
        _lenS = 512 - jax.random.randint(jax.random.fold_in(_rk, 7), (2,), 0, max(1, 512 // 4) + 1, jnp.int32)
        _lenS2 = 77 - jax.random.randint(jax.random.fold_in(_rk, 8), (2,), 0, max(1, 77 // 4) + 1, jnp.int32)
        cond_1024 = 0.000887014 + 1.03683 * jax.random.normal(jax.random.fold_in(_rk, 11), (2, 128), jnp.float32)
        _ctx_1024P = jax.random.normal(jax.random.fold_in(_rk, 12), (2, 16, 128), jnp.float32)
        _ctx_1024c = jax.random.dirichlet(jax.random.fold_in(_rk, 512), 0.3 * jnp.ones((16,), jnp.float32), (2, 77))
        _ctx_1024t = jnp.einsum('bsk,bkd->bsd', _ctx_1024c, _ctx_1024P)
        _ctx_1024t = _ctx_1024t * jax.lax.rsqrt(jnp.mean(jnp.square(_ctx_1024t)) + 1e-12) * 0.953939
        ctx_1024 = -0.000761806 + 0.999296 * (_ctx_1024t + 0.3 * jax.random.normal(jax.random.fold_in(_rk, 612), (2, 77, 128), jnp.float32))
        _validS = jnp.arange(512)[None, :] < _lenS[:, None]
        _validS2 = jnp.arange(77)[None, :] < _lenS2[:, None]
        _causal = jnp.tril(jnp.ones((512, 512), dtype=bool))
        mask_BxS_bf0 = jnp.logical_not(jnp.ones((2, 512), dtype=bool))
        mask_BxS2_bf0 = jnp.logical_not(jnp.ones((2, 77), dtype=bool))
        return (x, cond_1024, ctx_1024, mask_BxS_bf0, mask_BxS2_bf0)
    x, cond_1024, ctx_1024, mask_BxS_bf0, mask_BxS2_bf0 = _rec_inputs()

    def _L0_xcond_setup():
        import jax, jax.numpy as jnp
        import numpy as np
        import math
        B, S, CTX, D, H, DH = (2, 256, 32, 128, 16, 64)
        INNER = H * DH
        DFF = 4 * D

        def layernorm(x, eps=1e-05):
            m = jnp.mean(x, axis=-1, keepdims=True)
            v = jnp.var(x, axis=-1, keepdims=True)
            return (x - m) * jax.lax.rsqrt(v + eps)

        def adaln(x, t, w, b):
            emb = t @ w + b
            scale, shift = jnp.split(emb, 2, axis=-1)
            return layernorm(x) * (1.0 + scale) + shift

        def mha(xq, ctx, wq, wk, wv, wo, bo):
            b, sq, _ = xq.shape
            sk = ctx.shape[1]
            q = (xq @ wq).reshape(b, sq, H, DH).transpose(0, 2, 1, 3)
            k = (ctx @ wk).reshape(b, sk, H, DH).transpose(0, 2, 1, 3)
            v = (ctx @ wv).reshape(b, sk, H, DH).transpose(0, 2, 1, 3)
            scores = jnp.einsum('bhqd,bhkd->bhqk', q, k) / math.sqrt(DH)
            attn = jax.nn.softmax(scores, axis=-1)
            out = jnp.einsum('bhqk,bhkd->bhqd', attn, v)
            out = out.transpose(0, 2, 1, 3).reshape(b, sq, INNER)
            return out @ wo + bo

        def glu_ff(x, w1, b1, w2, b2):
            u = x @ w1 + b1
            a, gate = jnp.split(u, 2, axis=-1)
            return a * jax.nn.gelu(gate, approximate=False) @ w2 + b2
        key = jax.random.key(seed)
        ks = jax.random.split(key, 24)
        s = 1.0 / math.sqrt(D)

        def n(k, shape, scale=1.0):
            return jax.random.normal(k, shape, dtype=jnp.float32) * scale
        return {'x': n(ks[0], (B, S, D)), 't': n(ks[1], (B, 1, D)), 'context': n(ks[2], (B, CTX, D)), 'attn1_wq': n(ks[3], (D, INNER), s), 'attn1_wk': n(ks[4], (D, INNER), s), 'attn1_wv': n(ks[5], (D, INNER), s), 'attn1_wo': n(ks[6], (INNER, D), s), 'attn1_bo': n(ks[7], (D,), 0.01), 'attn2_wq': n(ks[8], (D, INNER), s), 'attn2_wk': n(ks[9], (D, INNER), s), 'attn2_wv': n(ks[10], (D, INNER), s), 'attn2_wo': n(ks[11], (INNER, D), s), 'attn2_bo': n(ks[12], (D,), 0.01), 'ff_w1': n(ks[13], (D, 2 * DFF), s), 'ff_b1': n(ks[14], (2 * DFF,), 0.01), 'ff_w2': n(ks[15], (DFF, D), 1.0 / math.sqrt(DFF)), 'ff_b2': n(ks[16], (D,), 0.01), 'norm1_w': n(ks[17], (D, 2 * D), s), 'norm1_b': n(ks[18], (2 * D,), 0.01), 'norm2_w': n(ks[19], (D, 2 * D), s), 'norm2_b': n(ks[20], (2 * D,), 0.01), 'norm3_w': n(ks[21], (D, 2 * D), s), 'norm3_b': n(ks[22], (2 * D,), 0.01)}
    _L0_xcond_all = _L0_xcond_setup()
    _L0_xcond_in = {k: v for k, v in _L0_xcond_all.items() if k in ('attn1_wq', 'attn1_wk', 'attn1_wv', 'attn1_wo', 'attn1_bo', 'attn2_wq', 'attn2_wk', 'attn2_wv', 'attn2_wo', 'attn2_bo', 'ff_w1', 'ff_b1', 'ff_w2', 'ff_b2', 'norm1_w', 'norm1_b', 'norm2_w', 'norm2_b', 'norm3_w', 'norm3_b')}
    del _L0_xcond_all

    def _L0_ffn_setup():
        import jax, jax.numpy as jnp
        import numpy as np
        B, S, D = (2, 128, 128)
        H, HD = (16, 64)
        E_R = 31
        K_ACT = 3
        INTER = 128
        EPS = 1e-05
        BASE = 10000.0

        def _rmsnorm(x, gamma):
            rms = jnp.sqrt(jnp.mean(x * x, axis=-1, keepdims=True) + EPS)
            return x / rms * gamma

        def _rope(x, theta):
            seq = x.shape[2]
            angles = jnp.arange(seq, dtype=theta.dtype)[:, None] * theta
            cos = jnp.cos(angles)[None, None]
            sin = jnp.sin(angles)[None, None]
            x1, x2 = (x[..., 0::2], x[..., 1::2])
            return jnp.concatenate([x1 * cos - x2 * sin, x1 * sin + x2 * cos], axis=-1)

        def _forward(x, theta, gamma1, gamma2, q_w, q_b, k_w, k_b, v_w, v_b, o_w, o_b, router_w, router_b, sh_w1, sh_b1, sh_w2, sh_b2, re_w1, re_b1, re_w2, re_b2):
            b, s, d = x.shape
            xn = _rmsnorm(x, gamma1)
            q = (xn @ q_w + q_b).reshape(b, s, H, HD).transpose(0, 2, 1, 3)
            k = (xn @ k_w + k_b).reshape(b, s, H, HD).transpose(0, 2, 1, 3)
            v = (xn @ v_w + v_b).reshape(b, s, H, HD).transpose(0, 2, 1, 3)
            q = _rope(q, theta)
            k = _rope(k, theta)
            scale = 1.0 / np.sqrt(HD)
            scores = jnp.einsum('bhqd,bhkd->bhqk', q, k) * scale
            causal = jnp.tril(jnp.ones((s, s), dtype=bool))
            scores = jnp.where(causal, scores, -jnp.inf)
            attn = jax.nn.softmax(scores, axis=-1)
            ctx = jnp.einsum('bhqk,bhkd->bhqd', attn, v)
            ctx = ctx.transpose(0, 2, 1, 3).reshape(b, s, H * HD)
            attn_out = ctx @ o_w + o_b + xn
            an = _rmsnorm(attn_out, gamma2)
            shared = jax.nn.gelu(an @ sh_w1 + sh_b1, approximate=False) @ sh_w2 + sh_b2
            logits = an @ router_w + router_b
            aff = jax.nn.softmax(logits, axis=-1)
            topv, topi = jax.lax.top_k(aff, K_ACT)
            gates = jnp.sum(jax.nn.one_hot(topi, E_R, dtype=aff.dtype) * topv[..., None], axis=-2)
            h = jax.nn.gelu(jnp.einsum('bsd,edh->besh', an, re_w1) + re_b1[None, :, None, :], approximate=False)
            routed = jnp.einsum('bse,besh,ehd->bsd', gates, h, re_w2) + jnp.einsum('bse,ed->bsd', gates, re_b2)
            return shared + routed + an + attn_out
        key = jax.random.key(seed)
        ks = jax.random.split(key, 24)
        s = 0.02
        theta = BASE ** (-jnp.arange(HD // 2, dtype=jnp.float32) * 2.0 / HD)
        inp = {'x': jax.random.normal(ks[0], (B, S, D), jnp.float32), 'positions': jnp.arange(S, dtype=jnp.int32), 'theta': theta, 'gamma1': jnp.ones((D,), jnp.float32), 'gamma2': jnp.ones((D,), jnp.float32), 'q_w': jax.random.normal(ks[1], (D, H * HD), jnp.float32) * s, 'q_b': jnp.zeros((H * HD,), jnp.float32), 'k_w': jax.random.normal(ks[2], (D, H * HD), jnp.float32) * s, 'k_b': jnp.zeros((H * HD,), jnp.float32), 'v_w': jax.random.normal(ks[3], (D, H * HD), jnp.float32) * s, 'v_b': jnp.zeros((H * HD,), jnp.float32), 'o_w': jax.random.normal(ks[4], (H * HD, D), jnp.float32) * s, 'o_b': jnp.zeros((D,), jnp.float32), 'router_w': jax.random.normal(ks[5], (D, E_R), jnp.float32) * s, 'router_b': jnp.zeros((E_R,), jnp.float32), 'sh_w1': jax.random.normal(ks[6], (D, INTER), jnp.float32) * s, 'sh_b1': jnp.zeros((INTER,), jnp.float32), 'sh_w2': jax.random.normal(ks[7], (INTER, D), jnp.float32) * s, 'sh_b2': jnp.zeros((D,), jnp.float32), 're_w1': jax.random.normal(ks[8], (E_R, D, INTER), jnp.float32) * s, 're_b1': jnp.zeros((E_R, INTER), jnp.float32), 're_w2': jax.random.normal(ks[9], (E_R, INTER, D), jnp.float32) * s, 're_b2': jnp.zeros((E_R, D), jnp.float32)}
        return inp
    _L0_ffn_all = _L0_ffn_setup()
    _L0_ffn_in = {k: v for k, v in _L0_ffn_all.items() if k in ('positions', 'theta', 'gamma1', 'gamma2', 'q_w', 'q_b', 'k_w', 'k_b', 'v_w', 'v_b', 'o_w', 'o_b', 'router_w', 'router_b', 'sh_w1', 'sh_b1', 'sh_w2', 'sh_b2', 're_w1', 're_b1', 're_w2', 're_b2')}
    del _L0_ffn_all

    def _L1_xcond_setup():
        import jax, jax.numpy as jnp
        import numpy as np
        NL, D, H, DFF = (6, 128, 16, 512)
        HD = D // H

        def _rope(x):
            L = x.shape[1]
            half = HD // 2
            inv = 1.0 / 10000.0 ** (jnp.arange(half, dtype=jnp.float32) / half)
            ang = jnp.arange(L, dtype=jnp.float32)[:, None] * inv
            cos = jnp.cos(ang)[None, :, None, :]
            sin = jnp.sin(ang)[None, :, None, :]
            x1, x2 = (x[..., :half], x[..., half:])
            return jnp.concatenate([x1 * cos - x2 * sin, x1 * sin + x2 * cos], axis=-1)

        def _ln(x, eps=1e-05):
            m = jnp.mean(x, axis=-1, keepdims=True)
            v = jnp.var(x, axis=-1, keepdims=True)
            return (x - m) * jax.lax.rsqrt(v + eps)

        def _adaln(x, emb, w, b):
            gb = emb[:, 0, :] @ w.T + b
            g, be = jnp.split(gb, 2, axis=-1)
            return _ln(x) * (1.0 + g[:, None, :]) + be[:, None, :]

        def _attn(q, k, v, mask):
            scores = jnp.einsum('bqhd,bkhd->bhqk', q, k) / np.float32(np.sqrt(HD))
            scores = jnp.where(mask[:, None, None, :], jnp.float32(-jnp.inf), scores)
            w = jax.nn.softmax(scores, axis=-1)
            return jnp.einsum('bhqk,bkhd->bqhd', w, v)
        key = jax.random.key(seed)
        ks = jax.random.split(key, 20)
        B, L, LC = (4, 128, 64)
        s = 0.02
        inp = {'x': jax.random.normal(ks[0], (B, L, D), jnp.float32), 'noise_emb': jax.random.normal(ks[1], (B, 1, D), jnp.float32), 'context': jax.random.normal(ks[2], (B, LC, D), jnp.float32), 'src_mask': jnp.zeros((B, L), bool), 'ctx_mask': jnp.zeros((B, LC), bool), 'n1_w': jax.random.normal(ks[3], (NL, 2 * D, D), jnp.float32) * s, 'n1_b': jnp.zeros((NL, 2 * D), jnp.float32), 'n2_w': jax.random.normal(ks[4], (NL, 2 * D, D), jnp.float32) * s, 'n2_b': jnp.zeros((NL, 2 * D), jnp.float32), 'n3_w': jax.random.normal(ks[5], (NL, 2 * D, D), jnp.float32) * s, 'n3_b': jnp.zeros((NL, 2 * D), jnp.float32), 'qkv_w': jax.random.normal(ks[6], (NL, 3 * D, D), jnp.float32) * s, 'so_w': jax.random.normal(ks[7], (NL, D, D), jnp.float32) * s, 'cq_w': jax.random.normal(ks[8], (NL, D, D), jnp.float32) * s, 'ck_w': jax.random.normal(ks[9], (NL, D, D), jnp.float32) * s, 'cv_w': jax.random.normal(ks[10], (NL, D, D), jnp.float32) * s, 'co_w': jax.random.normal(ks[11], (NL, D, D), jnp.float32) * s, 'f1_w': jax.random.normal(ks[12], (NL, DFF, D), jnp.float32) * s, 'f1_b': jnp.zeros((NL, DFF), jnp.float32), 'f2_w': jax.random.normal(ks[13], (NL, D, DFF), jnp.float32) * s, 'f2_b': jnp.zeros((NL, D), jnp.float32)}
        return inp
    _L1_xcond_all = _L1_xcond_setup()
    _L1_xcond_in = {k: v for k, v in _L1_xcond_all.items() if k in ('n1_w', 'n1_b', 'n2_w', 'n2_b', 'n3_w', 'n3_b', 'qkv_w', 'so_w', 'cq_w', 'ck_w', 'cv_w', 'co_w', 'f1_w', 'f1_b', 'f2_w', 'f2_b')}
    del _L1_xcond_all

    def _L1_ffn_setup():
        import jax, jax.numpy as jnp
        import numpy as np
        B, S, H = (2, 256, 128)
        E, F, K = (64, 64, 8)
        G, TG = (8, 4)
        SCALE = 2.5
        F_SH = 64

        def _gate(x, gate_w, gate_bias):
            scores = jax.nn.sigmoid(x @ gate_w.T)
            sc = scores + gate_bias[None, :]
            T = x.shape[0]
            group_scores = jax.lax.top_k(sc.reshape(T, G, E // G), 2)[0].sum(-1)
            _, gidx = jax.lax.top_k(group_scores, TG)
            gmask = jnp.zeros((T, G), sc.dtype).at[jnp.arange(T)[:, None], gidx].set(1.0)
            smask = jnp.repeat(gmask, E // G, axis=1)
            masked = jnp.where(smask > 0, sc, -jnp.inf)
            _, tidx = jax.lax.top_k(masked, K)
            tw = jnp.take_along_axis(scores, tidx, axis=1)
            tw = tw / (tw.sum(-1, keepdims=True) + 1e-20)
            return (tidx, tw * SCALE)
        key = jax.random.key(seed)
        ks = jax.random.split(key, 9)

        def w(k, shape, fan_in):
            return jax.random.normal(k, shape, jnp.float32) / np.float32(np.sqrt(fan_in))
        return {'hidden_states': jax.random.normal(ks[0], (B, S, H), jnp.float32), 'gate_w': w(ks[1], (E, H), H), 'gate_bias': jax.random.normal(ks[2], (E,), jnp.float32) * 0.01, 'We_gate': w(ks[3], (E, H, F), H), 'We_up': w(ks[4], (E, H, F), H), 'We_down': w(ks[5], (E, F, H), F), 'Ws_gate': w(ks[6], (H, F_SH), H), 'Ws_up': w(ks[7], (H, F_SH), H), 'Ws_down': w(ks[8], (F_SH, H), F_SH)}
    _L1_ffn_all = _L1_ffn_setup()
    _L1_ffn_in = {k: v for k, v in _L1_ffn_all.items() if k in ('gate_w', 'gate_bias', 'We_gate', 'We_up', 'We_down', 'Ws_gate', 'Ws_up', 'Ws_down')}
    del _L1_ffn_all
    return {'x': x, 'cond_1024': cond_1024, 'ctx_1024': ctx_1024, 'mask_BxS_bf0': mask_BxS_bf0, 'mask_BxS2_bf0': mask_BxS2_bf0, 'L0_xcond_attn1_wq': _L0_xcond_in['attn1_wq'], 'L0_xcond_attn1_wk': _L0_xcond_in['attn1_wk'], 'L0_xcond_attn1_wv': _L0_xcond_in['attn1_wv'], 'L0_xcond_attn1_wo': _L0_xcond_in['attn1_wo'], 'L0_xcond_attn1_bo': _L0_xcond_in['attn1_bo'], 'L0_xcond_attn2_wq': _L0_xcond_in['attn2_wq'], 'L0_xcond_attn2_wk': _L0_xcond_in['attn2_wk'], 'L0_xcond_attn2_wv': _L0_xcond_in['attn2_wv'], 'L0_xcond_attn2_wo': _L0_xcond_in['attn2_wo'], 'L0_xcond_attn2_bo': _L0_xcond_in['attn2_bo'], 'L0_xcond_ff_w1': _L0_xcond_in['ff_w1'], 'L0_xcond_ff_b1': _L0_xcond_in['ff_b1'], 'L0_xcond_ff_w2': _L0_xcond_in['ff_w2'], 'L0_xcond_ff_b2': _L0_xcond_in['ff_b2'], 'L0_xcond_norm1_w': _L0_xcond_in['norm1_w'], 'L0_xcond_norm1_b': _L0_xcond_in['norm1_b'], 'L0_xcond_norm2_w': _L0_xcond_in['norm2_w'], 'L0_xcond_norm2_b': _L0_xcond_in['norm2_b'], 'L0_xcond_norm3_w': _L0_xcond_in['norm3_w'], 'L0_xcond_norm3_b': _L0_xcond_in['norm3_b'], 'L0_ffn_positions': _L0_ffn_in['positions'], 'L0_ffn_theta': _L0_ffn_in['theta'], 'L0_ffn_gamma1': _L0_ffn_in['gamma1'], 'L0_ffn_gamma2': _L0_ffn_in['gamma2'], 'L0_ffn_q_w': _L0_ffn_in['q_w'], 'L0_ffn_q_b': _L0_ffn_in['q_b'], 'L0_ffn_k_w': _L0_ffn_in['k_w'], 'L0_ffn_k_b': _L0_ffn_in['k_b'], 'L0_ffn_v_w': _L0_ffn_in['v_w'], 'L0_ffn_v_b': _L0_ffn_in['v_b'], 'L0_ffn_o_w': _L0_ffn_in['o_w'], 'L0_ffn_o_b': _L0_ffn_in['o_b'], 'L0_ffn_router_w': _L0_ffn_in['router_w'], 'L0_ffn_router_b': _L0_ffn_in['router_b'], 'L0_ffn_sh_w1': _L0_ffn_in['sh_w1'], 'L0_ffn_sh_b1': _L0_ffn_in['sh_b1'], 'L0_ffn_sh_w2': _L0_ffn_in['sh_w2'], 'L0_ffn_sh_b2': _L0_ffn_in['sh_b2'], 'L0_ffn_re_w1': _L0_ffn_in['re_w1'], 'L0_ffn_re_b1': _L0_ffn_in['re_b1'], 'L0_ffn_re_w2': _L0_ffn_in['re_w2'], 'L0_ffn_re_b2': _L0_ffn_in['re_b2'], 'L1_xcond_n1_w': _L1_xcond_in['n1_w'], 'L1_xcond_n1_b': _L1_xcond_in['n1_b'], 'L1_xcond_n2_w': _L1_xcond_in['n2_w'], 'L1_xcond_n2_b': _L1_xcond_in['n2_b'], 'L1_xcond_n3_w': _L1_xcond_in['n3_w'], 'L1_xcond_n3_b': _L1_xcond_in['n3_b'], 'L1_xcond_qkv_w': _L1_xcond_in['qkv_w'], 'L1_xcond_so_w': _L1_xcond_in['so_w'], 'L1_xcond_cq_w': _L1_xcond_in['cq_w'], 'L1_xcond_ck_w': _L1_xcond_in['ck_w'], 'L1_xcond_cv_w': _L1_xcond_in['cv_w'], 'L1_xcond_co_w': _L1_xcond_in['co_w'], 'L1_xcond_f1_w': _L1_xcond_in['f1_w'], 'L1_xcond_f1_b': _L1_xcond_in['f1_b'], 'L1_xcond_f2_w': _L1_xcond_in['f2_w'], 'L1_xcond_f2_b': _L1_xcond_in['f2_b'], 'L1_ffn_gate_w': _L1_ffn_in['gate_w'], 'L1_ffn_gate_bias': _L1_ffn_in['gate_bias'], 'L1_ffn_We_gate': _L1_ffn_in['We_gate'], 'L1_ffn_We_up': _L1_ffn_in['We_up'], 'L1_ffn_We_down': _L1_ffn_in['We_down'], 'L1_ffn_Ws_gate': _L1_ffn_in['Ws_gate'], 'L1_ffn_Ws_up': _L1_ffn_in['Ws_up'], 'L1_ffn_Ws_down': _L1_ffn_in['Ws_down']}

def reference(x, cond_1024, ctx_1024, mask_BxS_bf0, mask_BxS2_bf0, L0_xcond_attn1_wq, L0_xcond_attn1_wk, L0_xcond_attn1_wv, L0_xcond_attn1_wo, L0_xcond_attn1_bo, L0_xcond_attn2_wq, L0_xcond_attn2_wk, L0_xcond_attn2_wv, L0_xcond_attn2_wo, L0_xcond_attn2_bo, L0_xcond_ff_w1, L0_xcond_ff_b1, L0_xcond_ff_w2, L0_xcond_ff_b2, L0_xcond_norm1_w, L0_xcond_norm1_b, L0_xcond_norm2_w, L0_xcond_norm2_b, L0_xcond_norm3_w, L0_xcond_norm3_b, L0_ffn_positions, L0_ffn_theta, L0_ffn_gamma1, L0_ffn_gamma2, L0_ffn_q_w, L0_ffn_q_b, L0_ffn_k_w, L0_ffn_k_b, L0_ffn_v_w, L0_ffn_v_b, L0_ffn_o_w, L0_ffn_o_b, L0_ffn_router_w, L0_ffn_router_b, L0_ffn_sh_w1, L0_ffn_sh_b1, L0_ffn_sh_w2, L0_ffn_sh_b2, L0_ffn_re_w1, L0_ffn_re_b1, L0_ffn_re_w2, L0_ffn_re_b2, L1_xcond_n1_w, L1_xcond_n1_b, L1_xcond_n2_w, L1_xcond_n2_b, L1_xcond_n3_w, L1_xcond_n3_b, L1_xcond_qkv_w, L1_xcond_so_w, L1_xcond_cq_w, L1_xcond_ck_w, L1_xcond_cv_w, L1_xcond_co_w, L1_xcond_f1_w, L1_xcond_f1_b, L1_xcond_f2_w, L1_xcond_f2_b, L1_ffn_gate_w, L1_ffn_gate_bias, L1_ffn_We_gate, L1_ffn_We_up, L1_ffn_We_down, L1_ffn_Ws_gate, L1_ffn_Ws_up, L1_ffn_Ws_down):
    import jax
    import jax.numpy as jnp

    def _L0_xcond_ref(x, t, context, attn1_wq, attn1_wk, attn1_wv, attn1_wo, attn1_bo, attn2_wq, attn2_wk, attn2_wv, attn2_wo, attn2_bo, ff_w1, ff_b1, ff_w2, ff_b2, norm1_w, norm1_b, norm2_w, norm2_b, norm3_w, norm3_b):
        import jax, jax.numpy as jnp
        import numpy as np
        import math
        B, S, CTX, D, H, DH = (2, 256, 32, 128, 16, 64)
        INNER = H * DH
        DFF = 4 * D

        def layernorm(x, eps=1e-05):
            m = jnp.mean(x, axis=-1, keepdims=True)
            v = jnp.var(x, axis=-1, keepdims=True)
            return (x - m) * jax.lax.rsqrt(v + eps)

        def adaln(x, t, w, b):
            emb = t @ w + b
            scale, shift = jnp.split(emb, 2, axis=-1)
            return layernorm(x) * (1.0 + scale) + shift

        def mha(xq, ctx, wq, wk, wv, wo, bo):
            b, sq, _ = xq.shape
            sk = ctx.shape[1]
            q = (xq @ wq).reshape(b, sq, H, DH).transpose(0, 2, 1, 3)
            k = (ctx @ wk).reshape(b, sk, H, DH).transpose(0, 2, 1, 3)
            v = (ctx @ wv).reshape(b, sk, H, DH).transpose(0, 2, 1, 3)
            scores = jnp.einsum('bhqd,bhkd->bhqk', q, k) / math.sqrt(DH)
            attn = jax.nn.softmax(scores, axis=-1)
            out = jnp.einsum('bhqk,bhkd->bhqd', attn, v)
            out = out.transpose(0, 2, 1, 3).reshape(b, sq, INNER)
            return out @ wo + bo

        def glu_ff(x, w1, b1, w2, b2):
            u = x @ w1 + b1
            a, gate = jnp.split(u, 2, axis=-1)
            return a * jax.nn.gelu(gate, approximate=False) @ w2 + b2
        h1 = adaln(x, t, norm1_w, norm1_b)
        x = mha(h1, h1, attn1_wq, attn1_wk, attn1_wv, attn1_wo, attn1_bo) + x
        h2 = adaln(x, t, norm2_w, norm2_b)
        x = mha(h2, context, attn2_wq, attn2_wk, attn2_wv, attn2_wo, attn2_bo) + x
        h3 = adaln(x, t, norm3_w, norm3_b)
        x = glu_ff(h3, ff_w1, ff_b1, ff_w2, ff_b2) + x
        return x

    def _L0_ffn_ref(x, positions, theta, gamma1, gamma2, q_w, q_b, k_w, k_b, v_w, v_b, o_w, o_b, router_w, router_b, sh_w1, sh_b1, sh_w2, sh_b2, re_w1, re_b1, re_w2, re_b2):
        import jax, jax.numpy as jnp
        import numpy as np
        B, S, D = (2, 128, 128)
        H, HD = (16, 64)
        E_R = 31
        K_ACT = 3
        INTER = 128
        EPS = 1e-05
        BASE = 10000.0

        def _rmsnorm(x, gamma):
            rms = jnp.sqrt(jnp.mean(x * x, axis=-1, keepdims=True) + EPS)
            return x / rms * gamma

        def _rope(x, theta):
            seq = x.shape[2]
            angles = jnp.arange(seq, dtype=theta.dtype)[:, None] * theta
            cos = jnp.cos(angles)[None, None]
            sin = jnp.sin(angles)[None, None]
            x1, x2 = (x[..., 0::2], x[..., 1::2])
            return jnp.concatenate([x1 * cos - x2 * sin, x1 * sin + x2 * cos], axis=-1)

        def _forward(x, theta, gamma1, gamma2, q_w, q_b, k_w, k_b, v_w, v_b, o_w, o_b, router_w, router_b, sh_w1, sh_b1, sh_w2, sh_b2, re_w1, re_b1, re_w2, re_b2):
            b, s, d = x.shape
            xn = _rmsnorm(x, gamma1)
            q = (xn @ q_w + q_b).reshape(b, s, H, HD).transpose(0, 2, 1, 3)
            k = (xn @ k_w + k_b).reshape(b, s, H, HD).transpose(0, 2, 1, 3)
            v = (xn @ v_w + v_b).reshape(b, s, H, HD).transpose(0, 2, 1, 3)
            q = _rope(q, theta)
            k = _rope(k, theta)
            scale = 1.0 / np.sqrt(HD)
            scores = jnp.einsum('bhqd,bhkd->bhqk', q, k) * scale
            causal = jnp.tril(jnp.ones((s, s), dtype=bool))
            scores = jnp.where(causal, scores, -jnp.inf)
            attn = jax.nn.softmax(scores, axis=-1)
            ctx = jnp.einsum('bhqk,bhkd->bhqd', attn, v)
            ctx = ctx.transpose(0, 2, 1, 3).reshape(b, s, H * HD)
            attn_out = ctx @ o_w + o_b + xn
            an = _rmsnorm(attn_out, gamma2)
            shared = jax.nn.gelu(an @ sh_w1 + sh_b1, approximate=False) @ sh_w2 + sh_b2
            logits = an @ router_w + router_b
            aff = jax.nn.softmax(logits, axis=-1)
            topv, topi = jax.lax.top_k(aff, K_ACT)
            gates = jnp.sum(jax.nn.one_hot(topi, E_R, dtype=aff.dtype) * topv[..., None], axis=-2)
            h = jax.nn.gelu(jnp.einsum('bsd,edh->besh', an, re_w1) + re_b1[None, :, None, :], approximate=False)
            routed = jnp.einsum('bse,besh,ehd->bsd', gates, h, re_w2) + jnp.einsum('bse,ed->bsd', gates, re_b2)
            return shared + routed + an + attn_out
        del positions
        return _forward(x, theta, gamma1, gamma2, q_w, q_b, k_w, k_b, v_w, v_b, o_w, o_b, router_w, router_b, sh_w1, sh_b1, sh_w2, sh_b2, re_w1, re_b1, re_w2, re_b2)

    def _L1_xcond_ref(x, noise_emb, context, src_mask, ctx_mask, n1_w, n1_b, n2_w, n2_b, n3_w, n3_b, qkv_w, so_w, cq_w, ck_w, cv_w, co_w, f1_w, f1_b, f2_w, f2_b):
        import jax, jax.numpy as jnp
        import numpy as np
        NL, D, H, DFF = (6, 128, 16, 512)
        HD = D // H

        def _rope(x):
            L = x.shape[1]
            half = HD // 2
            inv = 1.0 / 10000.0 ** (jnp.arange(half, dtype=jnp.float32) / half)
            ang = jnp.arange(L, dtype=jnp.float32)[:, None] * inv
            cos = jnp.cos(ang)[None, :, None, :]
            sin = jnp.sin(ang)[None, :, None, :]
            x1, x2 = (x[..., :half], x[..., half:])
            return jnp.concatenate([x1 * cos - x2 * sin, x1 * sin + x2 * cos], axis=-1)

        def _ln(x, eps=1e-05):
            m = jnp.mean(x, axis=-1, keepdims=True)
            v = jnp.var(x, axis=-1, keepdims=True)
            return (x - m) * jax.lax.rsqrt(v + eps)

        def _adaln(x, emb, w, b):
            gb = emb[:, 0, :] @ w.T + b
            g, be = jnp.split(gb, 2, axis=-1)
            return _ln(x) * (1.0 + g[:, None, :]) + be[:, None, :]

        def _attn(q, k, v, mask):
            scores = jnp.einsum('bqhd,bkhd->bhqk', q, k) / np.float32(np.sqrt(HD))
            scores = jnp.where(mask[:, None, None, :], jnp.float32(-jnp.inf), scores)
            w = jax.nn.softmax(scores, axis=-1)
            return jnp.einsum('bhqk,bkhd->bqhd', w, v)
        B, L, _ = x.shape
        LC = context.shape[1]
        for i in range(NL):
            xn = _adaln(x, noise_emb, n1_w[i], n1_b[i])
            qkv = xn @ qkv_w[i].T
            q, k, v = jnp.split(qkv, 3, axis=-1)
            q = _rope(q.reshape(B, L, H, HD))
            k = _rope(k.reshape(B, L, H, HD))
            v = v.reshape(B, L, H, HD)
            a = _attn(q, k, v, src_mask).reshape(B, L, D) @ so_w[i].T
            x = x + a
            xn = _adaln(x, noise_emb, n2_w[i], n2_b[i])
            q = _rope((xn @ cq_w[i].T).reshape(B, L, H, HD))
            k = _rope((context @ ck_w[i].T).reshape(B, LC, H, HD))
            v = (context @ cv_w[i].T).reshape(B, LC, H, HD)
            a = _attn(q, k, v, ctx_mask).reshape(B, L, D) @ co_w[i].T
            x = x + a
            xn = _adaln(x, noise_emb, n3_w[i], n3_b[i])
            h = jax.nn.gelu(xn @ f1_w[i].T + f1_b[i], approximate=False)
            x = x + (h @ f2_w[i].T + f2_b[i])
        return x

    def _L1_ffn_ref(hidden_states, gate_w, gate_bias, We_gate, We_up, We_down, Ws_gate, Ws_up, Ws_down):
        import jax, jax.numpy as jnp
        import numpy as np
        B, S, H = (2, 256, 128)
        E, F, K = (64, 64, 8)
        G, TG = (8, 4)
        SCALE = 2.5
        F_SH = 64

        def _gate(x, gate_w, gate_bias):
            scores = jax.nn.sigmoid(x @ gate_w.T)
            sc = scores + gate_bias[None, :]
            T = x.shape[0]
            group_scores = jax.lax.top_k(sc.reshape(T, G, E // G), 2)[0].sum(-1)
            _, gidx = jax.lax.top_k(group_scores, TG)
            gmask = jnp.zeros((T, G), sc.dtype).at[jnp.arange(T)[:, None], gidx].set(1.0)
            smask = jnp.repeat(gmask, E // G, axis=1)
            masked = jnp.where(smask > 0, sc, -jnp.inf)
            _, tidx = jax.lax.top_k(masked, K)
            tw = jnp.take_along_axis(scores, tidx, axis=1)
            tw = tw / (tw.sum(-1, keepdims=True) + 1e-20)
            return (tidx, tw * SCALE)
        b, s, h = hidden_states.shape
        x = hidden_states.reshape(-1, h).astype(jnp.float32)
        tidx, tw = _gate(x, gate_w, gate_bias)
        T = x.shape[0]
        w_dense = jnp.zeros((T, E), tw.dtype).at[jnp.arange(T)[:, None], tidx].add(tw)

        def body(acc, ws):
            wg, wu, wdn, cw = ws
            hmid = jax.nn.silu(x @ wg) * (x @ wu)
            return (acc + cw[:, None] * (hmid @ wdn), None)
        y, _ = jax.lax.scan(body, jnp.zeros_like(x), (We_gate, We_up, We_down, w_dense.T))
        y = y.reshape(b, s, h)
        shared = jax.nn.silu(hidden_states @ Ws_gate) * (hidden_states @ Ws_up) @ Ws_down
        return y + shared
    x = x + _L0_xcond_ref(_layernorm(x, axis=-1), cond_1024[:, None, :], ctx_1024, L0_xcond_attn1_wq, L0_xcond_attn1_wk, L0_xcond_attn1_wv, L0_xcond_attn1_wo, L0_xcond_attn1_bo, L0_xcond_attn2_wq, L0_xcond_attn2_wk, L0_xcond_attn2_wv, L0_xcond_attn2_wo, L0_xcond_attn2_bo, L0_xcond_ff_w1, L0_xcond_ff_b1, L0_xcond_ff_w2, L0_xcond_ff_b2, L0_xcond_norm1_w, L0_xcond_norm1_b, L0_xcond_norm2_w, L0_xcond_norm2_b, L0_xcond_norm3_w, L0_xcond_norm3_b)
    x = x + _L0_ffn_ref(_layernorm(x, axis=-1), L0_ffn_positions, L0_ffn_theta, L0_ffn_gamma1, L0_ffn_gamma2, L0_ffn_q_w, L0_ffn_q_b, L0_ffn_k_w, L0_ffn_k_b, L0_ffn_v_w, L0_ffn_v_b, L0_ffn_o_w, L0_ffn_o_b, L0_ffn_router_w, L0_ffn_router_b, L0_ffn_sh_w1, L0_ffn_sh_b1, L0_ffn_sh_w2, L0_ffn_sh_b2, L0_ffn_re_w1, L0_ffn_re_b1, L0_ffn_re_w2, L0_ffn_re_b2)
    x = x + _L1_xcond_ref(_layernorm(x, axis=-1), cond_1024[:, None, :], ctx_1024, mask_BxS_bf0, mask_BxS2_bf0, L1_xcond_n1_w, L1_xcond_n1_b, L1_xcond_n2_w, L1_xcond_n2_b, L1_xcond_n3_w, L1_xcond_n3_b, L1_xcond_qkv_w, L1_xcond_so_w, L1_xcond_cq_w, L1_xcond_ck_w, L1_xcond_cv_w, L1_xcond_co_w, L1_xcond_f1_w, L1_xcond_f1_b, L1_xcond_f2_w, L1_xcond_f2_b)
    x = x + _L1_ffn_ref(_layernorm(x, axis=-1), L1_ffn_gate_w, L1_ffn_gate_bias, L1_ffn_We_gate, L1_ffn_We_up, L1_ffn_We_down, L1_ffn_Ws_gate, L1_ffn_Ws_up, L1_ffn_Ws_down)
    return x

_drawn_inputs = setup_inputs


def setup_inputs(seed=0):
    import zlib

    import numpy as np

    out = dict(_drawn_inputs(seed))
    spreads = {'L0_ffn_gamma1': (1.0, 0.2),
     'L0_ffn_gamma2': (1.0, 0.2),
     'L0_ffn_q_b': (0.0, 2.0),
     'L0_ffn_k_b': (0.0, 2.0),
     'L0_ffn_v_b': (0.0, 0.374),
     'L0_ffn_o_b': (0.0, 0.1),
     'L0_ffn_router_b': (0.0, 0.8),
     'L0_ffn_sh_b1': (0.0, 0.8),
     'L0_ffn_sh_b2': (0.0, 0.442),
     'L0_ffn_re_b1': (0.0, 0.8),
     'L0_ffn_re_b2': (0.0, 0.8),
     'L1_xcond_n1_b': (0.0, 0.8),
     'L1_xcond_n2_b': (0.0, 0.8),
     'L1_xcond_n3_b': (0.0, 0.8),
     'L1_xcond_f1_b': (0.0, 0.709),
     'L1_xcond_f2_b': (0.0, 0.1)}
    factors = {'L0_xcond_attn1_bo': 8.0,
     'L0_xcond_attn2_bo': 21.878,
     'L0_xcond_ff_b1': 8.0,
     'L0_xcond_ff_b2': 24.036,
     'L0_xcond_norm1_b': 4.569,
     'L0_xcond_norm2_b': 8.0,
     'L0_xcond_norm3_b': 7.339,
     'L0_ffn_theta': 8.0,
     'L0_ffn_q_w': 8.0,
     'L0_ffn_k_w': 8.0,
     'L0_ffn_router_w': 8.0,
     'L0_ffn_sh_w1': 8.0,
     'L0_ffn_sh_w2': 8.0,
     'L0_ffn_re_w1': 8.0,
     'L0_ffn_re_w2': 8.0,
     'L1_xcond_n1_w': 8.0,
     'L1_xcond_n2_w': 8.0,
     'L1_xcond_n3_w': 7.318,
     'L1_xcond_qkv_w': 3.469,
     'L1_xcond_so_w': 3.75,
     'L1_xcond_cq_w': 8.0,
     'L1_xcond_ck_w': 8.0,
     'L1_xcond_cv_w': 5.103,
     'L1_xcond_co_w': 5.087,
     'L1_xcond_f1_w': 2.691,
     'L1_ffn_gate_bias': 9.516}
    for name, (base, spread) in spreads.items():
        noise = np.random.default_rng([zlib.crc32(name.encode()), seed]).standard_normal(out[name].shape)
        drawn = base * np.exp(spread * noise) if base else spread * noise
        out[name] = jnp.asarray(drawn.astype(out[name].dtype))
    for name, factor in factors.items():
        out[name] = (out[name] * factor).astype(out[name].dtype)
    return out
```

```python
from contextlib import ExitStack

import numpy as np
import concourse.bass as bass
from concourse import mybir

ALU = mybir.AluOpType
ACT = mybir.ActivationFunctionType
AX = mybir.AxisListType
F32 = mybir.dt.float32
BF16 = mybir.dt.bfloat16
I32 = mybir.dt.int32
U8 = mybir.dt.uint8

P = 128
B = 2
S = 512
TB = S // P
T = B * TB
CTX = 77
H = 16
DH = 64
PAIRS = H // 2
LAYERS = 6
HD = 8
EPS = 1e-5
NEG = -1.0e30
RSQRT_MAGIC = 0x5F3759DF

PW_Q, PW_QR, PW_K, PW_KR, PW_V, PW_O, PW = (P * i for i in range(7))
BIAS_V = 4

LQ, LQR, LK, LKR, LV = (P * i for i in range(5))
LSO, LCQ, LCQR, LCK, LCKR, LCV, LCO = (P * i for i in range(5, 12))
LF1 = 12 * P
LF2 = 16 * P
LB1 = 20 * P
LW = LB1 + 4
LOADS = ((LQ, LSO), (LSO, LF1), (LF1, LW))

R_BO1, R_BO2, R_FB2, R_OB, R_G1, R_G2, R_F2B = range(7)
ROWS = 6 + LAYERS

COMBOS = ((0, 0), (1, 0), (0, 1), (2, 0), (1, 1), (0, 2))
MASK_ROW = 64
MAX_ROW = 65

E_MOE = 32
E_R = 31
TOPK_PAD = 40
E_D = 64
F_D = 64
G_D = 8
PAIR_D = E_D // 2


class Chain:

    def __init__(self, eng, sem):
        self.eng, self.sem, self.base, self.n = eng, sem, 0, 0

    def step(self, ins):
        ins.then_inc(self.sem, 1)
        self.n += 1
        return ins

    def after(self, ins):
        self.step(ins)
        self.eng.wait_ge(self.sem, self.base + self.n)

    def loop(self, i, per):
        self.outer = (self.base, self.n, per)
        self.base, self.n = self.base + self.n + i * per, 0

    def loop_end(self, turns):
        base, n, per = self.outer
        assert self.n == per, (self.n, per)
        self.base, self.n = base, n + turns * per


def rstd_steps(c, dve, m, n, rms):
    v, y, t, u = m.lnv[:, 0:n], m.rs[:, 0:n], m.lnt[:, 0:n], m.lnu[:, 0:n]
    mean, var = m.mv[:, 0:n, 0], m.mv[:, 0:n, 1]
    if rms:
        c.after(dve.tensor_tensor(t, mean, mean, ALU.mult))
        c.after(dve.scalar_tensor_tensor(v, t, EPS, var, ALU.add, ALU.add))
    else:
        c.after(dve.tensor_scalar(v, var, EPS, None, ALU.add))
    c.after(dve.tensor_scalar(t.bitcast(I32), v.bitcast(I32), 1, None, ALU.arith_shift_right))
    c.after(dve.tensor_scalar(y.bitcast(I32), t.bitcast(I32), -1.0, float(RSQRT_MAGIC), ALU.mult, ALU.add))
    for _ in range(3):
        c.after(dve.tensor_tensor(t, y, y, ALU.mult))
        c.after(dve.scalar_tensor_tensor(u, t, -0.5, v, ALU.mult, ALU.mult))
        c.after(dve.scalar_tensor_tensor(y, u, 1.5, y, ALU.add, ALU.mult))


def norm_steps(c, dve, m, src, dst, n, rms=False, row=None, apart=None):
    if apart:
        dve.sem_inc(apart, 1)
    for t in range(n):
        ins = dve.bn_stats(m.st[:, t, :], src(t))
        c.after(ins) if t == n - 1 else c.step(ins)
    if apart:
        dve.sem_inc(apart, 1)
    for t in range(n):
        ins = dve.bn_aggr(m.mv[:, t, :], m.st[:, t, :])
        c.after(ins) if t == n - 1 else c.step(ins)
    rstd_steps(c, dve, m, n, rms)
    for t in range(n):
        if rms:
            ins = dve.scalar_tensor_tensor(dst(t), src(t), m.rs[:, t:t + 1], row, ALU.mult, ALU.mult)
        else:
            ins = dve.tensor_scalar(dst(t), src(t), m.mv[:, t, 0:1], m.rs[:, t:t + 1], ALU.subtract, ALU.mult)
        c.after(ins) if t == n - 1 else c.step(ins)


def close_sums(pe, m, banks, closed):
    for bank in banks:
        last = pe.matmul(m.ps[:, bank, :], lhsT=m.zero[:, 0:P], rhs=m.zero[:], start=False, stop=True)
    last.then_inc(closed, 1)


class Mem:
    pass


def build(nc, a, debug=None):
    ctx = ExitStack()
    with ctx:
        def sb(name, shape, dt=F32):
            return ctx.enter_context(nc.sbuf_tensor(name, shape, dt))

        taken = []

        def sem(name):
            taken.append(nc.alloc_semaphore(name=name))
            return taken[-1]

        def next_stage():
            nc.clear_and_free_semaphores(taken)
            taken.clear()
            nc.all_engine_barrier()

        m = Mem()
        m.sb, m.sem = sb, sem
        m.x = sb("x", [P, T, P])
        m.y = sb("y", [P, T, P])
        m.xn = sb("xn", [P, T, P])
        m.hT = sb("hT", [P, B, S])
        m.st = sb("st", [P, T, 6])
        m.mv = sb("mv", [P, T, 2])
        m.lnv = sb("lnv", [P, T])
        m.lnt = sb("lnt", [P, T])
        m.lnu = sb("lnu", [P, T])
        m.rs = sb("rs", [P, T])
        m.ident = sb("ident", [P, P])
        m.identb = sb("identb", [P, P], BF16)
        m.zero = sb("zero", [1, S], BF16)
        m.condT = sb("condT", [P, B])
        m.ctxT = sb("ctxT", [P, B, CTX])
        m.aff = sb("aff", [P, 21, 2, B])
        m.rows = sb("rows", [P, ROWS, P])
        m.ps = ctx.enter_context(nc.psum_tensor("ps", [P, 8, 512], F32))

        start(nc, a, m)
        stage_a(nc, a, m)
        next_stage()
        if debug == "A":
            return finish(nc, a, m)
        stage_b(nc, a, m)
        next_stage()
        if debug == "B":
            return finish(nc, a, m)
        stage_c(nc, a, m)
        next_stage()
        if debug == "C":
            return finish(nc, a, m)
        stage_d(nc, a, m)
        finish(nc, a, m)


def finish(nc, a, m):
    stored = m.sem("stored")
    with nc.Block() as block:
        @block.sync
        def _(sp):
            sp.dma_start(a["out"].rearrange("(t p) d -> p t d", p=P), m.x[:]).then_inc(stored, 16)
            sp.wait_ge(stored, 16)


def start(nc, a, m):
    loaded, ident_set, ident_made = m.sem("loaded"), m.sem("ident_set"), m.sem("ident_made")
    emb_done = m.sem("emb_done")
    aff_done = m.sem("aff_done")
    with nc.sbuf_tensor("normw", [P, 21 * 2 * P], F32) as normw, \
            nc.sbuf_tensor("normb", [P, 21, 2], F32) as normb, nc.Block() as block:
        @block.sync
        def _(sp):
            sp.dma_start(m.condT[:], a["condT"]).then_inc(loaded, 16)
            sp.dma_start(normw[:], a["norm_w"]).then_inc(loaded, 16)
            sp.dma_start(normb[:], a["norm_b"]).then_inc(loaded, 16)
            sp.dma_start(m.x[:], a["x"].rearrange("(t p) d -> p t d", p=P)).then_inc(loaded, 16)
            sp.dma_start(m.ctxT[:], a["ctxT"]).then_inc(loaded, 16)
            sp.dma_start(m.rows[:], a["rows"].rearrange("(o r) d -> o r d", o=1).broadcast_to([P, ROWS, P]))\
                .then_inc(loaded, 16)

        @block.gpsimd
        def _(pool):
            pool.memset(m.ident[:], 0.0).then_inc(ident_set, 1)
            pool.memset(m.identb[:], 0.0).then_inc(ident_set, 1)
            pool.wait_ge(ident_set, 2)
            for one in (m.ident, m.identb):
                pool.affine_select(out=one[:], in_=one[:], compare_op=ALU.not_equal, fill=1.0, base=0,
                                   pattern=[[-1, P]], channel_multiplier=1).then_inc(ident_made, 1)

        @block.tensor
        def _(pe):
            pe.wait_ge(loaded, 96)
            emb = m.ps[:, 0, 0:84].rearrange("p (k b) -> p k b", b=B)
            for k in range(42):
                last = pe.matmul(emb[:, k, :], lhsT=normw[:, k * P:(k + 1) * P], rhs=m.condT[:],
                                 start=True, stop=True)
            last.then_inc(emb_done, 1)

        @block.vector
        def _(dve):
            c = Chain(dve, aff_done)
            dve.wait_ge(emb_done, 1)
            emb = m.ps[:, 0, 0:84].rearrange("p (k s b) -> p k s b", s=2, b=B)
            for b in range(B):
                c.after(dve.tensor_tensor(m.aff[:, :, :, b], emb[:, :, :, b], normb[:], ALU.add))
            c.after(dve.tensor_scalar(m.aff[:, :, 0, :], m.aff[:, :, 0, :], 1.0, None, ALU.add))
            c.after(dve.memset(m.zero[:], 0.0))
            dve.wait_ge(ident_made, 2)


def norm_block(nc, m, name, k=None, first=None, add_row=None, rms_row=None, to_y=False,
               first_only=False):
    order = m.sem(name + "_order")
    xn_ready, turned, hT_ready = m.sem(name + "_xn"), m.sem(name + "_turned"), m.sem(name + "_hT")
    with nc.Block() as block:
        @block.vector
        def _(dve):
            c = Chain(dve, order)
            if first:
                norm_steps(c, dve, m, lambda t: m.x[:, t, :], lambda t: m.y[:, t, :], T)
            row = None if rms_row is None else m.rows[:, rms_row, :]
            source = m.x if first_only else m.y
            norm_steps(c, dve, m, lambda t: source[:, t, :], lambda t: m.xn[:, t, :], T, rms_row is not None, row)
            dve.sem_inc(xn_ready, 1)
            if to_y:
                c.after(dve.tensor_copy(m.y[:], m.xn[:]))
            if add_row is not None:
                c.after(dve.tensor_tensor(m.y[:], m.y[:],
                                          m.rows[:, add_row:add_row + 1, :].broadcast_to([P, T, P]), ALU.add))

        @block.tensor
        def _(pe):
            pe.wait_ge(xn_ready, 1)
            for b in range(B):
                for t in range(TB):
                    last = pe.transpose(m.ps[:, b, t * P:(t + 1) * P], m.xn[:, b * TB + t, :], m.ident[:])
                last.then_inc(turned, 1)

        @block.scalar
        def _(act):
            for b in range(B):
                act.wait_ge(turned, b + 1)
                if k is None:
                    act.activation(m.hT[:, b, :], m.ps[:, b, :], ACT.Copy).then_inc(hT_ready, 1)
                else:
                    act.activation(m.hT[:, b, :], m.ps[:, b, :], ACT.Identity, bias=m.aff[:, k, 1, b:b + 1],
                                   scale=m.aff[:, k, 0, b:b + 1]).then_inc(hT_ready, 1)


def attention_block(nc, m, w_pairs, name, cross=False, rope=None, causal=False, biases=None):
    sem = lambda s: m.sem(f"{name}_{s}")
    w_loaded, wo_loaded, bias_loaded = sem("w_loaded"), sem("wo_loaded"), sem("bias_loaded")
    proj_done, v_done = sem("proj_done"), sem("v_done")
    qk_ready, v_ready = sem("qk_ready"), sem("v_ready")
    roped = sem("roped")
    s_done, max_done = sem("s_done"), sem("max_done")
    nm_ready, nm_turned, nmT_ready = sem("nm_ready"), sem("nm_turned"), sem("nmT_ready")
    st_done, exp_done, pv_done = sem("st_done"), sem("exp_done"), sem("pv_done")
    cn_ready, c_turned, cT_ready = sem("cn_ready"), sem("c_turned"), sem("cT_ready")
    out_done, y_added = sem("out_done"), sem("y_added")
    ones_set, order, passed = sem("ones_set"), sem("order"), sem("passed")

    NK = CTX if cross else S
    groups = [list(range(TB))] if cross else [[t] for t in range(TB)]
    key_tiles = [(0, CTX)] if cross else [(j * P, P) for j in range(TB)]
    NG, KT = len(groups), len(key_tiles)
    units = [(b, h) for b in range(B) for h in range(2)]
    U = len(units)
    keys = lambda t: (t + 1) * P if causal else NK
    first_q = lambda j: j * P if causal else 0
    HALF = 0.125

    with nc.sbuf_tensor(name + "_w", [P, PW], F32) as w, \
            nc.sbuf_tensor(name + "_wo", [P, P], F32) as wo, \
            nc.sbuf_tensor(name + "_bias", [P, PAIRS, 5], F32) as bias, \
            nc.sbuf_tensor(name + "_q", [P, B, S], F32) as qT, \
            nc.sbuf_tensor(name + "_k", [P, B, S], F32) as kT, \
            nc.sbuf_tensor(name + "_rot", [P, B, 2, 2, S], F32) as rot, \
            nc.sbuf_tensor(name + "_v", [P, B, TB, 2, DH + 1], F32) as v, \
            nc.sbuf_tensor(name + "_nm", [P, B, 2, TB], F32) as nm, \
            nc.sbuf_tensor(name + "_nmp", [P, B, 2, TB, 2], BF16) as nmp, \
            nc.sbuf_tensor(name + "_nmT", [2, B, 2, S], BF16) as nmT, \
            nc.sbuf_tensor(name + "_ones", [2, P], BF16) as ones2, \
            nc.sbuf_tensor(name + "_p", [P, 2, KT, S], F32) as prob, \
            nc.sbuf_tensor(name + "_rden", [P, U, TB], F32) as rden, \
            nc.sbuf_tensor(name + "_cn", [P, B, TB, P], F32) as cn, \
            nc.sbuf_tensor(name + "_cT", [P, B, S], F32) as cT, nc.Block() as block:

        @block.sync
        def _(sp):
            if rope is not None:
                sp.dma_start(bias[:], biases).then_inc(bias_loaded, 16)
            sp.dma_start(w[:, 0:PW_O], w_pairs[0][:, 0:PW_O]).then_inc(w_loaded, 16)
            sp.dma_start(wo[:], w_pairs[0][:, PW_O:PW_O + P]).then_inc(wo_loaded, 16)
            with sp.Fori(1, PAIRS) as p:
                sp.wait_ge(v_done, p * B)
                sp.dma_start(w[:, 0:PW_O], w_pairs[p][:, 0:PW_O]).then_inc(w_loaded, 16)
                sp.wait_ge(out_done, p * B)
                sp.dma_start(wo[:], w_pairs[p][:, PW_O:PW_O + P]).then_inc(wo_loaded, 16)

        @block.gpsimd
        def _(pool):
            pool.memset(ones2[:], 1.0).then_inc(ones_set, 1)
            pool.memset(v[:, :, :, :, DH:DH + 1], 1.0).then_inc(ones_set, 1)
            if rope is not None:
                with pool.Fori(0, PAIRS) as p:
                    for b in range(B):
                        for i, dst in enumerate((qT, kT)):
                            pool.wait_ge(roped, (p * B + b) * 4 + 2 * i + 2)
                            pool.tensor_tensor(dst[:, b, :], rot[:, b, i, 0, :], rot[:, b, i, 1, :], ALU.add)\
                                .then_inc(qk_ready, 1)

        @block.tensor
        def _(pe):
            pe.wait_ge(ones_set, 2)

            def project(p, b):
                n = p * B + b
                jobs = ((0, PW_Q, 0), (1, PW_K, 2))
                for i, col, bank in jobs:
                    if b == 1:
                        if rope is None:
                            pe.wait_ge(qk_ready, (n - 1) * 2 + i + 1)
                        else:
                            pe.wait_ge(roped, (n - 1) * 4 + 2 * i + 2)
                    source = m.ctxT[:, b, :] if cross and i else m.hT[:, b, :]
                    width = CTX if cross and i else S
                    last = pe.matmul(m.ps[:, bank, 0:width], lhsT=w[:, col:col + P], rhs=source,
                                     start=True, stop=True)
                    if rope is not None:
                        last = pe.matmul(m.ps[:, bank + 1, 0:width], lhsT=w[:, col + P:col + 2 * P], rhs=source,
                                         start=True, stop=True)
                    last.then_inc(proj_done, 1)
                for j, (k0, kn) in enumerate(key_tiles):
                    source = m.ctxT[:, b, :] if cross else m.hT[:, b, k0:k0 + kn]
                    last = pe.matmul(m.ps[0:kn, 4 + b, j * P:(j + 1) * P], lhsT=source,
                                     rhs=w[:, PW_V:PW_V + P], start=True, stop=True)
                last.then_inc(v_done, 1)

            def scores(p, u):
                b, h = units[u]
                d0 = DH * h
                if h == 0:
                    pe.wait_ge(qk_ready, (p * B + b) * 2 + 2)
                for g, tiles in enumerate(groups):
                    i = u * NG + g
                    if i >= 2:
                        pe.wait_ge(max_done, p * U * NG + i - 1)
                    elif u == 0:
                        pe.wait_ge(qk_ready if rope is None else roped, (p + 1) * B * (2 if rope is None else 4))
                    for s, t in enumerate(tiles):
                        n = keys(t)
                        last = pe.matmul(m.ps[:, i % 2, s * NK:s * NK + n],
                                         lhsT=qT[d0:d0 + DH, b, t * P:(t + 1) * P],
                                         rhs=kT[d0:d0 + DH, b, 0:n], start=True, stop=not causal)
                        if causal:
                            last = pe.matmul(m.ps[:, i % 2, n - P:n], lhsT=m.identb[:], rhs=m.maskq[:],
                                             start=False, stop=True)
                    last.then_inc(s_done, 1)

            def turn_max(p, b):
                pe.wait_ge(nm_ready, p * B + b + 1)
                if b == 1:
                    pe.wait_ge(nmT_ready, p * B + 1)
                out = m.ps[0:2, 6, :].bitcast(BF16)
                for h in range(2):
                    for t in range(TB):
                        c = (h * TB + t) * P
                        last = pe.transpose(out[:, c:c + P], nmp[:, b, h, t, :], m.identb[:])
                last.then_inc(nm_turned, 1)

            def scores_T(p, u):
                b, h = units[u]
                d0 = DH * h
                if h == 0:
                    pe.wait_ge(nmT_ready, p * B + b + 1)
                for j, (k0, kn) in enumerate(key_tiles):
                    i = u * KT + j
                    if i >= 2:
                        pe.wait_ge(exp_done, p * U * KT + i - 1)
                    q0 = first_q(j)
                    bank = m.ps[0:kn, 2 + i % 2, q0:S]
                    pe.matmul(bank, lhsT=kT[d0:d0 + DH, b, k0:k0 + kn], rhs=qT[d0:d0 + DH, b, q0:S],
                              start=True, stop=False)
                    last = pe.matmul(bank, lhsT=ones2[:, 0:kn], rhs=nmT[:, b, h, q0:S], start=False,
                                     stop=not causal)
                    if causal:
                        last = pe.matmul(m.ps[0:kn, 2 + i % 2, q0:q0 + P], lhsT=m.identb[:], rhs=m.maskk[:],
                                         start=False, stop=True)
                    last.then_inc(st_done, 1)

            def weigh(p, u):
                b, h = units[u]
                if h == 0:
                    pe.wait_ge(v_ready, p * B + b + 1)
                pe.wait_ge(exp_done, (p * U + u + 1) * KT)
                if u >= 2:
                    pe.wait_ge(cn_ready, p * U + u - 1)
                for t in range(TB):
                    js = [j for j in range(KT) if first_q(j) <= t * P]
                    for j in js:
                        kn = key_tiles[j][1]
                        last = pe.matmul(m.ps[:, 4 + u % 2, t * (DH + 1):(t + 1) * (DH + 1)],
                                         lhsT=prob[0:kn, u % 2, j, t * P:(t + 1) * P],
                                         rhs=v[0:kn, b, j, h, :], start=j == 0, stop=j == js[-1])
                last.then_inc(pv_done, 1)

            def turn_context(p, b):
                pe.wait_ge(cn_ready, p * U + 2 * b + 2)
                if b == 1:
                    pe.wait_ge(y_added, p * B + b)
                for t in range(TB):
                    last = pe.transpose(m.ps[:, 7, t * P:(t + 1) * P], cn[:, b, t, :], m.ident[:])
                last.then_inc(c_turned, 1)

            def project_out(p, b):
                pe.wait_ge(cT_ready, p * B + b + 1)
                if b == 0:
                    pe.wait_ge(wo_loaded, 16 * (p + 1))
                for t in range(TB):
                    last = pe.matmul(m.ps[:, 7, t * P:(t + 1) * P], lhsT=cT[:, b, t * P:(t + 1) * P],
                                     rhs=wo[:], start=True, stop=True)
                last.then_inc(out_done, 1)

            with pe.Fori(0, PAIRS) as p:
                pe.wait_ge(w_loaded, 16 * (p + 1))
                project(p, 0)
                project(p, 1)
                scores(p, 0)
                scores(p, 1)
                scores(p, 2)
                turn_max(p, 0)
                scores_T(p, 0)
                scores(p, 3)
                scores_T(p, 1)
                weigh(p, 0)
                turn_max(p, 1)
                scores_T(p, 2)
                weigh(p, 1)
                scores_T(p, 3)
                turn_context(p, 0)
                weigh(p, 2)
                project_out(p, 0)
                weigh(p, 3)
                turn_context(p, 1)
                project_out(p, 1)

        @block.scalar
        def _(act):
            def evacuate(p, b):
                for i, dst in enumerate((qT, kT)):
                    width = CTX if cross and i else S
                    act.wait_ge(proj_done, (p * B + b) * 2 + i + 1)
                    act.activation(dst[:, b, 0:width], m.ps[:, 2 * i, 0:width], ACT.Copy).then_inc(qk_ready, 1)

            def copy_max(p, b):
                act.wait_ge(nm_turned, p * B + b + 1)
                act.activation(nmT[:, b, :, :], m.ps[0:2, 6, :].bitcast(BF16).rearrange("r (h q) -> r h q", h=2),
                               ACT.Copy).then_inc(nmT_ready, 1)

            def exps(p, u):
                if u >= 2:
                    act.wait_ge(pv_done, p * U + u - 1)
                for j, (k0, kn) in enumerate(key_tiles):
                    q0 = first_q(j)
                    act.wait_ge(st_done, (p * U + u) * KT + j + 1)
                    act.activation(prob[0:kn, u % 2, j, q0:S], m.ps[0:kn, 2 + (u * KT + j) % 2, q0:S], ACT.Exp,
                                   scale=HALF).then_inc(exp_done, 1)

            def copy_context(p, b):
                act.wait_ge(c_turned, p * B + b + 1)
                if rope is not None:
                    act.sem_inc(passed, 1)
                act.activation(cT[:, b, :], m.ps[:, 7, :], ACT.Identity,
                               bias=bias[:, p, BIAS_V:BIAS_V + 1] if rope is not None else 0.0)\
                    .then_inc(cT_ready, 1)

            if rope is not None:
                act.wait_ge(bias_loaded, 16)
            with act.Fori(0, PAIRS) as p:
                if rope is None:
                    evacuate(p, 0)
                    evacuate(p, 1)
                copy_max(p, 0)
                exps(p, 0)
                exps(p, 1)
                copy_max(p, 1)
                exps(p, 2)
                exps(p, 3)
                copy_context(p, 0)
                copy_context(p, 1)

        @block.vector
        def _(dve):
            c = Chain(dve, order)
            dve.wait_ge(ones_set, 2)
            if rope is not None:
                dve.wait_ge(bias_loaded, 16)

            def evacuate_v(p, b):
                dve.wait_ge(v_done, p * B + b + 1)
                kn = key_tiles[0][1]
                dve.tensor_copy(v[0:kn, b, 0:KT, :, 0:DH],
                                m.ps[0:kn, 4 + b, 0:KT * P].rearrange("p (t h d) -> p t h d", h=2, d=DH))\
                    .then_inc(v_ready, 1)

            def rotate(p, b):
                for i in range(2):
                    dve.wait_ge(proj_done, (p * B + b) * 2 + i + 1)
                    for r, table in enumerate(rope):
                        col = 2 * i + r
                        dve.scalar_tensor_tensor(rot[:, b, i, r, :], m.ps[:, 2 * i + r, :], bias[:, p, col:col + 1],
                                                 table[:], ALU.add, ALU.mult).then_inc(roped, 1)

            def row_max(p, u):
                b, h = units[u]
                for g, tiles in enumerate(groups):
                    i = u * NG + g
                    n = keys(tiles[0])
                    dve.wait_ge(s_done, p * U * NG + i + 1)
                    dve.tensor_reduce(nm[:, b, h, tiles[0]:tiles[-1] + 1],
                                      m.ps[:, i % 2, 0:len(tiles) * n].rearrange("p (t k) -> p t k", k=n),
                                      AX.X, ALU.max, negate=True).then_inc(max_done, 1)

            def split_max(p, b):
                dve.wait_ge(max_done, (p * U + 2 * b + 2) * NG)
                c.after(dve.tensor_copy(nmp[:, b, :, :, 0], nm[:, b, :, :]))
                dve.tensor_tensor(nmp[:, b, :, :, 1], nm[:, b, :, :], nmp[:, b, :, :, 0], ALU.subtract)\
                    .then_inc(nm_ready, 1)

            def normalise(p, u):
                b, h = units[u]
                dve.wait_ge(pv_done, p * U + u + 1)
                bank = m.ps[:, 4 + u % 2, 0:TB * (DH + 1)].rearrange("p (t d) -> p t d", d=DH + 1)
                c.after(dve.reciprocal(rden[:, u, :], bank[:, :, DH]))
                dve.tensor_tensor(cn[:, b, :, DH * h:DH * (h + 1)], bank[:, :, 0:DH],
                                  rden[:, u, :].rearrange("p (t o) -> p t o", o=1).broadcast_to([P, TB, DH]),
                                  ALU.mult).then_inc(cn_ready, 1)

            def add_out(p, b):
                dve.wait_ge(out_done, p * B + b + 1)
                y = m.y[:, b * TB:(b + 1) * TB, :]
                dve.tensor_tensor(y, y, m.ps[:, 7, :].rearrange("p (t d) -> p t d", t=TB), ALU.add)\
                    .then_inc(y_added, 1)

            with dve.Fori(0, PAIRS) as p:
                c.loop(p, B + U)
                if rope is not None:
                    rotate(p, 0)
                evacuate_v(p, 0)
                if rope is not None:
                    rotate(p, 1)
                evacuate_v(p, 1)
                row_max(p, 0)
                row_max(p, 1)
                split_max(p, 0)
                row_max(p, 2)
                row_max(p, 3)
                split_max(p, 1)
                normalise(p, 0)
                normalise(p, 1)
                normalise(p, 2)
                add_out(p, 0)
                normalise(p, 3)
                add_out(p, 1)
                c.loop_end(PAIRS)


def stage_a(nc, a, m):
    norm_block(nc, m, "A1n", k=0, first=True, add_row=R_BO1)
    attention_block(nc, m, a["A1_w"], "A1")
    norm_block(nc, m, "A2n", k=1, add_row=R_BO2)
    attention_block(nc, m, a["A2_w"], "A2", cross=True)
    norm_block(nc, m, "A3n", k=2, add_row=R_FB2)
    C4 = 4
    sem = lambda s: m.sem("A3_" + s)
    loaded, g_done, a_done, gelu_done, u_ready, f_done, y_added = \
        (sem(s) for s in ("loaded", "g_done", "a_done", "gelu_done", "u_ready", "f_done", "y_added"))
    with nc.sbuf_tensor("A3_w1", [P, 8 * P], F32) as w1, nc.sbuf_tensor("A3_b1", [P, 8], F32) as b1, \
            nc.sbuf_tensor("A3_w2", [P, C4, P], F32) as w2, \
            nc.sbuf_tensor("A3_g", [P, 2, S], F32) as g, \
            nc.sbuf_tensor("A3_u", [P, B, C4, S], F32) as u, nc.Block() as block:
        @block.sync
        def _(sp):
            sp.dma_start(w1[:], a["A_w1"]).then_inc(loaded, 16)
            sp.dma_start(b1[:], a["A_b1"]).then_inc(loaded, 16)
            sp.dma_start(w2[:], a["A_w2"]).then_inc(loaded, 16)

        @block.tensor
        def _(pe):
            pe.wait_ge(loaded, 48)
            for b in range(B):
                for i in range(C4):
                    n = b * C4 + i
                    if n >= 2:
                        pe.wait_ge(gelu_done, n - 1)
                    pe.matmul(m.ps[:, n % 2, :], lhsT=w1[:, (C4 + i) * P:(C4 + i + 1) * P], rhs=m.hT[:, b, :],
                              start=True, stop=True).then_inc(g_done, 1)
                    if n >= 2:
                        pe.wait_ge(u_ready, n - 1)
                    pe.matmul(m.ps[:, 2 + n % 2, :], lhsT=w1[:, i * P:(i + 1) * P], rhs=m.hT[:, b, :],
                              start=True, stop=True).then_inc(a_done, 1)
                for t in range(TB):
                    for i in range(C4):
                        if t == 0:
                            pe.wait_ge(u_ready, b * C4 + i + 1)
                        last = pe.matmul(m.ps[:, 4 + b, t * P:(t + 1) * P], lhsT=u[:, b, i, t * P:(t + 1) * P],
                                         rhs=w2[:, i, :], start=i == 0, stop=i == C4 - 1)
                last.then_inc(f_done, 1)

        @block.scalar
        def _(act):
            act.wait_ge(loaded, 48)
            for n in range(B * C4):
                act.wait_ge(g_done, n + 1)
                if n >= 2:
                    act.wait_ge(u_ready, n - 1)
                act.activation(g[:, n % 2, :], m.ps[:, n % 2, :], ACT.Gelu,
                               bias=b1[:, C4 + n % C4:C4 + n % C4 + 1]).then_inc(gelu_done, 1)

        @block.vector
        def _(dve):
            dve.wait_ge(loaded, 48)
            for b in range(B):
                for i in range(C4):
                    n = b * C4 + i
                    dve.wait_ge(gelu_done, n + 1)
                    dve.wait_ge(a_done, n + 1)
                    dve.scalar_tensor_tensor(u[:, b, i, :], m.ps[:, 2 + n % 2, :], b1[:, i:i + 1], g[:, n % 2, :],
                                             ALU.add, ALU.mult).then_inc(u_ready, 1)
            c = Chain(dve, y_added)
            for b in range(B):
                dve.wait_ge(f_done, b + 1)
                y, x = m.y[:, b * TB:(b + 1) * TB, :], m.x[:, b * TB:(b + 1) * TB, :]
                c.after(dve.tensor_tensor(y, y, m.ps[:, 4 + b, :].rearrange("p (t d) -> p t d", t=TB), ALU.add))
                c.after(dve.tensor_tensor(x, x, y, ALU.add))


def rope_tables(nc, a, m, cos, sin):
    sem = lambda s: m.sem("rope_" + s)
    loaded, order, reduced, done, zeroed, masked = (sem(s) for s in
                                                   ("loaded", "order", "reduced", "done", "zeroed", "masked"))
    TWO_PI = 6.283185307179586
    C1 = 6.28125
    C2 = float(np.float32(np.float64(TWO_PI - C1)).view(np.uint32) & 0xFFFFF000)
    C2 = float(np.uint32(np.float32(TWO_PI - C1).view(np.uint32) & 0xFFFFF000).view(np.float32))
    C3 = float(np.float32(TWO_PI - C1 - C2))
    ROUND = 12582912.0
    with nc.sbuf_tensor("rope_in", [P, 2], F32) as tin, nc.sbuf_tensor("rope_pos", [P, S], F32) as pos, \
            nc.sbuf_tensor("rope_n", [P, S], F32) as nrm, nc.sbuf_tensor("rope_r", [P, 2, S], F32) as r, \
            nc.sbuf_tensor("rope_t", [P, S], F32) as t, nc.Block() as block:
        @block.sync
        def _(sp):
            sp.dma_start(tin[:], a["theta"]).then_inc(loaded, 16)
            sp.dma_start(pos[:], a["positions"].rearrange("(o s) -> o s", o=1).broadcast_to([P, S]))\
                .then_inc(loaded, 16)

        @block.gpsimd
        def _(pool):
            pool.memset(m.maskq[:], 0.0).then_inc(zeroed, 1)
            pool.memset(m.maskk[:], 0.0).then_inc(zeroed, 1)
            pool.wait_ge(zeroed, 2)
            pool.affine_select(out=m.maskq[:], in_=m.maskq[:], compare_op=ALU.is_ge, fill=NEG, base=0,
                               pattern=[[-1, P]], channel_multiplier=1).then_inc(masked, 1)
            pool.affine_select(out=m.maskk[:], in_=m.maskk[:], compare_op=ALU.is_ge, fill=NEG, base=0,
                               pattern=[[1, P]], channel_multiplier=-1).then_inc(masked, 1)

        @block.vector
        def _(dve):
            c = Chain(dve, order)
            dve.wait_ge(loaded, 32)
            ang, s_r, c_r = pos[:], r[:, 0, :], r[:, 1, :]
            c.after(dve.tensor_scalar(ang, pos[:], tin[:, 0:1], None, ALU.mult))
            c.after(dve.tensor_scalar(nrm[:], ang, 1.0 / TWO_PI, ROUND, ALU.mult, ALU.add))
            c.after(dve.tensor_scalar(nrm[:], nrm[:], ROUND, None, ALU.subtract))
            c.after(dve.scalar_tensor_tensor(s_r, nrm[:], -C1, ang, ALU.mult, ALU.add))
            c.after(dve.scalar_tensor_tensor(s_r, nrm[:], -C2, s_r, ALU.mult, ALU.add))
            c.after(dve.scalar_tensor_tensor(s_r, nrm[:], -C3, s_r, ALU.mult, ALU.add))
            c.after(dve.tensor_scalar(c_r, s_r, TWO_PI / 4, None, ALU.add))
            c.after(dve.tensor_scalar(t[:], c_r, TWO_PI / 2, -TWO_PI, ALU.is_gt, ALU.mult))
            c.after(dve.tensor_tensor(c_r, c_r, t[:], ALU.add))
            PI = 3.1415925
            dve.tensor_scalar(r[:], r[:], -PI, PI, ALU.max, ALU.min).then_inc(reduced, 1)

        @block.scalar
        def _(act):
            act.wait_ge(reduced, 1)
            act.activation(sin[:], r[:, 0, :], ACT.Sin).then_inc(done, 1)
            act.activation(cos[:], r[:, 1, :], ACT.Sin).then_inc(done, 1)
            act.wait_ge(done, 2)
            act.activation(sin[:], sin[:], ACT.Copy, scale=tin[:, 1:2]).then_inc(done, 1)


def stage_b(nc, a, m):
    norm_block(nc, m, "B0n", first=True, rms_row=R_G1, to_y=True, add_row=R_OB)
    with nc.sbuf_tensor("B_cos", [P, S], F32) as cos, nc.sbuf_tensor("B_sin", [P, S], F32) as sin, \
            nc.sbuf_tensor("maskq", [P, P], BF16) as m.maskq, nc.sbuf_tensor("maskk", [P, P], BF16) as m.maskk:
        rope_tables(nc, a, m, cos, sin)
        attention_block(nc, m, a["B_w"], "B1", rope=(cos, sin), causal=True, biases=a["B_bias"])
    norm_block(nc, m, "B2n", rms_row=R_G2)

    gT = m.ctx_gT = None
    with nc.sbuf_tensor("B_gT", [P, T * P], BF16) as gT, nc.sbuf_tensor("B_sel", [P, E_MOE, P], BF16) as sel, \
            nc.sbuf_tensor("B_gates", [P, T, E_MOE], F32) as gates, \
            nc.sbuf_tensor("B_gT32", [E_MOE, T * P], F32) as gT32:
        router_b(nc, a, m, gates, gT, gT32, sel)
        experts_b(nc, a, m, gT, gT32, sel)


def router_b(nc, a, m, gates, gT, gT32, sel):
    sem = lambda s: m.sem("B3_" + s)
    loaded, logits_done, l_ready, e_done, order, gates_ready, turned, gT_ready, sel_set, sel_made = \
        (sem(s) for s in ("loaded", "logits_done", "l_ready", "e_done", "order", "gates_ready", "turned",
                          "gT_ready", "sel_set", "sel_made"))
    W = TOPK_PAD
    with nc.sbuf_tensor("B3_rw", [P, E_R], F32) as rw, nc.sbuf_tensor("B3_rb", [P, E_R], F32) as rb, \
            nc.sbuf_tensor("B3_l", [P, T, E_R], F32) as lg, nc.sbuf_tensor("B3_nm", [P, T], F32) as nm, \
            nc.sbuf_tensor("B3_aff", [P, T, W], F32) as aff, nc.sbuf_tensor("B3_rest", [P, T, W], F32) as rest, \
            nc.sbuf_tensor("B3_top", [P, T, 8], F32) as top, nc.sbuf_tensor("B3_sum", [P, T], F32) as ssum, \
            nc.sbuf_tensor("B3_rem", [3 * E_MOE, T * P], F32) as rem, nc.Block() as block:
        @block.sync
        def _(sp):
            sp.dma_start(rw[:], a["B_rw"]).then_inc(loaded, 16)
            sp.dma_start(rb[:], a["B_rb"].rearrange("(o e) -> o e", o=1).broadcast_to([P, E_R]))\
                .then_inc(loaded, 16)

        @block.gpsimd
        def _(pool):
            pool.memset(sel[:], 0.0).then_inc(sel_set, 1)
            pool.wait_ge(sel_set, 1)
            for part in range(3):
                pool.affine_select(out=sel[0:96, :, :], in_=sel[0:96, :, :], compare_op=ALU.not_equal, fill=1.0,
                                   base=-32 * part, pattern=[[-1, E_MOE], [0, P]], channel_multiplier=1)\
                    .then_inc(sel_made, 1)
                pool.wait_ge(sel_made, part + 1)

        @block.tensor
        def _(pe):
            pe.wait_ge(loaded, 32)
            for t in range(T):
                last = pe.matmul(m.ps[:, 0, t * 32:t * 32 + E_R], lhsT=m.hT[:, t // TB, t % TB * P:(t % TB + 1) * P],
                                 rhs=rw[:], start=True, stop=True)
            last.then_inc(logits_done, 1)
            pe.wait_ge(gates_ready, 1)
            for t in range(T):
                last = pe.transpose(m.ps[0:E_MOE, 1 + t // TB, t % TB * P:(t % TB + 1) * P], gates[:, t, :],
                                    m.ident[:])
            last.then_inc(turned, 1)

        @block.scalar
        def _(act):
            act.wait_ge(l_ready, 1)
            act.activation(aff[:, :, 0:E_R], lg[:], ACT.Exp).then_inc(e_done, 1)

        @block.vector
        def _(dve):
            c = Chain(dve, order)
            wide = lambda x, n: x.rearrange("p (t o) -> p t o", o=1).broadcast_to([P, T, n])
            c.step(dve.memset(aff[:, :, E_R:W], -1.0))
            dve.wait_ge(loaded, 32)
            dve.wait_ge(logits_done, 1)
            l_ps = m.ps[:, 0, 0:T * 32].rearrange("p (t e) -> p t e", e=32)[:, :, 0:E_R]
            c.after(dve.tensor_tensor(lg[:], l_ps, rb[:].rearrange("p (o e) -> p o e", o=1)
                                      .broadcast_to([P, T, E_R]), ALU.add))
            c.after(dve.tensor_reduce(nm[:], lg[:], AX.X, ALU.max))
            dve.tensor_tensor(lg[:], lg[:], wide(nm[:], E_R), ALU.subtract).then_inc(l_ready, 1)
            dve.wait_ge(e_done, 1)
            c.after(dve.tensor_reduce(ssum[:], aff[:, :, 0:E_R], AX.X, ALU.add))
            c.after(dve.reciprocal(ssum[:], ssum[:]))
            c.after(dve.tensor_tensor(aff[:, :, 0:E_R], aff[:, :, 0:E_R], wide(ssum[:], E_R), ALU.mult))
            for t in range(T):
                c.step(dve.max(top[:, t, :], aff[:, t, :]))
            c.after(dve.memset(gates[:], 1.0))
            c.after(dve.memset(top[:, :, 3:8], -1.0))
            for t in range(T):
                c.after(dve.match_replace(rest[:, t, :], top[:, t, :], aff[:, t, :], 0.0))
            dve.tensor_tensor(gates[:, :, 0:E_R], aff[:, :, 0:E_R], rest[:, :, 0:E_R], ALU.subtract)\
                .then_inc(gates_ready, 1)
            dve.wait_ge(turned, 1)
            g_ps = m.ps[0:E_MOE, 1:3, :].rearrange("p b s -> p (b s)")
            c.after(dve.tensor_copy(gT32[:], g_ps))
            c.after(dve.tensor_copy(gT[0:32, :], gT32[:]))
            c.after(dve.tensor_tensor(rem[0:32, :], gT32[:], gT[0:32, :], ALU.subtract))
            c.after(dve.tensor_copy(gT[32:64, :], rem[0:32, :]))
            c.after(dve.tensor_copy(rem[32:64, :], rem[0:32, :]))
            dve.tensor_tensor(gT[64:96, :], rem[32:64, :], gT[32:64, :], ALU.subtract).then_inc(gT_ready, 1)


def experts_b(nc, a, m, gT, gT32, sel):
    sem = lambda s: m.sem("B4_" + s)
    w_loaded, b_loaded, up_done, gb_done, gelu_done, h_ready, down_done = \
        (sem(s) for s in ("w_loaded0", "b_loaded", "up_done", "gb_done", "gelu_done", "h_ready", "down_done"))
    acc_ready, acc_turned, order, closed = sem("acc_ready"), sem("acc_turned"), sem("order"), sem("closed")
    UN = 2
    w_loaded = [w_loaded, sem("w_loaded1")]
    EW = 2 * P + 1
    with nc.sbuf_tensor("B4_w", [P, UN, EW], F32) as w, nc.sbuf_tensor("B4_b2", [E_MOE, P], F32) as b2, \
            nc.sbuf_tensor("B4_g", [P, B, S], F32) as g, nc.sbuf_tensor("B4_h", [P, B, S], F32) as h, \
            nc.sbuf_tensor("B4_acc", [P, B, S], F32) as acc, nc.Block() as block:
        @block.sync
        def _(sp):
            sp.dma_start(b2[:], a["B_b2"]).then_inc(b_loaded, 16)
            for k in range(UN):
                sp.dma_start(w[:, k, :], a["B_ew"][k]).then_inc(w_loaded[k], 16)
            with sp.Fori(1, E_MOE // UN) as i:
                for k in range(UN):
                    sp.wait_ge(down_done, i * UN * B)
                    sp.dma_start(w[:, k, :], a["B_ew"][i * UN + k]).then_inc(w_loaded[k], 16)

        @block.tensor
        def _(pe):
            pe.wait_ge(b_loaded, 16)
            for b in range(B):
                pe.matmul(m.ps[:, 4 + b, :], lhsT=b2[:], rhs=gT32[:, b * S:(b + 1) * S], start=True, stop=False)
            with pe.Fori(0, E_MOE // UN) as i:
                for k in range(UN):
                    e = i * UN + k
                    pe.wait_ge(w_loaded[k], 16 * (i + 1))
                    for b in range(B):
                        pe.matmul(m.ps[:, b, :], lhsT=w[:, k, 0:P], rhs=m.hT[:, b, :], start=True, stop=True)\
                            .then_inc(up_done, 1)
                    for b in range(B):
                        pe.matmul(m.ps[:, 2 + b, :], lhsT=sel[0:96, e, :], rhs=gT[0:96, b * S:(b + 1) * S],
                                  start=True, stop=True).then_inc(gb_done, 1)
                    for b in range(B):
                        pe.wait_ge(h_ready, e * B + b + 1)
                        pe.matmul(m.ps[:, 4 + b, :], lhsT=w[:, k, P:2 * P], rhs=h[:, b, :], start=False,
                                  stop=False).then_inc(down_done, 1)
            close_sums(pe, m, (4, 5), closed)
            pe.wait_ge(acc_ready, 2)
            for b in range(B):
                for t in range(TB):
                    last = pe.transpose(m.ps[:, 6 + b, t * P:(t + 1) * P], acc[:, b, t * P:(t + 1) * P], m.ident[:])
                last.then_inc(acc_turned, 1)

        @block.scalar
        def _(act):
            with act.Fori(0, E_MOE // UN) as i:
                for k in range(UN):
                    e = i * UN + k
                    for b in range(B):
                        act.wait_ge(up_done, e * B + b + 1)
                        act.activation(g[:, b, :], m.ps[:, b, :], ACT.Gelu, bias=w[:, k, 2 * P:2 * P + 1])\
                            .then_inc(gelu_done, 1)

        @block.vector
        def _(dve):
            with dve.Fori(0, E_MOE // UN) as i:
                for k in range(UN):
                    e = i * UN + k
                    for b in range(B):
                        dve.wait_ge(gelu_done, e * B + b + 1)
                        dve.wait_ge(gb_done, e * B + b + 1)
                        dve.tensor_tensor(h[:, b, :], g[:, b, :], m.ps[:, 2 + b, :], ALU.mult).then_inc(h_ready, 1)
            dve.wait_ge(closed, 1)
            for b in range(B):
                dve.tensor_copy(acc[:, b, :], m.ps[:, 4 + b, :]).then_inc(acc_ready, 1)
            c = Chain(dve, order)
            c.after(dve.tensor_tensor(m.y[:], m.y[:], m.xn[:], ALU.add))
            for b in range(B):
                tiles = slice(b * TB, (b + 1) * TB)
                dve.wait_ge(acc_turned, b + 1)
                c.after(dve.tensor_tensor(m.y[:, tiles, :], m.y[:, tiles, :],
                                          m.ps[:, 6 + b, :].rearrange("p (t d) -> p t d", t=TB), ALU.add))
                c.after(dve.tensor_tensor(m.x[:, tiles, :], m.x[:, tiles, :], m.y[:, tiles, :], ALU.add))


def stage_c(nc, a, m):
    first_norm = m.sem("C0_order")
    with nc.Block() as block:
        @block.vector
        def _(dve):
            c = Chain(dve, first_norm)
            norm_steps(c, dve, m, lambda t: m.x[:, t, :], lambda t: m.y[:, t, :], T)

    with ExitStack() as held:
        def sb(name, shape, dt=F32):
            return held.enter_context(nc.sbuf_tensor("C_" + name, shape, dt))

        (zeroed, ones_set, const_loaded, valid_ready, wqkv_loaded, wcross_loaded, wff_loaded,
         gelu_done, f1_done, f2_done, order, ctx_copied, ff_added, pe_passed, dve_passed) = \
            (m.sem("C_" + n) for n in
             ("zeroed", "ones_set", "const_loaded", "valid_ready", "wqkv_loaded", "wcross_loaded",
             "wff_loaded", "gelu_done", "f1_done", "f2_done", "order", "ctx_copied", "ff_added",
             "pe_passed", "dve_passed"))
        (xn_ready, turned, hT_ready) = \
            ([m.sem(f"C_{n}{i}") for i in range(3)] for n in
             ("xn_ready", "turned", "hT_ready"))
        (proj_done, v_done, v_ready, roped, q_sum, k_sum, q_p12, k_p12, q_rem, k_rem, q_p3, k_p3,
         q_stacked, k_stacked, s_done, max_done, nm_ready, nm_turned, nmT_ready, max_stacked, st_done,
         exp_done, pv_done, pv_copied, cn_ready, c_turned, cT_ready, out_done) = \
            ([m.sem(f"C_{n}{i}") for i in range(2)] for n in
             ("proj_done", "v_done", "v_ready", "roped", "q_sum", "k_sum", "q_p12", "k_p12", "q_rem",
             "k_rem", "q_p3", "k_p3", "q_stacked", "k_stacked", "s_done", "max_done", "nm_ready",
             "nm_turned", "nmT_ready", "max_stacked", "st_done", "exp_done", "pv_done", "pv_copied",
             "cn_ready", "c_turned", "cT_ready", "out_done"))

        w = sb("w", [P, LW])
        qs = sb("qs", [P, B, H, S], BF16)
        ks = sb("ks", [P, B, H, S], BF16)
        kc = sb("kc", [P, B, H, CTX], BF16)
        cos, sin = sb("cos", [P, S]), sb("sin", [P, S])
        rot = sb("rot", [P, 2, 2, S])
        full = sb("full", [P, 2, S])
        rem = sb("rem", [P, 2, S])
        parts = sb("parts", [P, 2, 3, S], BF16)
        va = sb("va", [P, B, TB, H, HD + 1])
        vc = sb("vc", [CTX, H, HD + 1])
        valid = sb("valid", [P, B, TB])
        validc = sb("validc", [CTX, B])
        mk, mkc = sb("mk", [P, B, TB], U8), sb("mkc", [CTX, B], U8)
        mrow, mrowc = sb("mrow", [MASK_ROW + 1, B, S], U8), sb("mrowc", [MASK_ROW + 1, B, CTX], U8)
        nm = sb("nm", [P, H, TB])
        nmp = sb("nmp", [P, TB, 2, H], BF16)
        nmT = sb("nmT", [2 * H, S], BF16)
        prob = sb("prob", [P, 2, TB, S])
        craw = sb("craw", [P, TB, H, HD + 1])
        rden = sb("rden", [P, TB, H])
        cn, cT = sb("cn", [P, TB, P]), sb("cT", [P, S])
        hT = sb("hT", [P, S])
        ctxb = sb("ctxb", [P, CTX])
        u = sb("u", [P, 4, S])
        ps = m.ps
        SCALE = 1.0 / float(np.sqrt(np.float32(HD)))
        UNITS = LAYERS * B
        HP = H // 2
        NK, KT = (S, CTX), (TB, 1)
        QCOL, KCOL, VCOL, OCOL = (LQ, LCQ), (LK, LCK), (LV, LCV), (LSO, LCO)
        CREDIT = 2

        with nc.Block() as block:
            @block.sync
            def _(sp):
                sp.dma_start(cos[:], a["C_cos"]).then_inc(const_loaded, 16)
                sp.dma_start(sin[:], a["C_sin"]).then_inc(const_loaded, 16)
                sp.dma_start(mk[:], a["mask_cols"]).then_inc(const_loaded, 16)
                sp.dma_start(mkc[:], a["maskc_cols"]).then_inc(const_loaded, 16)
                sp.dma_start(mrow[MASK_ROW:MASK_ROW + 1], a["mask_rows"].rearrange("(o b) s -> o b s", o=1))\
                    .then_inc(const_loaded, 16)
                sp.dma_start(mrowc[MASK_ROW:MASK_ROW + 1], a["maskc_rows"].rearrange("(o b) s -> o b s", o=1))\
                    .then_inc(const_loaded, 16)

                def load(part, l):
                    c0, c1 = LOADS[part]
                    sem = (wqkv_loaded, wcross_loaded, wff_loaded)[part]
                    sp.dma_start(w[:, c0:c1], a["C_w"][l][:, c0:c1]).then_inc(sem, 16)

                def stack(n, b, k):
                    kdst = (ks, kc)[k]
                    for i, (p12, p3, stacked) in enumerate(((q_p12[k], q_p3[k], q_stacked[k]),
                                                            (k_p12[k], k_p3[k], k_stacked[k]))):
                        width = NK[k] if i else S
                        for part in range(3):
                            if part < 2:
                                sp.wait_ge(p12, n * 2 + part + 1)
                            else:
                                sp.wait_ge(p3, n + 1)
                            for r, combo in enumerate(COMBOS):
                                if combo[i] == part:
                                    dst = (qs, kdst)[i][r * HD:(r + 1) * HD, b, :, 0:width]
                                    sp.dma_start(dst, parts[:, i, part, 0:width]).then_inc(stacked, 16)

                def stack_max(n, b, k):
                    sp.wait_ge(nmT_ready[k], n + 1)
                    for part in range(2):
                        sp.dma_start(qs[MAX_ROW + part:MAX_ROW + part + 1, b, :, :],
                                     nmT[part * H:(part + 1) * H, :]).then_inc(max_stacked[k], 16)

                def unit(n, l, b, last=False, reload=True):
                    if not last:
                        stack(n + 1, 1 - b, 0)
                        if b == 0 and reload:
                            sp.wait_ge(v_done[0], n + 2)
                            load(0, l + 1)
                        stack_max(n + 1, 1 - b, 0)
                    stack(n, b, 1)
                    stack_max(n, b, 1)
                    if b == 1 and reload:
                        sp.wait_ge(out_done[1], n + 1)
                        load(1, l + 1)
                        sp.wait_ge(f2_done, n + 1)
                        load(2, l + 1)

                for part in range(3):
                    load(part, 0)
                sp.wait_ge(zeroed, 3)
                stack(0, 0, 0)
                stack_max(0, 0, 0)
                with sp.Fori(0, LAYERS - 1) as l:
                    unit(l * B, l, 0)
                    unit(l * B + 1, l, 1)
                unit(UNITS - 2, LAYERS - 1, 0, reload=False)
                unit(UNITS - 1, LAYERS - 1, 1, last=True, reload=False)

            @block.gpsimd
            def _(pool):
                for one in (qs, ks, kc):
                    pool.memset(one[:], 0.0).then_inc(zeroed, 1)
                pool.wait_ge(zeroed, 3)
                pool.memset(qs[MASK_ROW:MASK_ROW + 1], 1.0).then_inc(ones_set, 1)
                pool.memset(ks[MASK_ROW:MASK_ROW + 3], 1.0).then_inc(ones_set, 1)
                pool.memset(kc[MASK_ROW:MASK_ROW + 3], 1.0).then_inc(ones_set, 1)

                def keys(n, k):
                    f, r, p = full[:, 1, 0:NK[k]], rem[:, 1, 0:NK[k]], parts[:, 1, :, 0:NK[k]]
                    pool.wait_ge(roped[k], n * 4 + 4)
                    pool.tensor_tensor(f, rot[:, 1, 0, 0:NK[k]], rot[:, 1, 1, 0:NK[k]], ALU.add)\
                        .then_inc(k_sum[k], 1)
                    pool.wait_ge(k_p12[k], n * 2 + 1)
                    pool.tensor_tensor(r, f, p[:, 0, :], ALU.subtract).then_inc(k_rem[k], 1)
                    pool.wait_ge(k_p12[k], n * 2 + 2)
                    pool.tensor_tensor(p[:, 2, :], r, p[:, 1, :], ALU.subtract).then_inc(k_p3[k], 1)

                def unit(n, last=False):
                    if not last:
                        keys(n + 1, 0)
                    b = n % B
                    if last:
                        pool.wait_ge(v_done[1], UNITS - 1)
                    pool.tensor_copy(ctxb[:], m.ctxT[:, b, :]).then_inc(ctx_copied, 1)
                    keys(n, 1)

                keys(0, 0)
                with pool.Fori(0, UNITS - 1) as n:
                    unit(n)
                unit(UNITS - 1, last=True)

            @block.tensor
            def _(pe):
                def turn_norm(n, i):
                    pe.wait_ge(xn_ready[i], n + 1)
                    for t in range(TB):
                        last = pe.transpose(ps[:, 7, t * P:(t + 1) * P], m.xn[:, t, :], m.ident[:])
                    last.then_inc(turned[i], 1)

                def project(n, k):
                    if k == 0:
                        pe.wait_ge(wqkv_loaded, (n // B + 1) * 16)
                    else:
                        pe.wait_ge(wcross_loaded, (n // B + 1) * 16)
                        pe.wait_ge(ctx_copied, n + 1)
                    pe.wait_ge(hT_ready[k], n + 1)
                    for i, col in enumerate((QCOL[k], KCOL[k])):
                        source = ctxb[:] if k and i else hT[:]
                        for r in range(2):
                            last = pe.matmul(ps[:, 2 * i + r, 0:source.shape[1]],
                                             lhsT=w[:, col + r * P:col + (r + 1) * P], rhs=source,
                                             start=True, stop=True)
                        last.then_inc(proj_done[k], 1)
                    if k:
                        pe.matmul(ps[0:CTX, 4, 0:P], lhsT=ctxb[:], rhs=w[:, LCV:LCV + P], start=True, stop=True)\
                            .then_inc(v_done[1], 1)
                    else:
                        for t in range(TB):
                            last = pe.matmul(ps[:, 4, t * P:(t + 1) * P], lhsT=hT[:, t * P:(t + 1) * P],
                                             rhs=w[:, LV:LV + P], start=True, stop=True)
                        last.then_inc(v_done[0], 1)

                def stacks_there(n, k):
                    pe.wait_ge(q_stacked[k], (n + 1) * 16 * len(COMBOS))
                    pe.wait_ge(k_stacked[k], (n + 1) * 16 * len(COMBOS))
                    pe.wait_ge(roped[k], n * 4 + 4)
                    pe.wait_ge(v_ready[k], n + 1)
                    pe.sem_inc(pe_passed, 1)

                def scores(n, b, h, j, g):
                    i = 2 * j + g
                    pe.wait_ge(max_done[0], (n * H + h - j) * 2 + i - 1 + CREDIT)
                    for t in (2 * g, 2 * g + 1):
                        last = pe.matmul(ps[:, 2 * (i % 2) + t % 2, :], lhsT=qs[0:MAX_ROW, b, h, t * P:(t + 1) * P],
                                         rhs=ks[0:MAX_ROW, b, h, :], start=True, stop=True)
                    last.then_inc(s_done[0], 1)

                def scores_T(n, b, h, j, kt):
                    i = 4 * j + kt
                    pe.wait_ge(exp_done[0], (n * H + h - j) * TB + i - 1 + CREDIT)
                    pe.matmul(ps[:, 4 + i % 2, :], lhsT=ks[0:MAX_ROW + 2, b, h, kt * P:(kt + 1) * P],
                              rhs=qs[0:MAX_ROW + 2, b, h, :],
                              start=True, stop=True).then_inc(st_done[0], 1)

                def weigh(n, b, h, j, t):
                    if t == 0:
                        pe.wait_ge(exp_done[0], (n * H + h + 1) * TB + CREDIT)
                        pe.wait_ge(pv_copied[0], n * H + h - 1 + CREDIT)
                    for kt in range(TB):
                        last = pe.matmul(ps[:, 6 + j, t * (HD + 1):(t + 1) * (HD + 1)],
                                         lhsT=prob[:, j, kt, t * P:(t + 1) * P], rhs=va[:, b, kt, h, :],
                                         start=kt == 0, stop=kt == TB - 1)
                    if t == TB - 1:
                        last.then_inc(pv_done[0], 1)

                def heads(n, b, nb, nxt, hp, first=False):
                    for j in range(2):
                        h = 2 * hp + j
                        for q in range(TB):
                            scores_T(n, b, h, j, q)
                            if nxt and q % 2 == 0:
                                scores(n + 1, nb, h, j, q // 2)
                            if not (first and j == 0):
                                weigh(n, b, h - 1, 1 - j, q)

                def self_attention(n, b, nxt):
                    pe.wait_ge(max_stacked[0], (n + 1) * 32)
                    nb = (n + 1) % B
                    heads(n, b, nb, nxt, 0, first=True)
                    pe.sem_inc(pe_passed, 1)
                    with pe.Fori(1, HP) as hp:
                        heads(n, b, nb, nxt, hp)
                    for t in range(TB):
                        weigh(n, b, H - 1, 1, t)

                def turn_max(n, k):
                    pe.wait_ge(nm_ready[k], n + 1)
                    out = ps[0:2 * H, 5, :].bitcast(BF16)
                    for t in range(TB):
                        last = pe.transpose(out[:, t * P:(t + 1) * P], nmp[:, t, :, :], m.identb[:])
                    last.then_inc(nm_turned[k], 1)

                def cross_max(n, b, hp):
                    for j in range(2):
                        h = 2 * hp + j
                        pe.wait_ge(max_done[1], n * H + h - 1 + CREDIT)
                        for t in range(TB):
                            last = pe.matmul(ps[:, j, t * CTX:(t + 1) * CTX], lhsT=qs[0:MAX_ROW, b, h, t * P:(t + 1) * P],
                                             rhs=kc[0:MAX_ROW, b, h, :], start=True, stop=True)
                        last.then_inc(s_done[1], 1)

                def cross_T(n, b, h, j):
                    pe.wait_ge(exp_done[1], n * H + h - 1 + CREDIT)
                    pe.matmul(ps[0:CTX, 2 + j, :], lhsT=kc[0:MAX_ROW + 2, b, h, :],
                              rhs=qs[0:MAX_ROW + 2, b, h, :],
                              start=True, stop=True).then_inc(st_done[1], 1)

                def cross_weigh(n, b, h, j):
                    pe.wait_ge(exp_done[1], n * H + h + 1 + CREDIT)
                    pe.wait_ge(pv_copied[1], n * H + h - 1 + CREDIT)
                    for t in range(TB):
                        last = pe.matmul(ps[:, 6 + j, t * (HD + 1):(t + 1) * (HD + 1)],
                                         lhsT=prob[0:CTX, j, 0, t * P:(t + 1) * P], rhs=vc[:, h, :],
                                         start=True, stop=True)
                    last.then_inc(pv_done[1], 1)

                def output(n, k):
                    pe.wait_ge(cn_ready[k], n + 1)
                    for t in range(TB):
                        last = pe.transpose(ps[:, 4, t * P:(t + 1) * P], cn[:, t, :], m.ident[:])
                    last.then_inc(c_turned[k], 1)
                    if k == 0:
                        pe.wait_ge(wcross_loaded, (n // B + 1) * 16)
                    pe.wait_ge(cT_ready[k], n + 1)
                    for t in range(TB):
                        last = pe.matmul(ps[:, 5, t * P:(t + 1) * P], lhsT=cT[:, t * P:(t + 1) * P],
                                         rhs=w[:, OCOL[k]:OCOL[k] + P], start=True, stop=True)
                    last.then_inc(out_done[k], 1)

                def rest(n, b):
                    output(n, 0)
                    turn_norm(n, 1)
                    project(n, 1)
                    stacks_there(n, 1)
                    with pe.Fori(0, HP) as hp:
                        cross_max(n, b, hp)
                    turn_max(n, 1)
                    pe.wait_ge(max_stacked[1], (n + 1) * 32)
                    cross_T(n, b, 0, 0)
                    cross_T(n, b, 1, 1)
                    cross_weigh(n, b, 0, 0)
                    with pe.Fori(1, HP) as hp:
                        cross_T(n, b, 2 * hp, 0)
                        cross_weigh(n, b, 2 * hp - 1, 1)
                        cross_T(n, b, 2 * hp + 1, 1)
                        cross_weigh(n, b, 2 * hp, 0)
                    cross_weigh(n, b, H - 1, 1)
                    output(n, 1)
                    turn_norm(n, 2)
                    pe.wait_ge(wff_loaded, (n // B + 1) * 16)
                    pe.wait_ge(hT_ready[2], n + 1)
                    for i in range(4):
                        pe.matmul(ps[:, i, :], lhsT=w[:, LF1 + i * P:LF1 + (i + 1) * P], rhs=hT[:],
                                  start=True, stop=True).then_inc(f1_done, 1)
                    for t in range(TB):
                        for i in range(4):
                            if t == 0:
                                pe.wait_ge(gelu_done, n * 4 + i + 1)
                            last = pe.matmul(ps[:, 4, t * P:(t + 1) * P], lhsT=u[:, i, t * P:(t + 1) * P],
                                             rhs=w[:, LF2 + i * P:LF2 + (i + 1) * P], start=i == 0, stop=i == 3)
                    last.then_inc(f2_done, 1)

                def begin(n):
                    turn_norm(n, 0)
                    project(n, 0)

                pe.wait_ge(ones_set, 3)
                pe.wait_ge(valid_ready, 4)
                begin(0)
                stacks_there(0, 0)
                with pe.Fori(0, HP) as hp:
                    for j in range(2):
                        scores(0, 0, 2 * hp + j, j, 0)
                        scores(0, 0, 2 * hp + j, j, 1)
                turn_max(0, 0)
                with pe.Fori(0, UNITS - 1) as n:
                    b = n % B
                    begin(n + 1)
                    stacks_there(n + 1, 0)
                    self_attention(n, b, True)
                    turn_max(n + 1, 0)
                    rest(n, b)
                pe.wait_ge(ff_added, UNITS - 1)
                self_attention(UNITS - 1, 1, False)
                rest(UNITS - 1, 1)

            @block.scalar
            def _(act):
                def copy_norm(n, i):
                    k = 3 + (n // B) * 3 + i
                    b = n % B
                    act.wait_ge(turned[i], n + 1)
                    act.activation(hT[:], ps[:, 7, :], ACT.Identity, bias=m.aff[:, k, 1, bass.ds(b, 1)],
                                   scale=m.aff[:, k, 0, bass.ds(b, 1)]).then_inc(hT_ready[i], 1)

                def split(n, k):
                    for i, (whole, p12) in enumerate(((q_sum[k], q_p12[k]), (k_sum[k], k_p12[k]))):
                        act.wait_ge(whole, n + 1)
                        width = NK[k] if i else S
                        act.activation(parts[:, i, 0, 0:width], full[:, i, 0:width], ACT.Copy).then_inc(p12, 1)
                    for i, (left, p12) in enumerate(((q_rem[k], q_p12[k]), (k_rem[k], k_p12[k]))):
                        act.wait_ge(left, n + 1)
                        width = NK[k] if i else S
                        act.activation(parts[:, i, 1, 0:width], rem[:, i, 0:width], ACT.Copy).then_inc(p12, 1)

                def values(n, b, k):
                    act.wait_ge(v_done[k], n + 1)
                    if k:
                        last = act.activation(vc[:, :, 0:HD], ps[0:CTX, 4, 0:P].rearrange("p (h d) -> p h d", d=HD),
                                              ACT.Copy, scale=validc[:, bass.ds(b, 1)])
                    else:
                        for t in range(TB):
                            last = act.activation(va[:, b, t, :, 0:HD],
                                                  ps[:, 4, t * P:(t + 1) * P].rearrange("p (h d) -> p h d", d=HD),
                                                  ACT.Copy, scale=valid[:, b, t:t + 1])
                    if k:
                        last = act.activation(vc[:, :, HD:HD + 1], validc[:, bass.ds(b, 1)]
                                              .rearrange("p (h o) -> p h o", o=1).broadcast_to([CTX, H, 1]), ACT.Copy)
                    last.then_inc(v_ready[k], 1)

                def copy_max(n, k, last=False):
                    act.wait_ge(nm_turned[k], n + 1)
                    if k == 1:
                        act.wait_ge(max_stacked[0], UNITS * 32 if last else (n + 2) * 32)
                    act.activation(nmT[:], ps[0:2 * H, 5, :].bitcast(BF16)[:, 0:S], ACT.Copy)\
                        .then_inc(nmT_ready[k], 1)

                def exps(n, h, j):
                    act.wait_ge(pv_done[0], n * H + h - 1 + CREDIT)
                    for kt in range(TB):
                        act.wait_ge(st_done[0], (n * H + h) * TB + kt + 1)
                        act.activation(prob[:, j, kt, :], ps[:, 4 + kt % 2, :], ACT.Exp, scale=SCALE)\
                            .then_inc(exp_done[0], 1)

                def copy_context(n, k):
                    act.wait_ge(c_turned[k], n + 1)
                    act.activation(cT[:], ps[:, 4, :], ACT.Copy).then_inc(cT_ready[k], 1)

                def begin(n):
                    copy_norm(n, 0)
                    values(n, n % B, 0)
                    split(n, 0)

                def rest(n, last=False):
                    copy_context(n, 0)
                    copy_norm(n, 1)
                    values(n, n % B, 1)
                    split(n, 1)
                    copy_max(n, 1, last)
                    with act.Fori(0, HP) as hp:
                        for j in range(2):
                            h = 2 * hp + j
                            act.wait_ge(pv_done[1], n * H + h - 1 + CREDIT)
                            act.wait_ge(st_done[1], n * H + h + 1)
                            act.activation(prob[0:CTX, j, 0, :], ps[0:CTX, 2 + j, :], ACT.Exp, scale=SCALE)\
                                .then_inc(exp_done[1], 1)
                    copy_context(n, 1)
                    copy_norm(n, 2)
                    for i in range(4):
                        act.wait_ge(f1_done, n * 4 + i + 1)
                        act.activation(u[:, i, :], ps[:, i, :], ACT.Gelu, bias=w[:, LB1 + i:LB1 + i + 1])\
                            .then_inc(gelu_done, 1)

                def self_exps(n):
                    with act.Fori(0, HP) as hp:
                        for j in range(2):
                            exps(n, 2 * hp + j, j)

                for k in range(2):
                    act.sem_inc(exp_done[k], CREDIT)
                act.wait_ge(valid_ready, 4)
                begin(0)
                copy_max(0, 0)
                with act.Fori(0, UNITS - 1) as n:
                    begin(n + 1)
                    self_exps(n)
                    copy_max(n + 1, 0)
                    rest(n)
                self_exps(UNITS - 1)
                rest(UNITS - 1, last=True)

            @block.vector
            def _(dve):
                c = Chain(dve, order)

                def norm(n, i):
                    b = n % B
                    norm_steps(c, dve, m, lambda t: m.y[:, b * TB + t, :], lambda t: m.xn[:, t, :], TB,
                               apart=dve_passed)
                    dve.sem_inc(xn_ready[i], 1)

                def rotate(n, k):
                    for i in range(2):
                        width = NK[k] if i else S
                        dve.wait_ge(proj_done[k], n * 2 + i + 1)
                        for r, table in enumerate((cos, sin)):
                            dve.tensor_tensor(rot[:, i, r, 0:width], ps[:, 2 * i + r, 0:width], table[:, 0:width],
                                              ALU.mult).then_inc(roped[k], 1)
                    dve.wait_ge(roped[k], n * 4 + 2)
                    dve.tensor_tensor(full[:, 0, :], rot[:, 0, 0, :], rot[:, 0, 1, :], ALU.add)\
                        .then_inc(q_sum[k], 1)
                    dve.wait_ge(q_p12[k], n * 2 + 1)
                    dve.tensor_tensor(rem[:, 0, :], full[:, 0, :], parts[:, 0, 0, :], ALU.subtract)\
                        .then_inc(q_rem[k], 1)
                    dve.wait_ge(q_p12[k], n * 2 + 2)
                    dve.tensor_tensor(parts[:, 0, 2, :], rem[:, 0, :], parts[:, 0, 1, :], ALU.subtract)\
                        .then_inc(q_p3[k], 1)

                def row_max(n, h, j, g):
                    i = 2 * j + g
                    dve.wait_ge(s_done[0], (n * H + h) * 2 + g + 1)
                    dve.tensor_reduce(nm[:, h, 2 * g:2 * g + 2], ps[:, 2 * (i % 2):2 * (i % 2) + 2, :],
                                      AX.X, ALU.max, negate=True).then_inc(max_done[0], 1)

                def copy_products(n, h, j, k):
                    dve.wait_ge(pv_done[k], n * H + h + 1 + CREDIT)
                    dve.tensor_copy(craw[:, :, h, :], ps[:, 6 + j, 0:TB * (HD + 1)]
                                    .rearrange("p (t d) -> p t d", d=HD + 1)).then_inc(pv_copied[k], 1)

                def split_max(n, k):
                    dve.wait_ge(max_done[k], (n + 1) * H * (2 if k == 0 else 1) + CREDIT)
                    by_tile = nm[:].rearrange("p h t -> p t h")
                    c.after(dve.tensor_copy(nmp[:, :, 0, :], by_tile))
                    dve.tensor_tensor(nmp[:, :, 1, :], by_tile, nmp[:, :, 0, :], ALU.subtract)\
                        .then_inc(nm_ready[k], 1)

                def normalise(n, k):
                    dve.wait_ge(pv_copied[k], (n + 1) * H + CREDIT)
                    c.after(dve.reciprocal(rden[:], craw[:, :, :, HD]))
                    dve.tensor_tensor(cn[:].rearrange("p t (h d) -> p t h d", d=HD), craw[:, :, :, 0:HD],
                                      rden[:].rearrange("p t (h o) -> p t h o", o=1)
                                      .broadcast_to([P, TB, H, HD]), ALU.mult).then_inc(cn_ready[k], 1)

                def add_bank(bank, b):
                    for t in range(TB):
                        y = m.y[:, b * TB + t, :]
                        c.after(dve.tensor_tensor(y, y, ps[:, bank, t * P:(t + 1) * P], ALU.add))

                def heads(n, nxt, hp, first=False):
                    for j in range(2):
                        h = 2 * hp + j
                        if nxt:
                            row_max(n + 1, h, j, 0)
                            row_max(n + 1, h, j, 1)
                        if not (first and j == 0):
                            copy_products(n, h - 1, 1 - j, 0)

                def self_attention(n, nxt):
                    heads(n, nxt, 0, first=True)
                    with dve.Fori(1, HP) as hp:
                        heads(n, nxt, hp)
                    if nxt:
                        split_max(n + 1, 0)
                    copy_products(n, H - 1, 1, 0)

                def rest(n):
                    b = n % B
                    normalise(n, 0)
                    dve.wait_ge(out_done[0], n + 1)
                    add_bank(5, b)
                    norm(n, 1)
                    rotate(n, 1)
                    with dve.Fori(0, HP) as hp:
                        for j in range(2):
                            h = 2 * hp + j
                            dve.wait_ge(s_done[1], n * H + h + 1)
                            dve.tensor_reduce(nm[:, h, :], ps[:, j, 0:TB * CTX]
                                              .rearrange("p (t k) -> p t k", k=CTX), AX.X, ALU.max, negate=True)\
                                .then_inc(max_done[1], 1)
                    split_max(n, 1)
                    with dve.Fori(0, HP) as hp:
                        for j in range(2):
                            copy_products(n, 2 * hp + j, j, 1)
                    normalise(n, 1)
                    dve.wait_ge(out_done[1], n + 1)
                    add_bank(5, b)
                    norm(n, 2)
                    for t in range(TB):
                        y = m.y[:, b * TB + t, :]
                        c.after(dve.tensor_tensor(y, y, m.rows[:, R_F2B + n // B, :], ALU.add))
                    dve.wait_ge(f2_done, n + 1)
                    add_bank(4, b)
                    dve.sem_inc(ff_added, 1)

                dve.wait_ge(zeroed, 3)
                dve.wait_ge(ones_set, 3)
                dve.wait_ge(const_loaded, 96)
                row = slice(MASK_ROW, MASK_ROW + 1)
                for b in range(B):
                    for one, source, width in ((ks, mrow, S), (kc, mrowc, CTX)):
                        c.step(dve.tensor_scalar(one[row, b, :, :], source[row, b:b + 1, :]
                                                 .broadcast_to([1, H, width]), NEG, None, ALU.mult))
                c.after(dve.tensor_scalar(valid[:], mk[:], -1.0, 1.0, ALU.mult, ALU.add))
                c.after(dve.tensor_scalar(validc[:], mkc[:], -1.0, 1.0, ALU.mult, ALU.add))
                for b in range(B):
                    for t in range(TB):
                        dve_ins = dve.tensor_copy(va[:, b, t, :, HD:HD + 1],
                                                  valid[:, b, t:t + 1].rearrange("p (h o) -> p h o", o=1)
                                                  .broadcast_to([P, H, 1]))
                        c.after(dve_ins)
                dve.sem_inc(valid_ready, 4)
                for sems in (max_done, pv_copied, pv_done):
                    for k in range(2):
                        dve.sem_inc(sems[k], CREDIT)
                norm(0, 0)
                rotate(0, 0)
                with dve.Fori(0, HP) as hp:
                    for j in range(2):
                        row_max(0, 2 * hp + j, j, 0)
                        row_max(0, 2 * hp + j, j, 1)
                split_max(0, 0)
                with dve.Fori(0, UNITS - 1) as n:
                    c.loop(n, C_STEPS)
                    norm(n + 1, 0)
                    rotate(n + 1, 0)
                    self_attention(n, True)
                    rest(n)
                    c.loop_end(UNITS - 1)
                self_attention(UNITS - 1, False)
                rest(UNITS - 1)
                c.after(dve.tensor_tensor(m.x[:], m.x[:], m.y[:], ALU.add))


C_STEPS = 3 * 24 + 2 + 2 + 16


def stage_d(nc, a, m):
    norm_block(nc, m, "D0n", first_only=True)
    with nc.sbuf_tensor("D_gT", [P, 2, T * P], BF16) as gT, nc.sbuf_tensor("D_sel", [P, PAIR_D, P], BF16) as sel:
        router_d(nc, a, m, gT, sel)
        experts_d(nc, a, m, gT, sel)


def router_d(nc, a, m, gT, sel):
    sem = lambda s: m.sem("D1_" + s)
    loaded, logits_done, scored, order, w_ready, turned, gT_ready, sel_set, sel_made = \
        (sem(s) for s in ("loaded", "logits_done", "scored", "order", "w_ready", "turned", "gT_ready",
                          "sel_set", "sel_made"))
    GE = E_D // G_D
    TAKEN = -2.0e30
    sb = lambda n, sh, dt=F32: nc.sbuf_tensor("D1_" + n, sh, dt)
    with sb("gw", [P, E_D]) as gw, sb("gb", [P, E_D]) as gb, sb("scores", [P, T, E_D]) as scores, \
            sb("sc", [P, T, E_D]) as sc, sb("top", [P, T, G_D, 8]) as top, sb("gs", [P, T, 16]) as gs, \
            sb("gtop", [P, T, 8]) as gtop, sb("grest", [P, T, 16]) as grest, sb("gmask", [P, T, G_D]) as gmask, \
            sb("masked", [P, T, E_D]) as masked, sb("off", [P, T, G_D]) as off, sb("etop", [P, T, 8]) as etop, \
            sb("erest", [P, T, E_D]) as erest, sb("wsum", [P, T]) as wsum, sb("wd", [P, T, E_D]) as wd, \
            sb("rem", [P, T * P]) as rem, nc.Block() as block:
        @block.sync
        def _(sp):
            sp.dma_start(gw[:], a["D_gw"]).then_inc(loaded, 16)
            sp.dma_start(gb[:], a["D_gb"].rearrange("(o e) -> o e", o=1).broadcast_to([P, E_D]))\
                .then_inc(loaded, 16)

        @block.gpsimd
        def _(pool):
            pool.memset(sel[:], 0.0).then_inc(sel_set, 1)
            pool.wait_ge(sel_set, 1)
            n = 0
            for part in range(2):
                for side in range(2):
                    view = sel[:, :, side * F_D:(side + 1) * F_D]
                    pool.affine_select(out=view, in_=view, compare_op=ALU.not_equal, fill=1.0,
                                       base=-E_D * part - side, pattern=[[-2, PAIR_D], [0, F_D]],
                                       channel_multiplier=1).then_inc(sel_made, 1)
                    n += 1
                    pool.wait_ge(sel_made, n)

        @block.tensor
        def _(pe):
            pe.wait_ge(loaded, 32)
            for t in range(T):
                last = pe.matmul(m.ps[:, 0, t * E_D:(t + 1) * E_D],
                                 lhsT=m.hT[:, t // TB, t % TB * P:(t % TB + 1) * P], rhs=gw[:],
                                 start=True, stop=True)
            last.then_inc(logits_done, 1)
            pe.wait_ge(w_ready, 1)
            for t in range(T):
                last = pe.transpose(m.ps[0:E_D, 1 + t // TB, t % TB * P:(t % TB + 1) * P], wd[:, t, :], m.ident[:])
            last.then_inc(turned, 1)

        @block.scalar
        def _(act):
            act.wait_ge(logits_done, 1)
            act.activation(scores[:], m.ps[:, 0, :].rearrange("p (t e) -> p t e", e=E_D), ACT.Sigmoid)\
                .then_inc(scored, 1)

        @block.vector
        def _(dve):
            c = Chain(dve, order)
            wide = lambda x, n: x.rearrange("p (t o) -> p t o", o=1).broadcast_to([P, T, n])
            c.step(dve.memset(gs[:], NEG))
            dve.wait_ge(loaded, 32)
            dve.wait_ge(scored, 1)
            c.after(dve.tensor_tensor(sc[:], scores[:], gb[:].rearrange("p (o e) -> p o e", o=1)
                                      .broadcast_to([P, T, E_D]), ALU.add))
            for t in range(T):
                for g in range(G_D):
                    c.step(dve.max(top[:, t, g, :], sc[:, t, g * GE:(g + 1) * GE]))
            dve.wait_ge(order, c.n)
            c.after(dve.tensor_tensor(gs[:, :, 0:G_D], top[:, :, :, 0], top[:, :, :, 1], ALU.add))
            for t in range(T):
                c.step(dve.max(gtop[:, t, :], gs[:, t, :]))
            dve.wait_ge(order, c.n)
            c.after(dve.memset(gtop[:, :, 4:8], NEG))
            for t in range(T):
                c.after(dve.match_replace(grest[:, t, :], gtop[:, t, :], gs[:, t, :], TAKEN))
            c.after(dve.tensor_scalar(gmask[:], grest[:, :, 0:G_D], TAKEN, None, ALU.is_equal))
            c.after(dve.tensor_scalar(off[:], gmask[:], -1.0, -NEG, ALU.add, ALU.mult))
            per_group = lambda x: x[:].rearrange("p t (g o) -> p t g o", o=1).broadcast_to([P, T, G_D, GE])
            by_group = lambda x: x[:].rearrange("p t (g e) -> p t g e", e=GE)
            c.after(dve.tensor_tensor(by_group(masked), by_group(sc), per_group(gmask), ALU.mult))
            c.after(dve.tensor_tensor(by_group(masked), by_group(masked), per_group(off), ALU.add))
            for t in range(T):
                c.step(dve.max(etop[:, t, :], masked[:, t, :]))
            dve.wait_ge(order, c.n)
            for t in range(T):
                c.after(dve.match_replace(erest[:, t, :], etop[:, t, :], masked[:, t, :], TAKEN))
            c.after(dve.scalar_tensor_tensor(wd[:], erest[:], TAKEN, scores[:], ALU.is_equal, ALU.mult))
            c.after(dve.tensor_reduce(wsum[:], wd[:], AX.X, ALU.add))
            c.after(dve.tensor_scalar(wsum[:], wsum[:], 1e-20, None, ALU.add))
            c.after(dve.reciprocal(wsum[:], wsum[:]))
            c.after(dve.tensor_tensor(wd[:], wd[:], wide(wsum[:], E_D), ALU.mult))
            dve.tensor_scalar(wd[:], wd[:], 2.5, None, ALU.mult).then_inc(w_ready, 1)
            dve.wait_ge(turned, 1)
            w_ps = m.ps[0:E_D, 1:3, :].rearrange("p b s -> p (b s)")
            lo, hi = slice(0, E_D), slice(E_D, P)
            c.after(dve.tensor_copy(gT[lo, 0, :], w_ps))
            c.after(dve.tensor_tensor(rem[lo, :], w_ps, gT[lo, 0, :], ALU.subtract))
            c.after(dve.tensor_copy(gT[lo, 1, :], rem[lo, :]))
            c.after(dve.tensor_copy(gT[hi, 0, :], gT[lo, 1, :]))
            dve.tensor_tensor(gT[lo, 1, :], rem[lo, :], gT[lo, 1, :], ALU.subtract).then_inc(gT_ready, 1)


def experts_d(nc, a, m, gT, sel):
    sem = lambda s: m.sem("D2_" + s)
    names = ("w_loaded0", "gate_done", "up_done", "wb_done", "silu_done", "mid_done", "h_ready", "down_done",
             "acc_ready", "acc_turned", "order")
    w_loaded, gate_done, up_done, wb_done, silu_done, mid_done, h_ready, down_done, acc_ready, acc_turned, order = \
        (sem(s) for s in names)
    closed = sem("closed")
    UN = 2
    w_loaded = [w_loaded, sem("w_loaded1")]
    with nc.sbuf_tensor("D2_w", [P, UN, 3, P], F32) as w, nc.sbuf_tensor("D2_ws", [P, 3, P], F32) as ws, \
            nc.sbuf_tensor("D2_g", [P, B, S], F32) as g, nc.sbuf_tensor("D2_t", [P, B, S], F32) as mid, \
            nc.sbuf_tensor("D2_h", [P, B, S], F32) as h, nc.sbuf_tensor("D2_acc", [P, B, S], F32) as acc, \
            nc.semaphore("D2_shared_loaded") as shared_loaded, nc.Block() as block:
        @block.sync
        def _(sp):
            sp.dma_start(ws[:], a["D_ws"]).then_inc(shared_loaded, 16)
            with sp.Fori(0, PAIR_D // UN) as i:
                for k in range(UN):
                    sp.wait_ge(down_done, (i * UN + 1) * B)
                    sp.dma_start(w[:, k, :, :], a["D_ew"][i * UN + k]).then_inc(w_loaded[k], 16)

        @block.tensor
        def _(pe):
            def pair(e, gate, up, down, rows, weigh, first, last):
                for b in range(B):
                    pe.matmul(m.ps[0:rows, b, :], lhsT=gate, rhs=m.hT[:, b, :], start=True, stop=True)\
                        .then_inc(gate_done, 1)
                    pe.matmul(m.ps[0:rows, 2 + b, :], lhsT=up, rhs=m.hT[:, b, :], start=True, stop=True)\
                        .then_inc(up_done, 1)
                    if weigh is not None:
                        pe.matmul(m.ps[:, 4 + b, :], lhsT=sel[:, weigh, :], rhs=gT[:, 0, b * S:(b + 1) * S],
                                  start=True, stop=False)
                        pe.matmul(m.ps[:, 4 + b, :], lhsT=sel[0:E_D, weigh, :],
                                  rhs=gT[0:E_D, 1, b * S:(b + 1) * S], start=False, stop=True).then_inc(wb_done, 1)
                for b in range(B):
                    pe.wait_ge(h_ready, e * B + b + 1)
                    pe.matmul(m.ps[:, 6 + b, :], lhsT=down, rhs=h[0:rows, b, :], start=first, stop=last).then_inc(down_done, 1)

            pe.wait_ge(shared_loaded, 16)
            pair(0, ws[:, 0, 0:F_D], ws[:, 1, 0:F_D], ws[0:F_D, 2, :], F_D, None, True, False)
            with pe.Fori(0, PAIR_D // UN) as i:
                for k in range(UN):
                    e = i * UN + k
                    pe.wait_ge(w_loaded[k], 16 * (i + 1))
                    pair(e + 1, w[:, k, 0, :], w[:, k, 1, :], w[:, k, 2, :], P, e, False, False)
            close_sums(pe, m, (6, 7), closed)
            pe.wait_ge(acc_ready, 2)
            for b in range(B):
                for t in range(TB):
                    last = pe.transpose(m.ps[:, b, t * P:(t + 1) * P], acc[:, b, t * P:(t + 1) * P], m.ident[:])
                last.then_inc(acc_turned, 1)

        @block.scalar
        def _(act):
            def pair(e, rows):
                for b in range(B):
                    act.wait_ge(gate_done, e * B + b + 1)
                    act.activation(g[0:rows, b, :], m.ps[0:rows, b, :], ACT.Silu).then_inc(silu_done, 1)

            pair(0, F_D)
            with act.Fori(0, PAIR_D) as e:
                pair(e + 1, P)

        @block.vector
        def _(dve):
            for b in range(B):
                dve.wait_ge(silu_done, b + 1)
                dve.wait_ge(up_done, b + 1)
                dve.tensor_tensor(h[0:F_D, b, :], g[0:F_D, b, :], m.ps[0:F_D, 2 + b, :], ALU.mult)\
                    .then_inc(h_ready, 1)
                dve.wait_ge(h_ready, b + 1)
                dve.sem_inc(mid_done, 1)
            with dve.Fori(1, PAIR_D + 1) as e:
                for b in range(B):
                    dve.wait_ge(silu_done, e * B + b + 1)
                    dve.wait_ge(up_done, e * B + b + 1)
                    dve.tensor_tensor(mid[:, b, :], g[:, b, :], m.ps[:, 2 + b, :], ALU.mult).then_inc(mid_done, 1)
                    dve.wait_ge(mid_done, e * B + b + 1)
                    dve.wait_ge(wb_done, e * B - B + b + 1)
                    dve.tensor_tensor(h[:, b, :], mid[:, b, :], m.ps[:, 4 + b, :], ALU.mult).then_inc(h_ready, 1)
            dve.wait_ge(closed, 1)
            for b in range(B):
                dve.tensor_copy(acc[:, b, :], m.ps[:, 6 + b, :]).then_inc(acc_ready, 1)
            c = Chain(dve, order)
            for b in range(B):
                x = m.x[:, b * TB:(b + 1) * TB, :]
                dve.wait_ge(acc_turned, b + 1)
                c.after(dve.tensor_tensor(x, x, m.ps[:, b, :].rearrange("p (t d) -> p t d", t=TB), ALU.add))


def kernel(**inputs):
    import numpy as np_
    import concourse.bacc as bacc
    from concourse.bass_utils import run_bass_kernel_spmd

    nc = bacc.Bacc("TRN2", target_bir_lowering=False, num_devices=1)
    arrays = lay_out({k: np_.asarray(v) for k, v in inputs.items()})
    aps = {n: nc.dram_tensor("in_" + n, x.shape, mybir.dt.from_np(x.dtype), kind="ExternalInput").ap()
           for n, x in arrays.items()}
    aps["out"] = nc.dram_tensor("out", (B * S, P), F32, kind="ExternalOutput").ap()
    build(nc, aps)
    r = run_bass_kernel_spmd(nc, [{"in_" + n: x for n, x in arrays.items()}], core_ids=[0])
    return r.results[0]["out"].reshape(B, S, P)


def lay_out(i):
    cat, stack = np.concatenate, np.stack
    out = {"x": i["x"].reshape(B * S, P), "condT": i["cond_1024"].T,
           "ctxT": i["ctx_1024"].transpose(2, 0, 1)}

    a, c = "L0_xcond_", "L1_xcond_"
    nw = [i[f"{a}norm{k}_w"] for k in (1, 2, 3)] + [i[f"{c}n{k}_w"][l].T for l in range(LAYERS) for k in (1, 2, 3)]
    nb = [i[f"{a}norm{k}_b"] for k in (1, 2, 3)] + [i[f"{c}n{k}_b"][l] for l in range(LAYERS) for k in (1, 2, 3)]
    out["norm_w"] = cat(nw, 1)
    out["norm_b"] = stack(nb).reshape(21, 2, P).transpose(2, 0, 1)
    f = "L0_ffn_"
    out["rows"] = cat([stack([i[a + "attn1_bo"], i[a + "attn2_bo"], i[a + "ff_b2"], i[f + "o_b"],
                              i[f + "gamma1"], i[f + "gamma2"]]), i[c + "f2_b"]])

    def pairs(q, qr, k, kr, v, o):
        cols = lambda x: x.reshape(P, PAIRS, P).transpose(1, 0, 2)
        return cat([cols(q), cols(qr), cols(k), cols(kr), cols(v), o.reshape(PAIRS, P, P)], 2)

    for n, s in (("A1_w", "attn1_"), ("A2_w", "attn2_")):
        q, k, v, o = (i[a + s + x] for x in ("wq", "wk", "wv", "wo"))
        out[n] = pairs(q, q, k, k, v, o)
    out["A_w1"] = i[a + "ff_w1"]
    out["A_b1"] = i[a + "ff_b1"].reshape(8, P).T
    out["A_w2"] = i[a + "ff_w2"].reshape(4, P, P).transpose(1, 0, 2)

    even_odd = np.arange(DH).reshape(DH // 2, 2).T.reshape(-1)
    order = (np.arange(H)[:, None] * DH + even_odd).reshape(-1)
    swap = (np.arange(H)[:, None] * DH + np.roll(even_odd, DH // 2)).reshape(-1)
    q, k, v, o = (i[f + x] for x in ("q_w", "k_w", "v_w", "o_w"))
    bq, bk, bv = (i[f + x] for x in ("q_b", "k_b", "v_b"))
    bias = stack([bq[order], bq[swap], bk[order], bk[swap], bv], 1).reshape(PAIRS, P, 5)
    out["B_bias"] = bias.transpose(1, 0, 2)
    out["B_w"] = pairs(q[:, order], q[:, swap], k[:, order], k[:, swap], v, o)
    half = DH // 2
    sign = np.tile(np.repeat(np.array([-1.0, 1.0], np.float32), half), 2)
    out["theta"] = stack([np.tile(i[f + "theta"], 4), sign], 1)
    out["positions"] = np.arange(S, dtype=np.float32)
    out["B_rw"], out["B_rb"] = i[f + "router_w"], i[f + "router_b"]
    w1 = cat([i[f + "re_w1"], i[f + "sh_w1"][None]])
    w2 = cat([i[f + "re_w2"], i[f + "sh_w2"][None]])
    b1 = cat([i[f + "re_b1"], i[f + "sh_b1"][None]])
    out["B_ew"] = cat([w1, w2, b1[:, :, None]], 2)
    out["B_b2"] = cat([i[f + "re_b2"], i[f + "sh_b2"][None]])

    place = (np.arange(HD)[:, None] + np.arange(H) * HD).reshape(-1)
    turned = (np.roll(np.arange(HD), HD // 2)[:, None] + np.arange(H) * HD).reshape(-1)
    layers = []
    for l in range(LAYERS):
        q, k, v = i[c + "qkv_w"][l].reshape(3, P, P)
        so, cq, ck, cv, co = (i[c + n + "_w"][l] for n in ("so", "cq", "ck", "cv", "co"))
        layers.append(cat([q[place].T, q[turned].T, k[place].T, k[turned].T, v.T, so.T, cq[place].T, cq[turned].T,
                           ck[place].T, ck[turned].T, cv.T, co.T, i[c + "f1_w"][l].T,
                           i[c + "f2_w"][l].T.reshape(4, P, P).transpose(1, 0, 2).reshape(P, 4 * P),
                           i[c + "f1_b"][l].reshape(4, P).T], 1))
    out["C_w"] = stack(layers)
    inv = (1.0 / np.float32(10000.0) ** (np.arange(HD // 2, dtype=np.float32) / np.float32(HD // 2)))
    angle = np.arange(S, dtype=np.float32)[:, None] * inv.astype(np.float32)
    row = np.repeat(np.arange(HD), H)
    side = np.where(row < HD // 2, np.float32(-1), np.float32(1))
    out["C_cos"] = np.cos(angle).T[row % (HD // 2)]
    out["C_sin"] = np.sin(angle).T[row % (HD // 2)] * side[:, None]
    ms, mc = i["mask_BxS_bf0"], i["mask_BxS2_bf0"]
    out["mask_rows"], out["maskc_rows"] = ms, mc
    out["mask_cols"] = ms.reshape(B, TB, P).transpose(2, 0, 1)
    out["maskc_cols"] = mc.T

    d = "L1_ffn_"
    out["D_gw"], out["D_gb"] = i[d + "gate_w"].T, i[d + "gate_bias"]
    side_by_side = lambda w: w.reshape(PAIR_D, 2, P, F_D).transpose(0, 2, 1, 3).reshape(PAIR_D, P, P)
    out["D_ew"] = stack([side_by_side(i[d + "We_gate"]), side_by_side(i[d + "We_up"]),
                         i[d + "We_down"].reshape(PAIR_D, P, P)], 2)
    wide = lambda w: cat([w, w], 1)
    down = i[d + "Ws_down"]
    out["D_ws"] = stack([wide(i[d + "Ws_gate"]), wide(i[d + "Ws_up"]), cat([down, down], 0)], 1)
    return {n: np.ascontiguousarray(x) for n, x in out.items()}
```

```python
from contextlib import ExitStack

import numpy as np
import concourse.bass as bass
from concourse import mybir

ALU = mybir.AluOpType
ACT = mybir.ActivationFunctionType
AX = mybir.AxisListType
F32 = mybir.dt.float32
BF16 = mybir.dt.bfloat16
I32 = mybir.dt.int32
U8 = mybir.dt.uint8

P = 128
B = 2
S = 512
TB = S // P
T = B * TB
CTX = 77
H = 16
DH = 64
PAIRS = H // 2
LAYERS = 6
HD = 8
EPS = 1e-5
NEG = -1.0e30
RSQRT_MAGIC = 0x5F3759DF

PW_Q, PW_QR, PW_K, PW_KR, PW_V, PW_O, PW = (P * i for i in range(7))
BIAS_V = 4

LQ, LQR, LK, LKR, LV = (P * i for i in range(5))
LSO, LCQ, LCQR, LCK, LCKR, LCV, LCO = (P * i for i in range(5, 12))
LF1 = 12 * P
LF2 = 16 * P
LB1 = 20 * P
LW = LB1 + 4
LOADS = ((LQ, LSO), (LSO, LF1), (LF1, LW))

R_BO1, R_BO2, R_FB2, R_OB, R_G1, R_G2, R_F2B = range(7)
ROWS = 6 + LAYERS

COMBOS = ((0, 0), (1, 0), (0, 1), (2, 0), (1, 1), (0, 2))
MASK_ROW = 64
QUAD = 4
QUADS = H // QUAD
VW = P // QUAD
MAX_ROW = 65

E_MOE = 32
E_R = 31
TOPK_PAD = 40
E_D = 64
F_D = 64
G_D = 8
PAIR_D = E_D // 2


class Chain:

    def __init__(self, eng, sem):
        self.eng, self.sem, self.base, self.n = eng, sem, 0, 0

    def step(self, ins):
        ins.then_inc(self.sem, 1)
        self.n += 1
        return ins

    def after(self, ins):
        self.step(ins)
        self.eng.wait_ge(self.sem, self.base + self.n)

    def loop(self, i, per):
        self.outer = (self.base, self.n, per)
        self.base, self.n = self.base + self.n + i * per, 0

    def loop_end(self, turns):
        base, n, per = self.outer
        assert self.n == per, (self.n, per)
        self.base, self.n = base, n + turns * per


def rstd_steps(c, dve, m, n, rms):
    v, y, t, u = m.lnv[:, 0:n], m.rs[:, 0:n], m.lnt[:, 0:n], m.lnu[:, 0:n]
    mean, var = m.mv[:, 0:n, 0], m.mv[:, 0:n, 1]
    if rms:
        c.after(dve.tensor_tensor(t, mean, mean, ALU.mult))
        c.after(dve.scalar_tensor_tensor(v, t, EPS, var, ALU.add, ALU.add))
    else:
        c.after(dve.tensor_scalar(v, var, EPS, None, ALU.add))
    c.after(dve.tensor_scalar(t.bitcast(I32), v.bitcast(I32), 1, None, ALU.arith_shift_right))
    c.after(dve.tensor_scalar(y.bitcast(I32), t.bitcast(I32), -1.0, float(RSQRT_MAGIC), ALU.mult, ALU.add))
    for _ in range(3):
        c.after(dve.tensor_tensor(t, y, y, ALU.mult))
        c.after(dve.scalar_tensor_tensor(u, t, -0.5, v, ALU.mult, ALU.mult))
        c.after(dve.scalar_tensor_tensor(y, u, 1.5, y, ALU.add, ALU.mult))


def norm_steps(c, dve, m, src, dst, n, rms=False, row=None, apart=None):
    if apart:
        dve.sem_inc(apart, 1)
    for t in range(n):
        ins = dve.bn_stats(m.st[:, t, :], src(t))
        c.after(ins) if t == n - 1 else c.step(ins)
    if apart:
        dve.sem_inc(apart, 1)
    for t in range(n):
        ins = dve.bn_aggr(m.mv[:, t, :], m.st[:, t, :])
        c.after(ins) if t == n - 1 else c.step(ins)
    rstd_steps(c, dve, m, n, rms)
    for t in range(n):
        if rms:
            ins = dve.scalar_tensor_tensor(dst(t), src(t), m.rs[:, t:t + 1], row, ALU.mult, ALU.mult)
        else:
            ins = dve.tensor_scalar(dst(t), src(t), m.mv[:, t, 0:1], m.rs[:, t:t + 1], ALU.subtract, ALU.mult)
        c.after(ins) if t == n - 1 else c.step(ins)


def close_sums(pe, m, banks, closed):
    for bank in banks:
        last = pe.matmul(m.ps[:, bank, :], lhsT=m.zero[:, 0:P], rhs=m.zero[:], start=False, stop=True)
    last.then_inc(closed, 1)


class Mem:
    pass


def build(nc, a, debug=None):
    ctx = ExitStack()
    with ctx:
        def sb(name, shape, dt=F32):
            return ctx.enter_context(nc.sbuf_tensor(name, shape, dt))

        taken = []

        def sem(name):
            taken.append(nc.alloc_semaphore(name=name))
            return taken[-1]

        def next_stage():
            nc.clear_and_free_semaphores(taken)
            taken.clear()
            nc.all_engine_barrier()

        m = Mem()
        m.sb, m.sem = sb, sem
        m.x = sb("x", [P, T, P])
        m.y = sb("y", [P, T, P])
        m.xn = sb("xn", [P, T, P])
        m.hT = sb("hT", [P, B, S])
        m.st = sb("st", [P, T, 6])
        m.mv = sb("mv", [P, T, 2])
        m.lnv = sb("lnv", [P, T])
        m.lnt = sb("lnt", [P, T])
        m.lnu = sb("lnu", [P, T])
        m.rs = sb("rs", [P, T])
        m.ident = sb("ident", [P, P])
        m.identb = sb("identb", [P, P], BF16)
        m.zero = sb("zero", [1, S], BF16)
        m.condT = sb("condT", [P, B])
        m.ctxT = sb("ctxT", [P, B, CTX])
        m.aff = sb("aff", [P, 21, 2, B])
        m.rows = sb("rows", [P, ROWS, P])
        m.ps = ctx.enter_context(nc.psum_tensor("ps", [P, 8, 512], F32))

        start(nc, a, m)
        stage_a(nc, a, m)
        next_stage()
        if debug == "A":
            return finish(nc, a, m)
        stage_b(nc, a, m)
        next_stage()
        if debug == "B":
            return finish(nc, a, m)
        stage_c(nc, a, m)
        next_stage()
        if debug == "C":
            return finish(nc, a, m)
        stage_d(nc, a, m)
        finish(nc, a, m)


def finish(nc, a, m):
    stored = m.sem("stored")
    with nc.Block() as block:
        @block.sync
        def _(sp):
            sp.dma_start(a["out"].rearrange("(t p) d -> p t d", p=P), m.x[:]).then_inc(stored, 16)
            sp.wait_ge(stored, 16)


def start(nc, a, m):
    loaded, ident_set, ident_made = m.sem("loaded"), m.sem("ident_set"), m.sem("ident_made")
    emb_done = m.sem("emb_done")
    aff_done = m.sem("aff_done")
    with nc.sbuf_tensor("normw", [P, 21 * 2 * P], F32) as normw, \
            nc.sbuf_tensor("normb", [P, 21, 2], F32) as normb, nc.Block() as block:
        @block.sync
        def _(sp):
            sp.dma_start(m.condT[:], a["condT"]).then_inc(loaded, 16)
            sp.dma_start(normw[:], a["norm_w"]).then_inc(loaded, 16)
            sp.dma_start(normb[:], a["norm_b"]).then_inc(loaded, 16)
            sp.dma_start(m.x[:], a["x"].rearrange("(t p) d -> p t d", p=P)).then_inc(loaded, 16)
            sp.dma_start(m.ctxT[:], a["ctxT"]).then_inc(loaded, 16)
            sp.dma_start(m.rows[:], a["rows"].rearrange("(o r) d -> o r d", o=1).broadcast_to([P, ROWS, P]))\
                .then_inc(loaded, 16)

        @block.gpsimd
        def _(pool):
            pool.memset(m.ident[:], 0.0).then_inc(ident_set, 1)
            pool.memset(m.identb[:], 0.0).then_inc(ident_set, 1)
            pool.wait_ge(ident_set, 2)
            for one in (m.ident, m.identb):
                pool.affine_select(out=one[:], in_=one[:], compare_op=ALU.not_equal, fill=1.0, base=0,
                                   pattern=[[-1, P]], channel_multiplier=1).then_inc(ident_made, 1)

        @block.tensor
        def _(pe):
            pe.wait_ge(loaded, 96)
            emb = m.ps[:, 0, 0:84].rearrange("p (k b) -> p k b", b=B)
            for k in range(42):
                last = pe.matmul(emb[:, k, :], lhsT=normw[:, k * P:(k + 1) * P], rhs=m.condT[:],
                                 start=True, stop=True)
            last.then_inc(emb_done, 1)

        @block.vector
        def _(dve):
            c = Chain(dve, aff_done)
            dve.wait_ge(emb_done, 1)
            emb = m.ps[:, 0, 0:84].rearrange("p (k s b) -> p k s b", s=2, b=B)
            for b in range(B):
                c.after(dve.tensor_tensor(m.aff[:, :, :, b], emb[:, :, :, b], normb[:], ALU.add))
            c.after(dve.tensor_scalar(m.aff[:, :, 0, :], m.aff[:, :, 0, :], 1.0, None, ALU.add))
            c.after(dve.memset(m.zero[:], 0.0))
            dve.wait_ge(ident_made, 2)


def norm_block(nc, m, name, k=None, first=None, add_row=None, rms_row=None, to_y=False,
               first_only=False):
    order = m.sem(name + "_order")
    xn_ready, turned, hT_ready = m.sem(name + "_xn"), m.sem(name + "_turned"), m.sem(name + "_hT")
    with nc.Block() as block:
        @block.vector
        def _(dve):
            c = Chain(dve, order)
            if first:
                norm_steps(c, dve, m, lambda t: m.x[:, t, :], lambda t: m.y[:, t, :], T)
            row = None if rms_row is None else m.rows[:, rms_row, :]
            source = m.x if first_only else m.y
            norm_steps(c, dve, m, lambda t: source[:, t, :], lambda t: m.xn[:, t, :], T, rms_row is not None, row)
            dve.sem_inc(xn_ready, 1)
            if to_y:
                c.after(dve.tensor_copy(m.y[:], m.xn[:]))
            if add_row is not None:
                c.after(dve.tensor_tensor(m.y[:], m.y[:],
                                          m.rows[:, add_row:add_row + 1, :].broadcast_to([P, T, P]), ALU.add))

        @block.tensor
        def _(pe):
            pe.wait_ge(xn_ready, 1)
            for b in range(B):
                for t in range(TB):
                    last = pe.transpose(m.ps[:, b, t * P:(t + 1) * P], m.xn[:, b * TB + t, :], m.ident[:])
                last.then_inc(turned, 1)

        @block.scalar
        def _(act):
            for b in range(B):
                act.wait_ge(turned, b + 1)
                if k is None:
                    act.activation(m.hT[:, b, :], m.ps[:, b, :], ACT.Copy).then_inc(hT_ready, 1)
                else:
                    act.activation(m.hT[:, b, :], m.ps[:, b, :], ACT.Identity, bias=m.aff[:, k, 1, b:b + 1],
                                   scale=m.aff[:, k, 0, b:b + 1]).then_inc(hT_ready, 1)


def attention_block(nc, m, w_pairs, name, cross=False, rope=None, causal=False, biases=None):
    sem = lambda s: m.sem(f"{name}_{s}")
    w_loaded, wo_loaded, bias_loaded = sem("w_loaded"), sem("wo_loaded"), sem("bias_loaded")
    proj_done, v_done = sem("proj_done"), sem("v_done")
    q_ready, k_summed, k_ready, v_ready = sem("q_ready"), sem("k_summed"), sem("k_ready"), sem("v_ready")
    roped = sem("roped")
    s_done, max_done = sem("s_done"), sem("max_done")
    nm_ready, nm_turned, nmT_ready = sem("nm_ready"), sem("nm_turned"), sem("nmT_ready")
    st_done, exp_done, pv_done = sem("st_done"), sem("exp_done"), sem("pv_done")
    cn_ready, cT_ready = sem("cn_ready"), sem("cT_ready")
    out_done, y_added = sem("out_done"), sem("y_added")
    ones_set, order, passed = sem("ones_set"), sem("order"), sem("passed")

    NK = CTX if cross else S
    groups = [list(range(TB))] if cross else [[t] for t in range(TB)]
    key_tiles = [(0, CTX)] if cross else [(j * P, P) for j in range(TB)]
    NG, KT = len(groups), len(key_tiles)
    units = [(b, h) for b in range(B) for h in range(2)]
    U = len(units)
    keys = lambda t: (t + 1) * P if causal else NK
    first_q = lambda j: j * P if causal else 0
    SCALE = 0.125
    SET = 7

    with nc.sbuf_tensor(name + "_w", [P, PW], F32) as w, \
            nc.sbuf_tensor(name + "_wo", [P, P], F32) as wo, \
            nc.sbuf_tensor(name + "_bias", [P, PAIRS, 5], F32) as bias, \
            nc.sbuf_tensor(name + "_q", [P, B, S], F32) as qT, \
            nc.sbuf_tensor(name + "_k", [P, B, S], F32) as kT, \
            nc.sbuf_tensor(name + "_kz", [P, B, 2, S], F32) as kz, \
            nc.sbuf_tensor(name + "_rot", [P, B, 2, 2, S], F32) as rot, \
            nc.sbuf_tensor(name + "_v", [P, B, KT, 2, P], F32) as v, \
            nc.sbuf_tensor(name + "_nm", [P, B, 2, TB], F32) as nm, \
            nc.sbuf_tensor(name + "_nmp", [P, B, 2, TB, 2], BF16) as nmp, \
            nc.sbuf_tensor(name + "_nmT", [P, B, 2, S], BF16) as nmT, \
            nc.sbuf_tensor(name + "_ones", [P, P], BF16) as ones2, \
            nc.sbuf_tensor(name + "_p", [P, 2, KT, S], F32) as prob, \
            nc.sbuf_tensor(name + "_rden", [P, B, S], F32) as rden, \
            nc.sbuf_tensor(name + "_cn", [P, B, S], F32) as cn, \
            nc.sbuf_tensor(name + "_cT", [P, B, S], F32) as cT, nc.Block() as block:

        @block.sync
        def _(sp):
            if rope is not None:
                sp.dma_start(bias[:], biases).then_inc(bias_loaded, 16)
            sp.dma_start(w[:, 0:PW_O], w_pairs[0][:, 0:PW_O]).then_inc(w_loaded, 16)
            sp.dma_start(wo[:], w_pairs[0][:, PW_O:PW_O + P]).then_inc(wo_loaded, 16)
            with sp.Fori(1, PAIRS) as p:
                sp.wait_ge(v_done, p * B)
                sp.dma_start(w[:, 0:PW_O], w_pairs[p][:, 0:PW_O]).then_inc(w_loaded, 16)
                sp.wait_ge(out_done, p * B)
                sp.dma_start(wo[:], w_pairs[p][:, PW_O:PW_O + P]).then_inc(wo_loaded, 16)

        @block.gpsimd
        def _(pool):
            pool.memset(ones2[:], 1.0).then_inc(ones_set, 1)
            pool.memset(kz[:], 0.0).then_inc(ones_set, 1)
            pool.memset(nmT[:], 0.0).then_inc(ones_set, 1)
            pool.memset(prob[:], 0.0).then_inc(ones_set, 1)
            pool.memset(v[:], 0.0).then_inc(ones_set, 1)
            for h in range(2):
                pool.wait_ge(ones_set, 5 + h)
                pool.memset(v[0:key_tiles[0][1], :, :, h, DH * (1 - h):DH * (2 - h)], 1.0).then_inc(ones_set, 1)
            if rope is not None:
                with pool.Fori(0, PAIRS) as p:
                    for b in range(B):
                        for i, (dst, ready) in enumerate(((qT, q_ready), (kT, k_summed))):
                            pool.wait_ge(roped, (p * B + b) * 4 + 2 * i + 2)
                            pool.tensor_tensor(dst[:, b, :], rot[:, b, i, 0, :], rot[:, b, i, 1, :], ALU.add)\
                                .then_inc(ready, 1)

        @block.tensor
        def _(pe):
            pe.wait_ge(ones_set, SET)

            def project(p, b):
                n = p * B + b
                jobs = ((0, PW_Q, 0), (1, PW_K, 2))
                for i, col, bank in jobs:
                    if b == 1:
                        if rope is None:
                            pe.wait_ge((q_ready, k_ready)[i], n)
                        else:
                            pe.wait_ge(roped, (n - 1) * 4 + 2 * i + 2)
                    source = m.ctxT[:, b, :] if cross and i else m.hT[:, b, :]
                    width = CTX if cross and i else S
                    last = pe.matmul(m.ps[:, bank, 0:width], lhsT=w[:, col:col + P], rhs=source,
                                     start=True, stop=True)
                    if rope is not None:
                        last = pe.matmul(m.ps[:, bank + 1, 0:width], lhsT=w[:, col + P:col + 2 * P], rhs=source,
                                         start=True, stop=True)
                    last.then_inc(proj_done, 1)
                for j, (k0, kn) in enumerate(key_tiles):
                    source = m.ctxT[:, b, :] if cross else m.hT[:, b, k0:k0 + kn]
                    last = pe.matmul(m.ps[0:kn, 4 + b, j * P:(j + 1) * P], lhsT=source,
                                     rhs=w[:, PW_V:PW_V + P], start=True, stop=True)
                last.then_inc(v_done, 1)

            def scores(p, u):
                b, h = units[u]
                if h == 0:
                    pe.wait_ge(q_ready, p * B + b + 1)
                    pe.wait_ge(k_ready, p * B + b + 1)
                for g, tiles in enumerate(groups):
                    i = u * NG + g
                    if i >= 2:
                        pe.wait_ge(max_done, p * U * NG + i - 1)
                    elif u == 0:
                        if rope is None:
                            pe.wait_ge(q_ready, (p + 1) * B)
                            pe.wait_ge(k_ready, (p + 1) * B)
                        else:
                            pe.wait_ge(roped, (p + 1) * B * 4)
                    for s, t in enumerate(tiles):
                        n = keys(t)
                        last = pe.matmul(m.ps[:, i % 2, s * NK:s * NK + n],
                                         lhsT=qT[:, b, t * P:(t + 1) * P],
                                         rhs=kz[:, b, h, 0:n], start=True, stop=not causal)
                        if causal:
                            last = pe.matmul(m.ps[:, i % 2, n - P:n], lhsT=m.identb[:], rhs=m.maskq[:],
                                             start=False, stop=True)
                    last.then_inc(s_done, 1)

            def turn_max(p, b):
                pe.wait_ge(nm_ready, p * B + b + 1)
                if b == 1:
                    pe.wait_ge(nmT_ready, p * B + 1)
                out = m.ps[0:2, 6, :].bitcast(BF16)
                for h in range(2):
                    for t in range(TB):
                        c = (h * TB + t) * P
                        last = pe.transpose(out[:, c:c + P], nmp[:, b, h, t, :], m.identb[:])
                last.then_inc(nm_turned, 1)

            def scores_T(p, u):
                b, h = units[u]
                if h == 0:
                    pe.wait_ge(nmT_ready, p * B + b + 1)
                for j, (k0, kn) in enumerate(key_tiles):
                    i = u * KT + j
                    if i >= 2:
                        pe.wait_ge(exp_done, p * U * KT + i - 1)
                    q0 = first_q(j)
                    bank = m.ps[0:kn, 2 + i % 2, q0:S]
                    pe.matmul(bank, lhsT=kz[:, b, h, k0:k0 + kn], rhs=qT[:, b, q0:S],
                              start=True, stop=False)
                    last = pe.matmul(bank, lhsT=ones2[:, 0:kn], rhs=nmT[:, b, h, q0:S], start=False,
                                     stop=not causal)
                    if causal:
                        last = pe.matmul(m.ps[0:kn, 2 + i % 2, q0:q0 + P], lhsT=m.identb[:], rhs=m.maskk[:],
                                         start=False, stop=True)
                    last.then_inc(st_done, 1)

            def weigh(p, u):
                b, h = units[u]
                if h == 0:
                    pe.wait_ge(v_ready, p * B + b + 1)
                pe.wait_ge(exp_done, (p * U + u + 1) * KT)
                if u >= 2:
                    pe.wait_ge(cn_ready, p * U + u - 1)
                js = [0, 2, 3, 1] if causal else list(range(KT))
                for j in js:
                    c0 = 0 if j == js[-1] else first_q(j)
                    last = pe.matmul(m.ps[:, 4 + u % 2, c0:S], lhsT=v[:, b, j, h, :],
                                     rhs=prob[:, u % 2, j, c0:S], start=j == js[0], stop=j == js[-1])
                last.then_inc(pv_done, 1)

            def project_out(p, b):
                pe.wait_ge(cT_ready, p * B + b + 1)
                if b == 1:
                    pe.wait_ge(y_added, p * B + b)
                if b == 0:
                    pe.wait_ge(wo_loaded, 16 * (p + 1))
                for t in range(TB):
                    last = pe.matmul(m.ps[:, 7, t * P:(t + 1) * P], lhsT=cT[:, b, t * P:(t + 1) * P],
                                     rhs=wo[:], start=True, stop=True)
                last.then_inc(out_done, 1)

            with pe.Fori(0, PAIRS) as p:
                pe.wait_ge(w_loaded, 16 * (p + 1))
                project(p, 0)
                project(p, 1)
                scores(p, 0)
                scores(p, 1)
                scores(p, 2)
                turn_max(p, 0)
                scores_T(p, 0)
                scores(p, 3)
                scores_T(p, 1)
                weigh(p, 0)
                turn_max(p, 1)
                scores_T(p, 2)
                weigh(p, 1)
                scores_T(p, 3)
                weigh(p, 2)
                project_out(p, 0)
                weigh(p, 3)
                project_out(p, 1)

        @block.scalar
        def _(act):
            def evacuate(p, b):
                if rope is None:
                    act.wait_ge(proj_done, (p * B + b) * 2 + 1)
                    act.activation(qT[:, b, :], m.ps[:, 0, :], ACT.Copy).then_inc(q_ready, 1)
                    act.wait_ge(proj_done, (p * B + b) * 2 + 2)
                else:
                    act.wait_ge(k_summed, p * B + b + 1)
                for h in range(2):
                    half = slice(DH * h, DH * (h + 1))
                    source = m.ps[half, 2, 0:NK] if rope is None else kT[half, b, :]
                    last = act.activation(kz[half, b, h, 0:NK], source, ACT.Copy)
                last.then_inc(k_ready, 1)

            def copy_max(p, b):
                act.wait_ge(nm_turned, p * B + b + 1)
                act.activation(nmT[0:2, b, :, :], m.ps[0:2, 6, :].bitcast(BF16).rearrange("r (h q) -> r h q", h=2),
                               ACT.Copy).then_inc(nmT_ready, 1)

            def exps(p, u):
                if u >= 2:
                    act.wait_ge(pv_done, p * U + u - 1)
                for j, (k0, kn) in enumerate(key_tiles):
                    q0 = first_q(j)
                    act.wait_ge(st_done, (p * U + u) * KT + j + 1)
                    act.activation(prob[0:kn, u % 2, j, q0:S], m.ps[0:kn, 2 + (u * KT + j) % 2, q0:S], ACT.Exp,
                                   scale=SCALE).then_inc(exp_done, 1)

            def copy_context(p, b):
                act.wait_ge(cn_ready, p * U + 2 * b + 2)
                if rope is not None:
                    act.sem_inc(passed, 1)
                act.activation(cT[:, b, :], cn[:, b, :], ACT.Identity,
                               bias=bias[:, p, BIAS_V:BIAS_V + 1] if rope is not None else 0.0)\
                    .then_inc(cT_ready, 1)

            if rope is not None:
                act.wait_ge(bias_loaded, 16)
            act.wait_ge(ones_set, SET)
            with act.Fori(0, PAIRS) as p:
                evacuate(p, 0)
                evacuate(p, 1)
                copy_max(p, 0)
                exps(p, 0)
                exps(p, 1)
                copy_max(p, 1)
                exps(p, 2)
                exps(p, 3)
                copy_context(p, 0)
                copy_context(p, 1)

        @block.vector
        def _(dve):
            c = Chain(dve, order)
            dve.wait_ge(ones_set, SET)
            if rope is not None:
                dve.wait_ge(bias_loaded, 16)

            def evacuate_v(p, b):
                dve.wait_ge(v_done, p * B + b + 1)
                kn = key_tiles[0][1]
                for h in range(2):
                    last = dve.tensor_copy(v[0:kn, b, :, h, DH * h:DH * (h + 1)],
                                           m.ps[0:kn, 4 + b, 0:KT * P].rearrange("p (t h d) -> p t h d", h=2, d=DH)
                                           [:, :, h, :])
                last.then_inc(v_ready, 1)

            def rotate(p, b):
                for i in range(2):
                    dve.wait_ge(proj_done, (p * B + b) * 2 + i + 1)
                    for r, table in enumerate(rope):
                        col = 2 * i + r
                        dve.scalar_tensor_tensor(rot[:, b, i, r, :], m.ps[:, 2 * i + r, :], bias[:, p, col:col + 1],
                                                 table[:], ALU.add, ALU.mult).then_inc(roped, 1)

            def row_max(p, u):
                b, h = units[u]
                for g, tiles in enumerate(groups):
                    i = u * NG + g
                    n = keys(tiles[0])
                    dve.wait_ge(s_done, p * U * NG + i + 1)
                    dve.tensor_reduce(nm[:, b, h, tiles[0]:tiles[-1] + 1],
                                      m.ps[:, i % 2, 0:len(tiles) * n].rearrange("p (t k) -> p t k", k=n),
                                      AX.X, ALU.max, negate=True).then_inc(max_done, 1)

            def split_max(p, b):
                dve.wait_ge(max_done, (p * U + 2 * b + 2) * NG)
                c.after(dve.tensor_copy(nmp[:, b, :, :, 0], nm[:, b, :, :]))
                dve.tensor_tensor(nmp[:, b, :, :, 1], nm[:, b, :, :], nmp[:, b, :, :, 0], ALU.subtract)\
                    .then_inc(nm_ready, 1)

            def normalise(p, u):
                b, h = units[u]
                dve.wait_ge(pv_done, p * U + u + 1)
                mine, other = slice(DH * h, DH * (h + 1)), slice(DH * (1 - h), DH * (2 - h))
                c.after(dve.reciprocal(rden[mine, b, :], m.ps[other, 4 + u % 2, :]))
                dve.tensor_tensor(cn[mine, b, :], m.ps[mine, 4 + u % 2, :], rden[mine, b, :], ALU.mult)\
                    .then_inc(cn_ready, 1)

            def add_out(p, b):
                dve.wait_ge(out_done, p * B + b + 1)
                y = m.y[:, b * TB:(b + 1) * TB, :]
                dve.tensor_tensor(y, y, m.ps[:, 7, :].rearrange("p (t d) -> p t d", t=TB), ALU.add)\
                    .then_inc(y_added, 1)

            with dve.Fori(0, PAIRS) as p:
                c.loop(p, B + U)
                if rope is not None:
                    rotate(p, 0)
                evacuate_v(p, 0)
                if rope is not None:
                    rotate(p, 1)
                evacuate_v(p, 1)
                row_max(p, 0)
                row_max(p, 1)
                split_max(p, 0)
                row_max(p, 2)
                row_max(p, 3)
                split_max(p, 1)
                normalise(p, 0)
                normalise(p, 1)
                normalise(p, 2)
                add_out(p, 0)
                normalise(p, 3)
                add_out(p, 1)
                c.loop_end(PAIRS)


def stage_a(nc, a, m):
    norm_block(nc, m, "A1n", k=0, first=True, add_row=R_BO1)
    attention_block(nc, m, a["A1_w"], "A1")
    norm_block(nc, m, "A2n", k=1, add_row=R_BO2)
    attention_block(nc, m, a["A2_w"], "A2", cross=True)
    norm_block(nc, m, "A3n", k=2, add_row=R_FB2)
    C4 = 4
    sem = lambda s: m.sem("A3_" + s)
    loaded, g_done, a_done, gelu_done, u_ready, f_done, y_added = \
        (sem(s) for s in ("loaded", "g_done", "a_done", "gelu_done", "u_ready", "f_done", "y_added"))
    with nc.sbuf_tensor("A3_w1", [P, 8 * P], F32) as w1, nc.sbuf_tensor("A3_b1", [P, 8], F32) as b1, \
            nc.sbuf_tensor("A3_w2", [P, C4, P], F32) as w2, \
            nc.sbuf_tensor("A3_g", [P, 2, S], F32) as g, \
            nc.sbuf_tensor("A3_u", [P, B, C4, S], F32) as u, nc.Block() as block:
        @block.sync
        def _(sp):
            sp.dma_start(w1[:], a["A_w1"]).then_inc(loaded, 16)
            sp.dma_start(b1[:], a["A_b1"]).then_inc(loaded, 16)
            sp.dma_start(w2[:], a["A_w2"]).then_inc(loaded, 16)

        @block.tensor
        def _(pe):
            pe.wait_ge(loaded, 48)
            for b in range(B):
                for i in range(C4):
                    n = b * C4 + i
                    if n >= 2:
                        pe.wait_ge(gelu_done, n - 1)
                    pe.matmul(m.ps[:, n % 2, :], lhsT=w1[:, (C4 + i) * P:(C4 + i + 1) * P], rhs=m.hT[:, b, :],
                              start=True, stop=True).then_inc(g_done, 1)
                    if n >= 2:
                        pe.wait_ge(u_ready, n - 1)
                    pe.matmul(m.ps[:, 2 + n % 2, :], lhsT=w1[:, i * P:(i + 1) * P], rhs=m.hT[:, b, :],
                              start=True, stop=True).then_inc(a_done, 1)
                for t in range(TB):
                    for i in range(C4):
                        if t == 0:
                            pe.wait_ge(u_ready, b * C4 + i + 1)
                        last = pe.matmul(m.ps[:, 4 + b, t * P:(t + 1) * P], lhsT=u[:, b, i, t * P:(t + 1) * P],
                                         rhs=w2[:, i, :], start=i == 0, stop=i == C4 - 1)
                last.then_inc(f_done, 1)

        @block.scalar
        def _(act):
            act.wait_ge(loaded, 48)
            for n in range(B * C4):
                act.wait_ge(g_done, n + 1)
                if n >= 2:
                    act.wait_ge(u_ready, n - 1)
                act.activation(g[:, n % 2, :], m.ps[:, n % 2, :], ACT.Gelu,
                               bias=b1[:, C4 + n % C4:C4 + n % C4 + 1]).then_inc(gelu_done, 1)

        @block.vector
        def _(dve):
            dve.wait_ge(loaded, 48)
            for b in range(B):
                for i in range(C4):
                    n = b * C4 + i
                    dve.wait_ge(gelu_done, n + 1)
                    dve.wait_ge(a_done, n + 1)
                    dve.scalar_tensor_tensor(u[:, b, i, :], m.ps[:, 2 + n % 2, :], b1[:, i:i + 1], g[:, n % 2, :],
                                             ALU.add, ALU.mult).then_inc(u_ready, 1)
            c = Chain(dve, y_added)
            for b in range(B):
                dve.wait_ge(f_done, b + 1)
                y, x = m.y[:, b * TB:(b + 1) * TB, :], m.x[:, b * TB:(b + 1) * TB, :]
                c.after(dve.tensor_tensor(y, y, m.ps[:, 4 + b, :].rearrange("p (t d) -> p t d", t=TB), ALU.add))
                c.after(dve.tensor_tensor(x, x, y, ALU.add))


def rope_tables(nc, a, m, cos, sin):
    sem = lambda s: m.sem("rope_" + s)
    loaded, order, reduced, done, zeroed, masked = (sem(s) for s in
                                                   ("loaded", "order", "reduced", "done", "zeroed", "masked"))
    TWO_PI = 6.283185307179586
    C1 = 6.28125
    C2 = float(np.float32(np.float64(TWO_PI - C1)).view(np.uint32) & 0xFFFFF000)
    C2 = float(np.uint32(np.float32(TWO_PI - C1).view(np.uint32) & 0xFFFFF000).view(np.float32))
    C3 = float(np.float32(TWO_PI - C1 - C2))
    ROUND = 12582912.0
    with nc.sbuf_tensor("rope_in", [P, 2], F32) as tin, nc.sbuf_tensor("rope_pos", [P, S], F32) as pos, \
            nc.sbuf_tensor("rope_n", [P, S], F32) as nrm, nc.sbuf_tensor("rope_r", [P, 2, S], F32) as r, \
            nc.sbuf_tensor("rope_t", [P, S], F32) as t, nc.Block() as block:
        @block.sync
        def _(sp):
            sp.dma_start(tin[:], a["theta"]).then_inc(loaded, 16)
            sp.dma_start(pos[:], a["positions"].rearrange("(o s) -> o s", o=1).broadcast_to([P, S]))\
                .then_inc(loaded, 16)

        @block.gpsimd
        def _(pool):
            pool.memset(m.maskq[:], 0.0).then_inc(zeroed, 1)
            pool.memset(m.maskk[:], 0.0).then_inc(zeroed, 1)
            pool.wait_ge(zeroed, 2)
            pool.affine_select(out=m.maskq[:], in_=m.maskq[:], compare_op=ALU.is_ge, fill=NEG, base=0,
                               pattern=[[-1, P]], channel_multiplier=1).then_inc(masked, 1)
            pool.affine_select(out=m.maskk[:], in_=m.maskk[:], compare_op=ALU.is_ge, fill=NEG, base=0,
                               pattern=[[1, P]], channel_multiplier=-1).then_inc(masked, 1)

        @block.vector
        def _(dve):
            c = Chain(dve, order)
            dve.wait_ge(loaded, 32)
            ang, s_r, c_r = pos[:], r[:, 0, :], r[:, 1, :]
            c.after(dve.tensor_scalar(ang, pos[:], tin[:, 0:1], None, ALU.mult))
            c.after(dve.tensor_scalar(nrm[:], ang, 1.0 / TWO_PI, ROUND, ALU.mult, ALU.add))
            c.after(dve.tensor_scalar(nrm[:], nrm[:], ROUND, None, ALU.subtract))
            c.after(dve.scalar_tensor_tensor(s_r, nrm[:], -C1, ang, ALU.mult, ALU.add))
            c.after(dve.scalar_tensor_tensor(s_r, nrm[:], -C2, s_r, ALU.mult, ALU.add))
            c.after(dve.scalar_tensor_tensor(s_r, nrm[:], -C3, s_r, ALU.mult, ALU.add))
            c.after(dve.tensor_scalar(c_r, s_r, TWO_PI / 4, None, ALU.add))
            c.after(dve.tensor_scalar(t[:], c_r, TWO_PI / 2, -TWO_PI, ALU.is_gt, ALU.mult))
            c.after(dve.tensor_tensor(c_r, c_r, t[:], ALU.add))
            PI = 3.1415925
            dve.tensor_scalar(r[:], r[:], -PI, PI, ALU.max, ALU.min).then_inc(reduced, 1)

        @block.scalar
        def _(act):
            act.wait_ge(reduced, 1)
            act.activation(sin[:], r[:, 0, :], ACT.Sin).then_inc(done, 1)
            act.activation(cos[:], r[:, 1, :], ACT.Sin).then_inc(done, 1)
            act.wait_ge(done, 2)
            act.activation(sin[:], sin[:], ACT.Copy, scale=tin[:, 1:2]).then_inc(done, 1)


def stage_b(nc, a, m):
    norm_block(nc, m, "B0n", first=True, rms_row=R_G1, to_y=True, add_row=R_OB)
    with nc.sbuf_tensor("B_cos", [P, S], F32) as cos, nc.sbuf_tensor("B_sin", [P, S], F32) as sin, \
            nc.sbuf_tensor("maskq", [P, P], BF16) as m.maskq, nc.sbuf_tensor("maskk", [P, P], BF16) as m.maskk:
        rope_tables(nc, a, m, cos, sin)
        attention_block(nc, m, a["B_w"], "B1", rope=(cos, sin), causal=True, biases=a["B_bias"])
    norm_block(nc, m, "B2n", rms_row=R_G2)

    gT = m.ctx_gT = None
    with nc.sbuf_tensor("B_gT", [P, T * P], BF16) as gT, nc.sbuf_tensor("B_sel", [P, E_MOE, P], BF16) as sel, \
            nc.sbuf_tensor("B_gates", [P, T, E_MOE], F32) as gates, \
            nc.sbuf_tensor("B_gT32", [E_MOE, T * P], F32) as gT32:
        router_b(nc, a, m, gates, gT, gT32, sel)
        experts_b(nc, a, m, gT, gT32, sel)


def router_b(nc, a, m, gates, gT, gT32, sel):
    sem = lambda s: m.sem("B3_" + s)
    loaded, logits_done, l_ready, e_done, order, gates_ready, turned, gT_ready, sel_set, sel_made = \
        (sem(s) for s in ("loaded", "logits_done", "l_ready", "e_done", "order", "gates_ready", "turned",
                          "gT_ready", "sel_set", "sel_made"))
    W = TOPK_PAD
    with nc.sbuf_tensor("B3_rw", [P, E_R], F32) as rw, nc.sbuf_tensor("B3_rb", [P, E_R], F32) as rb, \
            nc.sbuf_tensor("B3_l", [P, T, E_R], F32) as lg, nc.sbuf_tensor("B3_nm", [P, T], F32) as nm, \
            nc.sbuf_tensor("B3_aff", [P, T, W], F32) as aff, nc.sbuf_tensor("B3_rest", [P, T, W], F32) as rest, \
            nc.sbuf_tensor("B3_top", [P, T, 8], F32) as top, nc.sbuf_tensor("B3_sum", [P, T], F32) as ssum, \
            nc.sbuf_tensor("B3_rem", [3 * E_MOE, T * P], F32) as rem, nc.Block() as block:
        @block.sync
        def _(sp):
            sp.dma_start(rw[:], a["B_rw"]).then_inc(loaded, 16)
            sp.dma_start(rb[:], a["B_rb"].rearrange("(o e) -> o e", o=1).broadcast_to([P, E_R]))\
                .then_inc(loaded, 16)

        @block.gpsimd
        def _(pool):
            pool.memset(sel[:], 0.0).then_inc(sel_set, 1)
            pool.wait_ge(sel_set, 1)
            for part in range(3):
                pool.affine_select(out=sel[0:96, :, :], in_=sel[0:96, :, :], compare_op=ALU.not_equal, fill=1.0,
                                   base=-32 * part, pattern=[[-1, E_MOE], [0, P]], channel_multiplier=1)\
                    .then_inc(sel_made, 1)
                pool.wait_ge(sel_made, part + 1)

        @block.tensor
        def _(pe):
            pe.wait_ge(loaded, 32)
            for t in range(T):
                last = pe.matmul(m.ps[:, 0, t * 32:t * 32 + E_R], lhsT=m.hT[:, t // TB, t % TB * P:(t % TB + 1) * P],
                                 rhs=rw[:], start=True, stop=True)
            last.then_inc(logits_done, 1)
            pe.wait_ge(gates_ready, 1)
            for t in range(T):
                last = pe.transpose(m.ps[0:E_MOE, 1 + t // TB, t % TB * P:(t % TB + 1) * P], gates[:, t, :],
                                    m.ident[:])
            last.then_inc(turned, 1)

        @block.scalar
        def _(act):
            act.wait_ge(l_ready, 1)
            act.activation(aff[:, :, 0:E_R], lg[:], ACT.Exp).then_inc(e_done, 1)

        @block.vector
        def _(dve):
            c = Chain(dve, order)
            wide = lambda x, n: x.rearrange("p (t o) -> p t o", o=1).broadcast_to([P, T, n])
            c.step(dve.memset(aff[:, :, E_R:W], -1.0))
            dve.wait_ge(loaded, 32)
            dve.wait_ge(logits_done, 1)
            l_ps = m.ps[:, 0, 0:T * 32].rearrange("p (t e) -> p t e", e=32)[:, :, 0:E_R]
            c.after(dve.tensor_tensor(lg[:], l_ps, rb[:].rearrange("p (o e) -> p o e", o=1)
                                      .broadcast_to([P, T, E_R]), ALU.add))
            c.after(dve.tensor_reduce(nm[:], lg[:], AX.X, ALU.max))
            dve.tensor_tensor(lg[:], lg[:], wide(nm[:], E_R), ALU.subtract).then_inc(l_ready, 1)
            dve.wait_ge(e_done, 1)
            c.after(dve.tensor_reduce(ssum[:], aff[:, :, 0:E_R], AX.X, ALU.add))
            c.after(dve.reciprocal(ssum[:], ssum[:]))
            c.after(dve.tensor_tensor(aff[:, :, 0:E_R], aff[:, :, 0:E_R], wide(ssum[:], E_R), ALU.mult))
            for t in range(T):
                c.step(dve.max(top[:, t, :], aff[:, t, :]))
            c.after(dve.memset(gates[:], 1.0))
            c.after(dve.memset(top[:, :, 3:8], -1.0))
            for t in range(T):
                c.after(dve.match_replace(rest[:, t, :], top[:, t, :], aff[:, t, :], 0.0))
            dve.tensor_tensor(gates[:, :, 0:E_R], aff[:, :, 0:E_R], rest[:, :, 0:E_R], ALU.subtract)\
                .then_inc(gates_ready, 1)
            dve.wait_ge(turned, 1)
            g_ps = m.ps[0:E_MOE, 1:3, :].rearrange("p b s -> p (b s)")
            c.after(dve.tensor_copy(gT32[:], g_ps))
            c.after(dve.tensor_copy(gT[0:32, :], gT32[:]))
            c.after(dve.tensor_tensor(rem[0:32, :], gT32[:], gT[0:32, :], ALU.subtract))
            c.after(dve.tensor_copy(gT[32:64, :], rem[0:32, :]))
            c.after(dve.tensor_copy(rem[32:64, :], rem[0:32, :]))
            dve.tensor_tensor(gT[64:96, :], rem[32:64, :], gT[32:64, :], ALU.subtract).then_inc(gT_ready, 1)


def experts_b(nc, a, m, gT, gT32, sel):
    sem = lambda s: m.sem("B4_" + s)
    w_loaded, b_loaded, up_done, gb_done, gelu_done, h_ready, down_done = \
        (sem(s) for s in ("w_loaded0", "b_loaded", "up_done", "gb_done", "gelu_done", "h_ready", "down_done"))
    acc_ready, acc_turned, order, closed = sem("acc_ready"), sem("acc_turned"), sem("order"), sem("closed")
    UN = 2
    w_loaded = [w_loaded, sem("w_loaded1")]
    EW = 2 * P + 1
    with nc.sbuf_tensor("B4_w", [P, UN, EW], F32) as w, nc.sbuf_tensor("B4_b2", [E_MOE, P], F32) as b2, \
            nc.sbuf_tensor("B4_g", [P, B, S], F32) as g, nc.sbuf_tensor("B4_h", [P, B, S], F32) as h, \
            nc.sbuf_tensor("B4_acc", [P, B, S], F32) as acc, nc.Block() as block:
        @block.sync
        def _(sp):
            sp.dma_start(b2[:], a["B_b2"]).then_inc(b_loaded, 16)
            for k in range(UN):
                sp.dma_start(w[:, k, :], a["B_ew"][k]).then_inc(w_loaded[k], 16)
            with sp.Fori(1, E_MOE // UN) as i:
                for k in range(UN):
                    sp.wait_ge(down_done, i * UN * B)
                    sp.dma_start(w[:, k, :], a["B_ew"][i * UN + k]).then_inc(w_loaded[k], 16)

        @block.tensor
        def _(pe):
            pe.wait_ge(b_loaded, 16)
            for b in range(B):
                pe.matmul(m.ps[:, 4 + b, :], lhsT=b2[:], rhs=gT32[:, b * S:(b + 1) * S], start=True, stop=False)
            with pe.Fori(0, E_MOE // UN) as i:
                for k in range(UN):
                    e = i * UN + k
                    pe.wait_ge(w_loaded[k], 16 * (i + 1))
                    for b in range(B):
                        pe.matmul(m.ps[:, b, :], lhsT=w[:, k, 0:P], rhs=m.hT[:, b, :], start=True, stop=True)\
                            .then_inc(up_done, 1)
                    for b in range(B):
                        pe.matmul(m.ps[:, 2 + b, :], lhsT=sel[0:96, e, :], rhs=gT[0:96, b * S:(b + 1) * S],
                                  start=True, stop=True).then_inc(gb_done, 1)
                    for b in range(B):
                        pe.wait_ge(h_ready, e * B + b + 1)
                        pe.matmul(m.ps[:, 4 + b, :], lhsT=w[:, k, P:2 * P], rhs=h[:, b, :], start=False,
                                  stop=False).then_inc(down_done, 1)
            close_sums(pe, m, (4, 5), closed)
            pe.wait_ge(acc_ready, 2)
            for b in range(B):
                for t in range(TB):
                    last = pe.transpose(m.ps[:, 6 + b, t * P:(t + 1) * P], acc[:, b, t * P:(t + 1) * P], m.ident[:])
                last.then_inc(acc_turned, 1)

        @block.scalar
        def _(act):
            with act.Fori(0, E_MOE // UN) as i:
                for k in range(UN):
                    e = i * UN + k
                    for b in range(B):
                        act.wait_ge(up_done, e * B + b + 1)
                        act.activation(g[:, b, :], m.ps[:, b, :], ACT.Gelu, bias=w[:, k, 2 * P:2 * P + 1])\
                            .then_inc(gelu_done, 1)

        @block.vector
        def _(dve):
            with dve.Fori(0, E_MOE // UN) as i:
                for k in range(UN):
                    e = i * UN + k
                    for b in range(B):
                        dve.wait_ge(gelu_done, e * B + b + 1)
                        dve.wait_ge(gb_done, e * B + b + 1)
                        dve.tensor_tensor(h[:, b, :], g[:, b, :], m.ps[:, 2 + b, :], ALU.mult).then_inc(h_ready, 1)
            dve.wait_ge(closed, 1)
            for b in range(B):
                dve.tensor_copy(acc[:, b, :], m.ps[:, 4 + b, :]).then_inc(acc_ready, 1)
            c = Chain(dve, order)
            c.after(dve.tensor_tensor(m.y[:], m.y[:], m.xn[:], ALU.add))
            for b in range(B):
                tiles = slice(b * TB, (b + 1) * TB)
                dve.wait_ge(acc_turned, b + 1)
                c.after(dve.tensor_tensor(m.y[:, tiles, :], m.y[:, tiles, :],
                                          m.ps[:, 6 + b, :].rearrange("p (t d) -> p t d", t=TB), ALU.add))
                c.after(dve.tensor_tensor(m.x[:, tiles, :], m.x[:, tiles, :], m.y[:, tiles, :], ALU.add))


def stage_c(nc, a, m):
    first_norm = m.sem("C0_order")
    with nc.Block() as block:
        @block.vector
        def _(dve):
            c = Chain(dve, first_norm)
            norm_steps(c, dve, m, lambda t: m.x[:, t, :], lambda t: m.y[:, t, :], T)

    with ExitStack() as held:
        def sb(name, shape, dt=F32):
            return held.enter_context(nc.sbuf_tensor("C_" + name, shape, dt))

        (zeroed, ones_set, const_loaded, valid_ready, wqkv_loaded, wcross_loaded, wff_loaded,
         gelu_done, f1_done, f2_done, order, ctx_copied, ff_added, pe_passed, dve_passed, rows_ready,
         rows_stacked, vq_ready, pool_passed) = \
            (m.sem("C_" + n) for n in
             ("zeroed", "ones_set", "const_loaded", "valid_ready", "wqkv_loaded", "wcross_loaded",
             "wff_loaded", "gelu_done", "f1_done", "f2_done", "order", "ctx_copied", "ff_added",
             "pe_passed", "dve_passed", "rows_ready", "rows_stacked", "vq_ready", "pool_passed"))
        (xn_ready, turned, hT_ready) = \
            ([m.sem(f"C_{n}{i}") for i in range(3)] for n in
             ("xn_ready", "turned", "hT_ready"))
        (proj_done, v_done, v_ready, roped, q_sum, k_sum, q_p12, k_p12, q_rem, k_rem, q_p3, k_p3,
         q_stacked, k_stacked, s_done, max_done, nm_ready, nm_turned, nmT_ready, max_stacked, st_done,
         exp_done, pv_done, pv_copied, cw_turned, cn_ready, c_turned, cT_ready, out_done) = \
            ([m.sem(f"C_{n}{i}") for i in range(2)] for n in
             ("proj_done", "v_done", "v_ready", "roped", "q_sum", "k_sum", "q_p12", "k_p12", "q_rem",
             "k_rem", "q_p3", "k_p3", "q_stacked", "k_stacked", "s_done", "max_done", "nm_ready",
             "nm_turned", "nmT_ready", "max_stacked", "st_done", "exp_done", "pv_done", "pv_copied",
             "cw_turned", "cn_ready", "c_turned", "cT_ready", "out_done"))

        w = sb("w", [P, LW])
        qs = sb("qs", [P, B, H, S], BF16)
        ks = sb("ks", [P, B, H, S], BF16)
        kc = sb("kc", [P, B, H, CTX], BF16)
        cos, sin = sb("cos", [P, S]), sb("sin", [P, S])
        rot = sb("rot", [P, 2, 2, S])
        full = sb("full", [P, 2, S])
        rem = sb("rem", [P, 2, S])
        parts = sb("parts", [P, 2, 3, S], BF16)
        va = sb("va", [P, B, TB, H, HD + 1])
        vq = sb("vq", [P, TB, QUAD, VW])
        vc = sb("vc", [P, H, VW])
        valid = sb("valid", [P, B, TB])
        validc = sb("validc", [CTX, B])
        mk, mkc = sb("mk", [P, B, TB], U8), sb("mkc", [CTX, B], U8)
        mrow, mrowc = sb("mrow", [MASK_ROW + 1, B, S], U8), sb("mrowc", [MASK_ROW + 1, B, CTX], U8)
        qrow = sb("qrow", [96, S], BF16)
        krow, kcrow = sb("krow", [96, B, S], BF16), sb("kcrow", [96, B, CTX], BF16)
        no_max = sb("no_max", [2 * H, S], BF16)
        nm = sb("nm", [P, H, TB])
        nmp = sb("nmp", [P, TB, 2, H], BF16)
        nmT = sb("nmT", [2 * H, S], BF16)
        prob = sb("prob", [P, 2, QUAD, S])
        cw = sb("cw", [P, QUADS, S])
        rden = sb("rden", [P, QUADS, TB * QUAD])
        cn, cT = sb("cn", [P, TB, P]), sb("cT", [P, S])
        hT = sb("hT", [P, S])
        ctxb = sb("ctxb", [P, CTX])
        u = sb("u", [P, 4, S])
        ps = m.ps
        SCALE = 1.0 / float(np.sqrt(np.float32(HD)))
        UNITS = LAYERS * B
        HP = H // 2
        NK, KT = (S, CTX), (TB, 1)
        QCOL, KCOL, VCOL, OCOL = (LQ, LCQ), (LK, LCK), (LV, LCV), (LSO, LCO)
        CREDIT = 2
        ZEROED = 6
        PV_CREDIT = 4

        with nc.Block() as block:
            @block.sync
            def _(sp):
                sp.dma_start(cos[:], a["C_cos"]).then_inc(const_loaded, 16)
                sp.dma_start(sin[:], a["C_sin"]).then_inc(const_loaded, 16)
                sp.dma_start(mk[:], a["mask_cols"]).then_inc(const_loaded, 16)
                sp.dma_start(mkc[:], a["maskc_cols"]).then_inc(const_loaded, 16)
                sp.dma_start(mrow[MASK_ROW:MASK_ROW + 1], a["mask_rows"].rearrange("(o b) s -> o b s", o=1))\
                    .then_inc(const_loaded, 16)
                sp.dma_start(mrowc[MASK_ROW:MASK_ROW + 1], a["maskc_rows"].rearrange("(o b) s -> o b s", o=1))\
                    .then_inc(const_loaded, 16)

                def load(part, l):
                    c0, c1 = LOADS[part]
                    sem = (wqkv_loaded, wcross_loaded, wff_loaded)[part]
                    sp.dma_start(w[:, c0:c1], a["C_w"][l][:, c0:c1]).then_inc(sem, 16)

                def stack(n, b, k):
                    kdst = (ks, kc)[k]
                    for i, (p12, p3, stacked) in enumerate(((q_p12[k], q_p3[k], q_stacked[k]),
                                                            (k_p12[k], k_p3[k], k_stacked[k]))):
                        width = NK[k] if i else S
                        for part in range(3):
                            if part < 2:
                                sp.wait_ge(p12, n * 2 + part + 1)
                            else:
                                sp.wait_ge(p3, n + 1)
                            for r, combo in enumerate(COMBOS):
                                if combo[i] == part:
                                    dst = (qs, kdst)[i][r * HD:(r + 1) * HD, b, :, 0:width]
                                    sp.dma_start(dst, parts[:, i, part, 0:width]).then_inc(stacked, 16)
                            if k == 0 and i == 0 and part == 0:
                                sp.dma_start(qs[MAX_ROW:MAX_ROW + 2, b, :, :], no_max[:]).then_inc(stacked, 16)

                def stack_max(n, b, k):
                    sp.wait_ge(nmT_ready[k], n + 1)
                    sp.dma_start(qs[MAX_ROW:MAX_ROW + 2, b, :, :], nmT[:]).then_inc(max_stacked[k], 16)

                def unit(n, l, b, last=False, reload=True):
                    if not last:
                        stack(n + 1, 1 - b, 0)
                        if b == 0 and reload:
                            sp.wait_ge(v_done[0], n + 2)
                            load(0, l + 1)
                        stack_max(n + 1, 1 - b, 0)
                    stack(n, b, 1)
                    stack_max(n, b, 1)
                    if b == 1 and reload:
                        sp.wait_ge(out_done[1], n + 1)
                        load(1, l + 1)
                        sp.wait_ge(f2_done, n + 1)
                        load(2, l + 1)

                for part in range(3):
                    load(part, 0)
                sp.wait_ge(zeroed, ZEROED)
                sp.wait_ge(rows_ready, 1)
                rows = slice(MASK_ROW, 96)
                every = lambda x, width: x.rearrange("p (h s) -> p h s", h=1).broadcast_to([32, H, width])
                for b in range(B):
                    sp.dma_start(qs[rows, b, :, :], every(qrow[rows, :], S)).then_inc(rows_stacked, 16)
                    sp.dma_start(ks[rows, b, :, :], every(krow[rows, b, :], S)).then_inc(rows_stacked, 16)
                    sp.dma_start(kc[rows, b, :, :], every(kcrow[rows, b, :], CTX)).then_inc(rows_stacked, 16)
                sp.wait_ge(rows_stacked, 96)
                stack(0, 0, 0)
                stack_max(0, 0, 0)
                with sp.Fori(0, LAYERS - 1) as l:
                    unit(l * B, l, 0)
                    unit(l * B + 1, l, 1)
                unit(UNITS - 2, LAYERS - 1, 0, reload=False)
                unit(UNITS - 1, LAYERS - 1, 1, last=True, reload=False)

            @block.gpsimd
            def _(pool):
                for one in (qrow, krow, kcrow):
                    pool.memset(one[MASK_ROW:96], 0.0).then_inc(ones_set, 1)
                pool.wait_ge(ones_set, 3)
                for one, count in ((qrow, 1), (krow, 3), (kcrow, 3)):
                    pool.memset(one[MASK_ROW:MASK_ROW + count], 1.0).then_inc(ones_set, 1)
                pool.wait_ge(ones_set, 6)
                for one in (no_max, ks, kc, vq, vc):
                    pool.memset(one[:], 0.0).then_inc(zeroed, 1)

                def keys(n, k):
                    f, r, p = full[:, 1, 0:NK[k]], rem[:, 1, 0:NK[k]], parts[:, 1, :, 0:NK[k]]
                    pool.wait_ge(roped[k], n * 4 + 4)
                    pool.tensor_tensor(f, rot[:, 1, 0, 0:NK[k]], rot[:, 1, 1, 0:NK[k]], ALU.add)\
                        .then_inc(k_sum[k], 1)
                    pool.wait_ge(k_p12[k], n * 2 + 1)
                    pool.tensor_tensor(r, f, p[:, 0, :], ALU.subtract).then_inc(k_rem[k], 1)
                    pool.wait_ge(k_p12[k], n * 2 + 2)
                    pool.tensor_tensor(p[:, 2, :], r, p[:, 1, :], ALU.subtract).then_inc(k_p3[k], 1)

                def quad_values(n, b, q):
                    for kt in range(TB):
                        pool.wait_ge(pv_done[0], (n * QUADS + q) * TB + kt - TB + 1 + PV_CREDIT)
                        pool.tensor_copy(vq[:, kt, :, 0:HD + 1], va[:, b, kt, bass.ds(q * QUAD, QUAD), :])\
                            .then_inc(vq_ready, 1)

                def unit(n, last=False):
                    b = n % B
                    if not last:
                        keys(n + 1, 0)
                    pool.wait_ge(v_ready[0], n + 1)
                    pool.sem_inc(pool_passed, 1)
                    with pool.Fori(0, QUADS) as q:
                        quad_values(n, b, q)
                    if last:
                        pool.wait_ge(v_done[1], UNITS - 1)
                    pool.tensor_copy(ctxb[:], m.ctxT[:, b, :]).then_inc(ctx_copied, 1)
                    keys(n, 1)

                keys(0, 0)
                with pool.Fori(0, UNITS - 1) as n:
                    unit(n)
                unit(UNITS - 1, last=True)

            @block.tensor
            def _(pe):
                def turn_norm(n, i):
                    pe.wait_ge(xn_ready[i], n + 1)
                    for t in range(TB):
                        last = pe.transpose(ps[:, 7, t * P:(t + 1) * P], m.xn[:, t, :], m.ident[:])
                    last.then_inc(turned[i], 1)

                def project(n, k):
                    if k == 0:
                        pe.wait_ge(wqkv_loaded, (n // B + 1) * 16)
                    else:
                        pe.wait_ge(wcross_loaded, (n // B + 1) * 16)
                        pe.wait_ge(ctx_copied, n + 1)
                    pe.wait_ge(hT_ready[k], n + 1)
                    for i, col in enumerate((QCOL[k], KCOL[k])):
                        source = ctxb[:] if k and i else hT[:]
                        for r in range(2):
                            last = pe.matmul(ps[:, 2 * i + r, 0:source.shape[1]],
                                             lhsT=w[:, col + r * P:col + (r + 1) * P], rhs=source,
                                             start=True, stop=True)
                        last.then_inc(proj_done[k], 1)
                    if k:
                        pe.matmul(ps[0:CTX, 4, 0:P], lhsT=ctxb[:], rhs=w[:, LCV:LCV + P], start=True, stop=True)\
                            .then_inc(v_done[1], 1)
                    else:
                        for t in range(TB):
                            last = pe.matmul(ps[:, 4, t * P:(t + 1) * P], lhsT=hT[:, t * P:(t + 1) * P],
                                             rhs=w[:, LV:LV + P], start=True, stop=True)
                        last.then_inc(v_done[0], 1)

                def stacks_there(n, k):
                    pe.wait_ge(q_stacked[k], (n + 1) * 16 * (len(COMBOS) + 1 - k))
                    pe.wait_ge(k_stacked[k], (n + 1) * 16 * len(COMBOS))
                    pe.wait_ge(roped[k], n * 4 + 4)
                    pe.wait_ge(v_ready[k], n + 1)
                    pe.sem_inc(pe_passed, 1)

                def scores(n, b, h, g):
                    pe.wait_ge(max_done[0], (n * H + h) * 2 + g - 1 + CREDIT)
                    for t in (2 * g, 2 * g + 1):
                        last = pe.matmul(ps[:, t, :], lhsT=qs[:, b, h, t * P:(t + 1) * P], rhs=ks[:, b, h, :],
                                         start=True, stop=True)
                    last.then_inc(s_done[0], 1)

                def scores_T(n, b, q, kt, j):
                    i = kt * QUAD + j
                    pe.wait_ge(exp_done[0], (n * QUADS + q) * TB * QUAD + i - 1 + CREDIT)
                    pe.matmul(ps[:, 4 + j % 2, :], lhsT=ks[:, b, q * QUAD + j, kt * P:(kt + 1) * P],
                              rhs=qs[:, b, q * QUAD + j, :], start=True, stop=True).then_inc(st_done[0], 1)

                def weigh(n, q, kt):
                    slot = (n * QUADS + q) * TB + kt
                    pe.wait_ge(exp_done[0], (slot + 1) * QUAD + CREDIT)
                    pe.wait_ge(vq_ready, slot + 1)
                    if kt == 0:
                        pe.wait_ge(pv_copied[0], n * QUADS + q + CREDIT)
                    for j in range(QUAD):
                        last = pe.matmul(ps[j * VW:(j + 1) * VW, 6, :], lhsT=vq[:, kt, j, :],
                                         rhs=prob[:, kt % 2, j, :], start=kt == 0, stop=kt == TB - 1)
                    last.then_inc(pv_done[0], 1)

                def quad(n, b, nb, nxt, q, first=False):
                    for kt in range(TB):
                        scores_T(n, b, q, kt, 0)
                        if nxt:
                            scores(n + 1, nb, q * QUAD + kt, 0)
                        scores_T(n, b, q, kt, 1)
                        if kt:
                            weigh(n, q, kt - 1)
                        elif not first:
                            weigh(n, q - 1, TB - 1)
                        scores_T(n, b, q, kt, 2)
                        if nxt:
                            scores(n + 1, nb, q * QUAD + kt, 1)
                        scores_T(n, b, q, kt, 3)

                def self_attention(n, b, nxt):
                    pe.wait_ge(max_stacked[0], (n + 1) * 16)
                    nb = (n + 1) % B
                    pe.sem_inc(pe_passed, 1)
                    quad(n, b, nb, nxt, 0, first=True)
                    pe.sem_inc(pe_passed, 1)
                    with pe.Fori(1, QUADS) as q:
                        quad(n, b, nb, nxt, q)
                    weigh(n, QUADS - 1, TB - 1)

                def turn_max(n, k):
                    pe.wait_ge(nm_ready[k], n + 1)
                    out = ps[0:2 * H, 5, :].bitcast(BF16)
                    for t in range(TB):
                        last = pe.transpose(out[:, t * P:(t + 1) * P], nmp[:, t, :, :], m.identb[:])
                    last.then_inc(nm_turned[k], 1)

                def cross_max(n, b, hp):
                    for j in range(2):
                        h = 2 * hp + j
                        pe.wait_ge(max_done[1], n * H + h - 1 + CREDIT)
                        for t in range(TB):
                            last = pe.matmul(ps[:, j, t * CTX:(t + 1) * CTX], lhsT=qs[0:MAX_ROW, b, h, t * P:(t + 1) * P],
                                             rhs=kc[0:MAX_ROW, b, h, :], start=True, stop=True)
                        last.then_inc(s_done[1], 1)

                def cross_T(n, b, i):
                    pe.wait_ge(exp_done[1], n * HP + i - 1 + CREDIT)
                    for j in range(2):
                        last = pe.matmul(ps[0:CTX, 2 * (i % 2) + j, :], lhsT=kc[:, b, 2 * i + j, :],
                                         rhs=qs[:, b, 2 * i + j, :], start=True, stop=True)
                    last.then_inc(st_done[1], 1)

                def cross_weigh(n, q):
                    pe.wait_ge(exp_done[1], n * HP + 2 * q + 2 + CREDIT)
                    pe.wait_ge(pv_copied[1], n * QUADS + q - 1 + CREDIT)
                    for j in range(QUAD):
                        last = pe.matmul(ps[j * VW:(j + 1) * VW, 6 + q % 2, :], lhsT=vc[:, q * QUAD + j, :],
                                         rhs=prob[:, q % 2, j, :], start=True, stop=True)
                    last.then_inc(pv_done[1], 1)

                def output(n, k):
                    for q in range(QUADS):
                        pe.wait_ge(pv_copied[k], n * QUADS + q + 1 + CREDIT)
                        for t in range(TB):
                            last = pe.transpose(ps[:, q, t * P:(t + 1) * P], cw[:, q, t * P:(t + 1) * P],
                                                m.ident[:])
                        last.then_inc(cw_turned[k], 1)
                    pe.wait_ge(cn_ready[k], (n + 1) * QUADS)
                    for t in range(TB):
                        last = pe.transpose(ps[:, 4, t * P:(t + 1) * P], cn[:, t, :], m.ident[:])
                    last.then_inc(c_turned[k], 1)
                    if k == 0:
                        pe.wait_ge(wcross_loaded, (n // B + 1) * 16)
                    pe.wait_ge(cT_ready[k], n + 1)
                    for t in range(TB):
                        last = pe.matmul(ps[:, 5, t * P:(t + 1) * P], lhsT=cT[:, t * P:(t + 1) * P],
                                         rhs=w[:, OCOL[k]:OCOL[k] + P], start=True, stop=True)
                    last.then_inc(out_done[k], 1)

                def rest(n, b):
                    output(n, 0)
                    turn_norm(n, 1)
                    project(n, 1)
                    stacks_there(n, 1)
                    with pe.Fori(0, HP) as hp:
                        cross_max(n, b, hp)
                    turn_max(n, 1)
                    pe.wait_ge(max_stacked[1], (n + 1) * 16)
                    for i in range(HP):
                        cross_T(n, b, i)
                        if i >= 2 and i % 2 == 0:
                            cross_weigh(n, i // 2 - 1)
                    cross_weigh(n, QUADS - 1)
                    output(n, 1)
                    turn_norm(n, 2)
                    pe.wait_ge(wff_loaded, (n // B + 1) * 16)
                    pe.wait_ge(hT_ready[2], n + 1)
                    for i in range(4):
                        pe.matmul(ps[:, i, :], lhsT=w[:, LF1 + i * P:LF1 + (i + 1) * P], rhs=hT[:],
                                  start=True, stop=True).then_inc(f1_done, 1)
                    for t in range(TB):
                        for i in range(4):
                            if t == 0:
                                pe.wait_ge(gelu_done, n * 4 + i + 1)
                            last = pe.matmul(ps[:, 4, t * P:(t + 1) * P], lhsT=u[:, i, t * P:(t + 1) * P],
                                             rhs=w[:, LF2 + i * P:LF2 + (i + 1) * P], start=i == 0, stop=i == 3)
                    last.then_inc(f2_done, 1)

                def begin(n):
                    turn_norm(n, 0)
                    project(n, 0)

                pe.wait_ge(zeroed, ZEROED)
                pe.wait_ge(rows_stacked, 96)
                pe.wait_ge(valid_ready, 4)
                begin(0)
                stacks_there(0, 0)
                with pe.Fori(0, HP) as hp:
                    for j in range(2):
                        scores(0, 0, 2 * hp + j, 0)
                        scores(0, 0, 2 * hp + j, 1)
                turn_max(0, 0)
                with pe.Fori(0, UNITS - 1) as n:
                    b = n % B
                    begin(n + 1)
                    stacks_there(n + 1, 0)
                    self_attention(n, b, True)
                    turn_max(n + 1, 0)
                    rest(n, b)
                pe.wait_ge(ff_added, UNITS - 1)
                self_attention(UNITS - 1, 1, False)
                rest(UNITS - 1, 1)

            @block.scalar
            def _(act):
                def copy_norm(n, i):
                    k = 3 + (n // B) * 3 + i
                    b = n % B
                    act.wait_ge(turned[i], n + 1)
                    act.activation(hT[:], ps[:, 7, :], ACT.Identity, bias=m.aff[:, k, 1, bass.ds(b, 1)],
                                   scale=m.aff[:, k, 0, bass.ds(b, 1)]).then_inc(hT_ready[i], 1)

                def split(n, k):
                    for i, (whole, p12) in enumerate(((q_sum[k], q_p12[k]), (k_sum[k], k_p12[k]))):
                        act.wait_ge(whole, n + 1)
                        width = NK[k] if i else S
                        act.activation(parts[:, i, 0, 0:width], full[:, i, 0:width], ACT.Copy).then_inc(p12, 1)
                    for i, (left, p12) in enumerate(((q_rem[k], q_p12[k]), (k_rem[k], k_p12[k]))):
                        act.wait_ge(left, n + 1)
                        width = NK[k] if i else S
                        act.activation(parts[:, i, 1, 0:width], rem[:, i, 0:width], ACT.Copy).then_inc(p12, 1)

                def values(n, b, k):
                    act.wait_ge(v_done[k], n + 1)
                    if k:
                        last = act.activation(vc[0:CTX, :, 0:HD], ps[0:CTX, 4, 0:P].rearrange("p (h d) -> p h d", d=HD),
                                              ACT.Copy, scale=validc[:, bass.ds(b, 1)])
                    else:
                        for t in range(TB):
                            last = act.activation(va[:, b, t, :, 0:HD],
                                                  ps[:, 4, t * P:(t + 1) * P].rearrange("p (h d) -> p h d", d=HD),
                                                  ACT.Copy, scale=valid[:, b, t:t + 1])
                    if k:
                        last = act.activation(vc[0:CTX, :, HD:HD + 1], validc[:, bass.ds(b, 1)]
                                              .rearrange("p (h o) -> p h o", o=1).broadcast_to([CTX, H, 1]), ACT.Copy)
                    last.then_inc(v_ready[k], 1)

                def copy_max(n, k, last=False):
                    act.wait_ge(nm_turned[k], n + 1)
                    if k == 1:
                        act.wait_ge(max_stacked[0], UNITS * 16 if last else (n + 2) * 16)
                    act.activation(nmT[:], ps[0:2 * H, 5, :].bitcast(BF16)[:, 0:S], ACT.Copy)\
                        .then_inc(nmT_ready[k], 1)

                def exps(n, q):
                    for kt in range(TB):
                        slot = (n * QUADS + q) * TB + kt
                        act.wait_ge(pv_done[0], slot - 1 + PV_CREDIT)
                        for j in range(QUAD):
                            act.wait_ge(st_done[0], slot * QUAD + j + 1)
                            act.activation(prob[:, kt % 2, j, :], ps[:, 4 + j % 2, :], ACT.Exp, scale=SCALE)\
                                .then_inc(exp_done[0], 1)

                def copy_context(n, k):
                    act.wait_ge(c_turned[k], n + 1)
                    act.activation(cT[:], ps[:, 4, :], ACT.Copy).then_inc(cT_ready[k], 1)

                def begin(n):
                    copy_norm(n, 0)
                    values(n, n % B, 0)
                    split(n, 0)

                def rest(n, last=False):
                    copy_context(n, 0)
                    copy_norm(n, 1)
                    values(n, n % B, 1)
                    split(n, 1)
                    copy_max(n, 1, last)
                    for i in range(HP):
                        q, pair = i // 2, i % 2
                        if pair == 0:
                            act.wait_ge(pv_done[1], n * QUADS + q - 1 + CREDIT)
                        act.wait_ge(st_done[1], n * HP + i + 1)
                        act.activation(prob[0:CTX, q % 2, 2 * pair:2 * pair + 2, :],
                                       ps[0:CTX, 2 * pair:2 * pair + 2, :], ACT.Exp, scale=SCALE)\
                            .then_inc(exp_done[1], 1)
                    copy_context(n, 1)
                    copy_norm(n, 2)
                    for i in range(4):
                        act.wait_ge(f1_done, n * 4 + i + 1)
                        act.activation(u[:, i, :], ps[:, i, :], ACT.Gelu, bias=w[:, LB1 + i:LB1 + i + 1])\
                            .then_inc(gelu_done, 1)

                def self_exps(n):
                    with act.Fori(0, QUADS) as q:
                        exps(n, q)

                for k in range(2):
                    act.sem_inc(exp_done[k], CREDIT)
                act.wait_ge(valid_ready, 4)
                begin(0)
                copy_max(0, 0)
                with act.Fori(0, UNITS - 1) as n:
                    begin(n + 1)
                    self_exps(n)
                    copy_max(n + 1, 0)
                    rest(n)
                self_exps(UNITS - 1)
                rest(UNITS - 1, last=True)

            @block.vector
            def _(dve):
                c = Chain(dve, order)

                def norm(n, i):
                    b = n % B
                    norm_steps(c, dve, m, lambda t: m.y[:, b * TB + t, :], lambda t: m.xn[:, t, :], TB,
                               apart=dve_passed)
                    dve.sem_inc(xn_ready[i], 1)

                def rotate(n, k):
                    for i in range(2):
                        width = NK[k] if i else S
                        dve.wait_ge(proj_done[k], n * 2 + i + 1)
                        for r, table in enumerate((cos, sin)):
                            dve.tensor_tensor(rot[:, i, r, 0:width], ps[:, 2 * i + r, 0:width], table[:, 0:width],
                                              ALU.mult).then_inc(roped[k], 1)
                    dve.wait_ge(roped[k], n * 4 + 2)
                    dve.tensor_tensor(full[:, 0, :], rot[:, 0, 0, :], rot[:, 0, 1, :], ALU.add)\
                        .then_inc(q_sum[k], 1)
                    dve.wait_ge(q_p12[k], n * 2 + 1)
                    dve.tensor_tensor(rem[:, 0, :], full[:, 0, :], parts[:, 0, 0, :], ALU.subtract)\
                        .then_inc(q_rem[k], 1)
                    dve.wait_ge(q_p12[k], n * 2 + 2)
                    dve.tensor_tensor(parts[:, 0, 2, :], rem[:, 0, :], parts[:, 0, 1, :], ALU.subtract)\
                        .then_inc(q_p3[k], 1)

                def row_max(n, h, g):
                    dve.wait_ge(s_done[0], (n * H + h) * 2 + g + 1)
                    dve.tensor_reduce(nm[:, h, 2 * g:2 * g + 2], ps[:, 2 * g:2 * g + 2, :],
                                      AX.X, ALU.max, negate=True).then_inc(max_done[0], 1)

                def copy_sums(n, q, k):
                    if k == 0:
                        dve.wait_ge(pv_done[0], (n * QUADS + q + 1) * TB + PV_CREDIT)
                    else:
                        dve.wait_ge(pv_done[1], n * QUADS + q + 1 + CREDIT)
                    dve.tensor_copy(cw[:, q, :], ps[:, 6 + (q % 2 if k else 0), :]).then_inc(pv_copied[k], 1)

                def split_max(n, k):
                    dve.wait_ge(max_done[k], (n + 1) * H * (2 if k == 0 else 1) + CREDIT)
                    by_tile = nm[:].rearrange("p h t -> p t h")
                    c.after(dve.tensor_copy(nmp[:, :, 0, :], by_tile))
                    dve.tensor_tensor(nmp[:, :, 1, :], by_tile, nmp[:, :, 0, :], ALU.subtract)\
                        .then_inc(nm_ready[k], 1)

                def normalise(n, k):
                    by_head = lambda q: ps[:, q, :].rearrange("p (t j d) -> p t j d", t=TB, j=QUAD)
                    dve.wait_ge(cw_turned[k], (n + 1) * QUADS)
                    c.after(dve.reciprocal(rden[:], ps[:, 0:QUADS, :].rearrange("p q (i d) -> p q i d", d=VW)
                                           [:, :, :, HD]))
                    for q in range(QUADS):
                        dve.tensor_tensor(cn[:, :, q * QUAD * HD:(q + 1) * QUAD * HD]
                                          .rearrange("p t (j d) -> p t j d", d=HD), by_head(q)[:, :, :, 0:HD],
                                          rden[:, q, :].rearrange("p (t j o) -> p t j o", t=TB, o=1)
                                          .broadcast_to([P, TB, QUAD, HD]), ALU.mult).then_inc(cn_ready[k], 1)

                def add_bank(bank, b):
                    for t in range(TB):
                        y = m.y[:, b * TB + t, :]
                        c.after(dve.tensor_tensor(y, y, ps[:, bank, t * P:(t + 1) * P], ALU.add))

                def quad(n, nxt, q, first=False):
                    for kt in range(TB):
                        if nxt:
                            row_max(n + 1, q * QUAD + kt, 0)
                        if kt == 0 and not first:
                            copy_sums(n, q - 1, 0)
                        if nxt:
                            row_max(n + 1, q * QUAD + kt, 1)

                def self_attention(n, nxt):
                    quad(n, nxt, 0, first=True)
                    with dve.Fori(1, QUADS) as q:
                        quad(n, nxt, q)
                    if nxt:
                        split_max(n + 1, 0)
                    copy_sums(n, QUADS - 1, 0)

                def rest(n):
                    b = n % B
                    normalise(n, 0)
                    dve.wait_ge(out_done[0], n + 1)
                    add_bank(5, b)
                    norm(n, 1)
                    rotate(n, 1)
                    with dve.Fori(0, HP) as hp:
                        for j in range(2):
                            h = 2 * hp + j
                            dve.wait_ge(s_done[1], n * H + h + 1)
                            dve.tensor_reduce(nm[:, h, :], ps[:, j, 0:TB * CTX]
                                              .rearrange("p (t k) -> p t k", k=CTX), AX.X, ALU.max, negate=True)\
                                .then_inc(max_done[1], 1)
                    split_max(n, 1)
                    for q in range(QUADS):
                        copy_sums(n, q, 1)
                    normalise(n, 1)
                    dve.wait_ge(out_done[1], n + 1)
                    add_bank(5, b)
                    norm(n, 2)
                    for t in range(TB):
                        y = m.y[:, b * TB + t, :]
                        c.after(dve.tensor_tensor(y, y, m.rows[:, R_F2B + n // B, :], ALU.add))
                    dve.wait_ge(f2_done, n + 1)
                    add_bank(4, b)
                    dve.sem_inc(ff_added, 1)

                dve.memset(qs[:], 0.0).then_inc(zeroed, 1)
                dve.wait_ge(ones_set, 6)
                dve.wait_ge(const_loaded, 96)
                row = slice(MASK_ROW, MASK_ROW + 1)
                c.step(dve.tensor_scalar(krow[row], mrow[row], NEG, None, ALU.mult))
                c.after(dve.tensor_scalar(kcrow[row], mrowc[row], NEG, None, ALU.mult))
                dve.sem_inc(rows_ready, 1)
                c.after(dve.tensor_scalar(valid[:], mk[:], -1.0, 1.0, ALU.mult, ALU.add))
                c.after(dve.tensor_scalar(validc[:], mkc[:], -1.0, 1.0, ALU.mult, ALU.add))
                for b in range(B):
                    for t in range(TB):
                        dve_ins = dve.tensor_copy(va[:, b, t, :, HD:HD + 1],
                                                  valid[:, b, t:t + 1].rearrange("p (h o) -> p h o", o=1)
                                                  .broadcast_to([P, H, 1]))
                        c.after(dve_ins)
                dve.sem_inc(valid_ready, 4)
                for sems in (max_done, pv_copied):
                    for k in range(2):
                        dve.sem_inc(sems[k], CREDIT)
                dve.sem_inc(pv_done[0], PV_CREDIT)
                dve.sem_inc(pv_done[1], CREDIT)
                norm(0, 0)
                rotate(0, 0)
                with dve.Fori(0, HP) as hp:
                    for j in range(2):
                        row_max(0, 2 * hp + j, 0)
                        row_max(0, 2 * hp + j, 1)
                split_max(0, 0)
                with dve.Fori(0, UNITS - 1) as n:
                    c.loop(n, C_STEPS)
                    norm(n + 1, 0)
                    rotate(n + 1, 0)
                    self_attention(n, True)
                    rest(n)
                    c.loop_end(UNITS - 1)
                self_attention(UNITS - 1, False)
                rest(UNITS - 1)
                c.after(dve.tensor_tensor(m.x[:], m.x[:], m.y[:], ALU.add))


C_STEPS = 3 * 24 + 2 + 2 + 16


def stage_d(nc, a, m):
    norm_block(nc, m, "D0n", first_only=True)
    with nc.sbuf_tensor("D_gT", [P, 2, T * P], BF16) as gT, nc.sbuf_tensor("D_sel", [P, PAIR_D, P], BF16) as sel:
        router_d(nc, a, m, gT, sel)
        experts_d(nc, a, m, gT, sel)


def router_d(nc, a, m, gT, sel):
    sem = lambda s: m.sem("D1_" + s)
    loaded, logits_done, scored, order, w_ready, turned, gT_ready, sel_set, sel_made = \
        (sem(s) for s in ("loaded", "logits_done", "scored", "order", "w_ready", "turned", "gT_ready",
                          "sel_set", "sel_made"))
    GE = E_D // G_D
    TAKEN = -2.0e30
    sb = lambda n, sh, dt=F32: nc.sbuf_tensor("D1_" + n, sh, dt)
    with sb("gw", [P, E_D]) as gw, sb("gb", [P, E_D]) as gb, sb("scores", [P, T, E_D]) as scores, \
            sb("sc", [P, T, E_D]) as sc, sb("top", [P, T, G_D, 8]) as top, sb("gs", [P, T, 16]) as gs, \
            sb("gtop", [P, T, 8]) as gtop, sb("grest", [P, T, 16]) as grest, sb("gmask", [P, T, G_D]) as gmask, \
            sb("masked", [P, T, E_D]) as masked, sb("off", [P, T, G_D]) as off, sb("etop", [P, T, 8]) as etop, \
            sb("erest", [P, T, E_D]) as erest, sb("wsum", [P, T]) as wsum, sb("wd", [P, T, E_D]) as wd, \
            sb("rem", [P, T * P]) as rem, nc.Block() as block:
        @block.sync
        def _(sp):
            sp.dma_start(gw[:], a["D_gw"]).then_inc(loaded, 16)
            sp.dma_start(gb[:], a["D_gb"].rearrange("(o e) -> o e", o=1).broadcast_to([P, E_D]))\
                .then_inc(loaded, 16)

        @block.gpsimd
        def _(pool):
            pool.memset(sel[:], 0.0).then_inc(sel_set, 1)
            pool.wait_ge(sel_set, 1)
            n = 0
            for part in range(2):
                for side in range(2):
                    view = sel[:, :, side * F_D:(side + 1) * F_D]
                    pool.affine_select(out=view, in_=view, compare_op=ALU.not_equal, fill=1.0,
                                       base=-E_D * part - side, pattern=[[-2, PAIR_D], [0, F_D]],
                                       channel_multiplier=1).then_inc(sel_made, 1)
                    n += 1
                    pool.wait_ge(sel_made, n)

        @block.tensor
        def _(pe):
            pe.wait_ge(loaded, 32)
            for t in range(T):
                last = pe.matmul(m.ps[:, 0, t * E_D:(t + 1) * E_D],
                                 lhsT=m.hT[:, t // TB, t % TB * P:(t % TB + 1) * P], rhs=gw[:],
                                 start=True, stop=True)
            last.then_inc(logits_done, 1)
            pe.wait_ge(w_ready, 1)
            for t in range(T):
                last = pe.transpose(m.ps[0:E_D, 1 + t // TB, t % TB * P:(t % TB + 1) * P], wd[:, t, :], m.ident[:])
            last.then_inc(turned, 1)

        @block.scalar
        def _(act):
            act.wait_ge(logits_done, 1)
            act.activation(scores[:], m.ps[:, 0, :].rearrange("p (t e) -> p t e", e=E_D), ACT.Sigmoid)\
                .then_inc(scored, 1)

        @block.vector
        def _(dve):
            c = Chain(dve, order)
            wide = lambda x, n: x.rearrange("p (t o) -> p t o", o=1).broadcast_to([P, T, n])
            c.step(dve.memset(gs[:], NEG))
            dve.wait_ge(loaded, 32)
            dve.wait_ge(scored, 1)
            c.after(dve.tensor_tensor(sc[:], scores[:], gb[:].rearrange("p (o e) -> p o e", o=1)
                                      .broadcast_to([P, T, E_D]), ALU.add))
            for t in range(T):
                for g in range(G_D):
                    c.step(dve.max(top[:, t, g, :], sc[:, t, g * GE:(g + 1) * GE]))
            dve.wait_ge(order, c.n)
            c.after(dve.tensor_tensor(gs[:, :, 0:G_D], top[:, :, :, 0], top[:, :, :, 1], ALU.add))
            for t in range(T):
                c.step(dve.max(gtop[:, t, :], gs[:, t, :]))
            dve.wait_ge(order, c.n)
            c.after(dve.memset(gtop[:, :, 4:8], NEG))
            for t in range(T):
                c.after(dve.match_replace(grest[:, t, :], gtop[:, t, :], gs[:, t, :], TAKEN))
            c.after(dve.tensor_scalar(gmask[:], grest[:, :, 0:G_D], TAKEN, None, ALU.is_equal))
            c.after(dve.tensor_scalar(off[:], gmask[:], -1.0, -NEG, ALU.add, ALU.mult))
            per_group = lambda x: x[:].rearrange("p t (g o) -> p t g o", o=1).broadcast_to([P, T, G_D, GE])
            by_group = lambda x: x[:].rearrange("p t (g e) -> p t g e", e=GE)
            c.after(dve.tensor_tensor(by_group(masked), by_group(sc), per_group(gmask), ALU.mult))
            c.after(dve.tensor_tensor(by_group(masked), by_group(masked), per_group(off), ALU.add))
            for t in range(T):
                c.step(dve.max(etop[:, t, :], masked[:, t, :]))
            dve.wait_ge(order, c.n)
            for t in range(T):
                c.after(dve.match_replace(erest[:, t, :], etop[:, t, :], masked[:, t, :], TAKEN))
            c.after(dve.scalar_tensor_tensor(wd[:], erest[:], TAKEN, scores[:], ALU.is_equal, ALU.mult))
            c.after(dve.tensor_reduce(wsum[:], wd[:], AX.X, ALU.add))
            c.after(dve.tensor_scalar(wsum[:], wsum[:], 1e-20, None, ALU.add))
            c.after(dve.reciprocal(wsum[:], wsum[:]))
            c.after(dve.tensor_tensor(wd[:], wd[:], wide(wsum[:], E_D), ALU.mult))
            dve.tensor_scalar(wd[:], wd[:], 2.5, None, ALU.mult).then_inc(w_ready, 1)
            dve.wait_ge(turned, 1)
            w_ps = m.ps[0:E_D, 1:3, :].rearrange("p b s -> p (b s)")
            lo, hi = slice(0, E_D), slice(E_D, P)
            c.after(dve.tensor_copy(gT[lo, 0, :], w_ps))
            c.after(dve.tensor_tensor(rem[lo, :], w_ps, gT[lo, 0, :], ALU.subtract))
            c.after(dve.tensor_copy(gT[lo, 1, :], rem[lo, :]))
            c.after(dve.tensor_copy(gT[hi, 0, :], gT[lo, 1, :]))
            dve.tensor_tensor(gT[lo, 1, :], rem[lo, :], gT[lo, 1, :], ALU.subtract).then_inc(gT_ready, 1)


def experts_d(nc, a, m, gT, sel):
    sem = lambda s: m.sem("D2_" + s)
    names = ("w_loaded0", "gate_done", "up_done", "wb_done", "silu_done", "mid_done", "h_ready", "down_done",
             "acc_ready", "acc_turned", "order")
    w_loaded, gate_done, up_done, wb_done, silu_done, mid_done, h_ready, down_done, acc_ready, acc_turned, order = \
        (sem(s) for s in names)
    closed = sem("closed")
    UN = 2
    w_loaded = [w_loaded, sem("w_loaded1")]
    with nc.sbuf_tensor("D2_w", [P, UN, 3, P], F32) as w, nc.sbuf_tensor("D2_ws", [P, 3, P], F32) as ws, \
            nc.sbuf_tensor("D2_g", [P, B, S], F32) as g, nc.sbuf_tensor("D2_t", [P, B, S], F32) as mid, \
            nc.sbuf_tensor("D2_h", [P, B, S], F32) as h, nc.sbuf_tensor("D2_acc", [P, B, S], F32) as acc, \
            nc.semaphore("D2_shared_loaded") as shared_loaded, nc.Block() as block:
        @block.sync
        def _(sp):
            sp.dma_start(ws[:], a["D_ws"]).then_inc(shared_loaded, 16)
            with sp.Fori(0, PAIR_D // UN) as i:
                for k in range(UN):
                    sp.wait_ge(down_done, (i * UN + 1) * B)
                    sp.dma_start(w[:, k, :, :], a["D_ew"][i * UN + k]).then_inc(w_loaded[k], 16)

        @block.tensor
        def _(pe):
            def pair(e, gate, up, down, rows, weigh, first, last):
                for b in range(B):
                    pe.matmul(m.ps[0:rows, b, :], lhsT=gate, rhs=m.hT[:, b, :], start=True, stop=True)\
                        .then_inc(gate_done, 1)
                    pe.matmul(m.ps[0:rows, 2 + b, :], lhsT=up, rhs=m.hT[:, b, :], start=True, stop=True)\
                        .then_inc(up_done, 1)
                    if weigh is not None:
                        pe.matmul(m.ps[:, 4 + b, :], lhsT=sel[:, weigh, :], rhs=gT[:, 0, b * S:(b + 1) * S],
                                  start=True, stop=False)
                        pe.matmul(m.ps[:, 4 + b, :], lhsT=sel[0:E_D, weigh, :],
                                  rhs=gT[0:E_D, 1, b * S:(b + 1) * S], start=False, stop=True).then_inc(wb_done, 1)
                for b in range(B):
                    pe.wait_ge(h_ready, e * B + b + 1)
                    pe.matmul(m.ps[:, 6 + b, :], lhsT=down, rhs=h[0:rows, b, :], start=first, stop=last).then_inc(down_done, 1)

            pe.wait_ge(shared_loaded, 16)
            pair(0, ws[:, 0, 0:F_D], ws[:, 1, 0:F_D], ws[0:F_D, 2, :], F_D, None, True, False)
            with pe.Fori(0, PAIR_D // UN) as i:
                for k in range(UN):
                    e = i * UN + k
                    pe.wait_ge(w_loaded[k], 16 * (i + 1))
                    pair(e + 1, w[:, k, 0, :], w[:, k, 1, :], w[:, k, 2, :], P, e, False, False)
            close_sums(pe, m, (6, 7), closed)
            pe.wait_ge(acc_ready, 2)
            for b in range(B):
                for t in range(TB):
                    last = pe.transpose(m.ps[:, b, t * P:(t + 1) * P], acc[:, b, t * P:(t + 1) * P], m.ident[:])
                last.then_inc(acc_turned, 1)

        @block.scalar
        def _(act):
            def pair(e, rows):
                for b in range(B):
                    act.wait_ge(gate_done, e * B + b + 1)
                    act.activation(g[0:rows, b, :], m.ps[0:rows, b, :], ACT.Silu).then_inc(silu_done, 1)

            pair(0, F_D)
            with act.Fori(0, PAIR_D) as e:
                pair(e + 1, P)

        @block.vector
        def _(dve):
            for b in range(B):
                dve.wait_ge(silu_done, b + 1)
                dve.wait_ge(up_done, b + 1)
                dve.tensor_tensor(h[0:F_D, b, :], g[0:F_D, b, :], m.ps[0:F_D, 2 + b, :], ALU.mult)\
                    .then_inc(h_ready, 1)
                dve.wait_ge(h_ready, b + 1)
                dve.sem_inc(mid_done, 1)
            with dve.Fori(1, PAIR_D + 1) as e:
                for b in range(B):
                    dve.wait_ge(silu_done, e * B + b + 1)
                    dve.wait_ge(up_done, e * B + b + 1)
                    dve.tensor_tensor(mid[:, b, :], g[:, b, :], m.ps[:, 2 + b, :], ALU.mult).then_inc(mid_done, 1)
                    dve.wait_ge(mid_done, e * B + b + 1)
                    dve.wait_ge(wb_done, e * B - B + b + 1)
                    dve.tensor_tensor(h[:, b, :], mid[:, b, :], m.ps[:, 4 + b, :], ALU.mult).then_inc(h_ready, 1)
            dve.wait_ge(closed, 1)
            for b in range(B):
                dve.tensor_copy(acc[:, b, :], m.ps[:, 6 + b, :]).then_inc(acc_ready, 1)
            c = Chain(dve, order)
            for b in range(B):
                x = m.x[:, b * TB:(b + 1) * TB, :]
                dve.wait_ge(acc_turned, b + 1)
                c.after(dve.tensor_tensor(x, x, m.ps[:, b, :].rearrange("p (t d) -> p t d", t=TB), ALU.add))


def kernel(**inputs):
    import numpy as np_
    import concourse.bacc as bacc
    from concourse.bass_utils import run_bass_kernel_spmd

    nc = bacc.Bacc("TRN2", target_bir_lowering=False, num_devices=1)
    arrays = lay_out({k: np_.asarray(v) for k, v in inputs.items()})
    aps = {n: nc.dram_tensor("in_" + n, x.shape, mybir.dt.from_np(x.dtype), kind="ExternalInput").ap()
           for n, x in arrays.items()}
    aps["out"] = nc.dram_tensor("out", (B * S, P), F32, kind="ExternalOutput").ap()
    build(nc, aps)
    r = run_bass_kernel_spmd(nc, [{"in_" + n: x for n, x in arrays.items()}], core_ids=[0])
    return r.results[0]["out"].reshape(B, S, P)


def lay_out(i):
    cat, stack = np.concatenate, np.stack
    out = {"x": i["x"].reshape(B * S, P), "condT": i["cond_1024"].T,
           "ctxT": i["ctx_1024"].transpose(2, 0, 1)}

    a, c = "L0_xcond_", "L1_xcond_"
    nw = [i[f"{a}norm{k}_w"] for k in (1, 2, 3)] + [i[f"{c}n{k}_w"][l].T for l in range(LAYERS) for k in (1, 2, 3)]
    nb = [i[f"{a}norm{k}_b"] for k in (1, 2, 3)] + [i[f"{c}n{k}_b"][l] for l in range(LAYERS) for k in (1, 2, 3)]
    out["norm_w"] = cat(nw, 1)
    out["norm_b"] = stack(nb).reshape(21, 2, P).transpose(2, 0, 1)
    f = "L0_ffn_"
    out["rows"] = cat([stack([i[a + "attn1_bo"], i[a + "attn2_bo"], i[a + "ff_b2"], i[f + "o_b"],
                              i[f + "gamma1"], i[f + "gamma2"]]), i[c + "f2_b"]])

    def pairs(q, qr, k, kr, v, o):
        cols = lambda x: x.reshape(P, PAIRS, P).transpose(1, 0, 2)
        return cat([cols(q), cols(qr), cols(k), cols(kr), cols(v), o.reshape(PAIRS, P, P)], 2)

    for n, s in (("A1_w", "attn1_"), ("A2_w", "attn2_")):
        q, k, v, o = (i[a + s + x] for x in ("wq", "wk", "wv", "wo"))
        out[n] = pairs(q, q, k, k, v, o)
    out["A_w1"] = i[a + "ff_w1"]
    out["A_b1"] = i[a + "ff_b1"].reshape(8, P).T
    out["A_w2"] = i[a + "ff_w2"].reshape(4, P, P).transpose(1, 0, 2)

    even_odd = np.arange(DH).reshape(DH // 2, 2).T.reshape(-1)
    order = (np.arange(H)[:, None] * DH + even_odd).reshape(-1)
    swap = (np.arange(H)[:, None] * DH + np.roll(even_odd, DH // 2)).reshape(-1)
    q, k, v, o = (i[f + x] for x in ("q_w", "k_w", "v_w", "o_w"))
    bq, bk, bv = (i[f + x] for x in ("q_b", "k_b", "v_b"))
    bias = stack([bq[order], bq[swap], bk[order], bk[swap], bv], 1).reshape(PAIRS, P, 5)
    out["B_bias"] = bias.transpose(1, 0, 2)
    out["B_w"] = pairs(q[:, order], q[:, swap], k[:, order], k[:, swap], v, o)
    half = DH // 2
    sign = np.tile(np.repeat(np.array([-1.0, 1.0], np.float32), half), 2)
    out["theta"] = stack([np.tile(i[f + "theta"], 4), sign], 1)
    out["positions"] = np.arange(S, dtype=np.float32)
    out["B_rw"], out["B_rb"] = i[f + "router_w"], i[f + "router_b"]
    w1 = cat([i[f + "re_w1"], i[f + "sh_w1"][None]])
    w2 = cat([i[f + "re_w2"], i[f + "sh_w2"][None]])
    b1 = cat([i[f + "re_b1"], i[f + "sh_b1"][None]])
    out["B_ew"] = cat([w1, w2, b1[:, :, None]], 2)
    out["B_b2"] = cat([i[f + "re_b2"], i[f + "sh_b2"][None]])

    place = (np.arange(HD)[:, None] + np.arange(H) * HD).reshape(-1)
    turned = (np.roll(np.arange(HD), HD // 2)[:, None] + np.arange(H) * HD).reshape(-1)
    layers = []
    for l in range(LAYERS):
        q, k, v = i[c + "qkv_w"][l].reshape(3, P, P)
        so, cq, ck, cv, co = (i[c + n + "_w"][l] for n in ("so", "cq", "ck", "cv", "co"))
        layers.append(cat([q[place].T, q[turned].T, k[place].T, k[turned].T, v.T, so.T, cq[place].T, cq[turned].T,
                           ck[place].T, ck[turned].T, cv.T, co.T, i[c + "f1_w"][l].T,
                           i[c + "f2_w"][l].T.reshape(4, P, P).transpose(1, 0, 2).reshape(P, 4 * P),
                           i[c + "f1_b"][l].reshape(4, P).T], 1))
    out["C_w"] = stack(layers)
    inv = (1.0 / np.float32(10000.0) ** (np.arange(HD // 2, dtype=np.float32) / np.float32(HD // 2)))
    angle = np.arange(S, dtype=np.float32)[:, None] * inv.astype(np.float32)
    row = np.repeat(np.arange(HD), H)
    side = np.where(row < HD // 2, np.float32(-1), np.float32(1))
    out["C_cos"] = np.cos(angle).T[row % (HD // 2)]
    out["C_sin"] = np.sin(angle).T[row % (HD // 2)] * side[:, None]
    ms, mc = i["mask_BxS_bf0"], i["mask_BxS2_bf0"]
    out["mask_rows"], out["maskc_rows"] = ms, mc
    out["mask_cols"] = ms.reshape(B, TB, P).transpose(2, 0, 1)
    out["maskc_cols"] = mc.T

    d = "L1_ffn_"
    out["D_gw"], out["D_gb"] = i[d + "gate_w"].T, i[d + "gate_bias"]
    side_by_side = lambda w: w.reshape(PAIR_D, 2, P, F_D).transpose(0, 2, 1, 3).reshape(PAIR_D, P, P)
    out["D_ew"] = stack([side_by_side(i[d + "We_gate"]), side_by_side(i[d + "We_up"]),
                         i[d + "We_down"].reshape(PAIR_D, P, P)], 2)
    wide = lambda w: cat([w, w], 1)
    down = i[d + "Ws_down"]
    out["D_ws"] = stack([wide(i[d + "Ws_gate"]), wide(i[d + "Ws_up"]), cat([down, down], 0)], 1)
    return {n: np.ascontiguousarray(x) for n, x in out.items()}
```
